# Optimizing a Trainium2 kernel written in Bass

```python
import numpy as np
import jax
import jax.numpy as jnp

def _softmax(x, axis=-1):
    return jax.nn.softmax(x, axis=axis)

def _gelu(x):
    return jax.nn.gelu(x, approximate=True)

def _silu(x):
    return jax.nn.silu(x)

def _sigmoid(x):
    return jax.nn.sigmoid(x)

def _layernorm(x, axis=-1, eps=1e-05):
    m = jnp.mean(x, axis=axis, keepdims=True)
    v = jnp.var(x, axis=axis, keepdims=True)
    return (x - m) / jnp.sqrt(v + eps)

def _scatter_add(tgt, idx, src, axis=0):
    return tgt.at[idx].add(src)

def _segment_sum(src, seg, n):
    return jax.ops.segment_sum(src, seg, n)
kernel_name = 'mk_prb_d1_jaxref_r4_f2f730'

def setup_inputs(seed: int=0):
    np.random.seed(seed)
    _w = jnp.asarray

    def _L0_attn_setup():
        import jax, jax.numpy as jnp
        import numpy as np
        D_MODEL = 256
        N_HEADS = 16
        HEAD_DIM = D_MODEL // N_HEADS
        ROPE_BASE = 10000.0

        def _rope(q, k):
            S, Dh = (q.shape[1], q.shape[-1])
            inv_freq = 1.0 / ROPE_BASE ** (jnp.arange(0, Dh, 2, dtype=jnp.float32) / Dh)
            t = jnp.arange(S, dtype=jnp.float32)
            freqs = jnp.outer(t, inv_freq)
            emb = jnp.concatenate([freqs, freqs], axis=-1)
            cos = jnp.cos(emb)[None, :, None, :]
            sin = jnp.sin(emb)[None, :, None, :]

            def rotate_half(v):
                v1, v2 = (v[..., :Dh // 2], v[..., Dh // 2:])
                return jnp.concatenate([-v2, v1], axis=-1)
            return (q * cos + rotate_half(q) * sin, k * cos + rotate_half(k) * sin)
        key = jax.random.key(seed)
        ks = jax.random.split(key, 5)
        B, S = (1, 1024)
        scale = 1.0 / np.sqrt(D_MODEL)
        x = jax.random.normal(ks[0], (B, S, D_MODEL), dtype=jnp.float32)
        Wq = jax.random.normal(ks[1], (D_MODEL, D_MODEL), dtype=jnp.float32) * scale
        Wk = jax.random.normal(ks[2], (D_MODEL, D_MODEL), dtype=jnp.float32) * scale
        Wv = jax.random.normal(ks[3], (D_MODEL, D_MODEL), dtype=jnp.float32) * scale
        Wo = jax.random.normal(ks[4], (D_MODEL, D_MODEL), dtype=jnp.float32) * scale
        return {'x': x, 'Wq': Wq, 'Wk': Wk, 'Wv': Wv, 'Wo': Wo}
    _L0_attn_in = _L0_attn_setup()

    def _L0_ffn_setup():
        import jax, jax.numpy as jnp
        import numpy as np
        TOPK = 4
        key = jax.random.key(seed)
        ks = jax.random.split(key, 9)
        B, T, D = (4, 512, 256)
        E, H = (32, 128)
        HS = H * TOPK
        s = lambda k, shape, fan: jax.random.normal(k, shape, dtype=jnp.float32) / np.sqrt(fan)
        return {'x': jax.random.normal(ks[0], (B, T, D), dtype=jnp.float32), 'router_w': s(ks[1], (E, D), D), 'router_bias': jnp.zeros((E,), dtype=jnp.float32), 'gate_w': s(ks[2], (E, H, D), D), 'up_w': s(ks[3], (E, H, D), D), 'down_w': s(ks[4], (E, D, H), H), 'sgate_w': s(ks[5], (HS, D), D), 'sup_w': s(ks[6], (HS, D), D), 'sdown_w': s(ks[7], (D, HS), HS)}
    _L0_ffn_in = _L0_ffn_setup()
    _d = {'L0_attn_x': _L0_attn_in['x'], 'L0_attn_Wq': _L0_attn_in['Wq'], 'L0_attn_Wk': _L0_attn_in['Wk'], 'L0_attn_Wv': _L0_attn_in['Wv'], 'L0_attn_Wo': _L0_attn_in['Wo'], 'L0_ffn_router_w': _L0_ffn_in['router_w'], 'L0_ffn_router_bias': _L0_ffn_in['router_bias'], 'L0_ffn_gate_w': _L0_ffn_in['gate_w'], 'L0_ffn_up_w': _L0_ffn_in['up_w'], 'L0_ffn_down_w': _L0_ffn_in['down_w'], 'L0_ffn_sgate_w': _L0_ffn_in['sgate_w'], 'L0_ffn_sup_w': _L0_ffn_in['sup_w'], 'L0_ffn_sdown_w': _L0_ffn_in['sdown_w']}
    _x0 = _d['L0_attn_x']
    _d['L0_attn_x'] = jax.random.normal(jax.random.fold_in(jax.random.key(seed), 1), (16, 512, 256), dtype=_x0.dtype)
    del _x0
    return _d

def reference(L0_attn_x, L0_attn_Wq, L0_attn_Wk, L0_attn_Wv, L0_attn_Wo, L0_ffn_router_w, L0_ffn_router_bias, L0_ffn_gate_w, L0_ffn_up_w, L0_ffn_down_w, L0_ffn_sgate_w, L0_ffn_sup_w, L0_ffn_sdown_w):

    def _L0_attn_ref(x, Wq, Wk, Wv, Wo):
        import jax, jax.numpy as jnp
        import numpy as np
        D_MODEL = 256
        N_HEADS = 16
        HEAD_DIM = D_MODEL // N_HEADS
        ROPE_BASE = 10000.0

        def _rope(q, k):
            S, Dh = (q.shape[1], q.shape[-1])
            inv_freq = 1.0 / ROPE_BASE ** (jnp.arange(0, Dh, 2, dtype=jnp.float32) / Dh)
            t = jnp.arange(S, dtype=jnp.float32)
            freqs = jnp.outer(t, inv_freq)
            emb = jnp.concatenate([freqs, freqs], axis=-1)
            cos = jnp.cos(emb)[None, :, None, :]
            sin = jnp.sin(emb)[None, :, None, :]

            def rotate_half(v):
                v1, v2 = (v[..., :Dh // 2], v[..., Dh // 2:])
                return jnp.concatenate([-v2, v1], axis=-1)
            return (q * cos + rotate_half(q) * sin, k * cos + rotate_half(k) * sin)
        B, S, _ = x.shape
        H, Dh = (N_HEADS, HEAD_DIM)
        q = (x @ Wq.T).reshape(B, S, H, Dh)
        k = (x @ Wk.T).reshape(B, S, H, Dh)
        v = (x @ Wv.T).reshape(B, S, H, Dh)
        q, k = _rope(q, k)
        scale = 1.0 / np.sqrt(Dh)
        scores = jnp.einsum('bqhd,bkhd->bhqk', q, k) * scale
        causal = jnp.triu(jnp.ones((S, S), dtype=bool), k=1)
        scores = jnp.where(causal, -jnp.inf, scores)
        attn = jax.nn.softmax(scores, axis=-1)
        out = jnp.einsum('bhqk,bkhd->bqhd', attn, v).reshape(B, S, H * Dh)
        return out @ Wo.T

    def _L0_ffn_ref(x, router_w, router_bias, gate_w, up_w, down_w, sgate_w, sup_w, sdown_w):
        import jax, jax.numpy as jnp
        import numpy as np
        TOPK = 4
        B, T, D = x.shape
        flat = x.reshape(B * T, D)
        logits = flat.astype(jnp.float32) @ router_w.T + router_bias
        scores = jax.nn.softmax(logits, axis=-1)
        topk_scores, topk_idx = jax.lax.top_k(scores, TOPK)
        topk_scores = topk_scores / jnp.clip(topk_scores.sum(axis=-1, keepdims=True), 1e-12, None)
        h = jax.nn.silu(jnp.einsum('nd,ehd->neh', flat, gate_w)) * jnp.einsum('nd,ehd->neh', flat, up_w)
        expert_out = jnp.einsum('neh,edh->ned', h, down_w)
        sel = jnp.take_along_axis(expert_out, topk_idx[:, :, None], axis=1)
        out = (sel * topk_scores.astype(flat.dtype)[:, :, None]).sum(axis=1)
        out = out + jax.nn.silu(flat @ sgate_w.T) * (flat @ sup_w.T) @ sdown_w.T
        return out.reshape(B, T, D)
    x = L0_attn_x
    xn = _layernorm(x, axis=-1)
    x = x + _L0_attn_ref(xn, L0_attn_Wq, L0_attn_Wk, L0_attn_Wv, L0_attn_Wo) + _L0_ffn_ref(xn, L0_ffn_router_w, L0_ffn_router_bias, L0_ffn_gate_w, L0_ffn_up_w, L0_ffn_down_w, L0_ffn_sgate_w, L0_ffn_sup_w, L0_ffn_sdown_w)
    return x

_drawn_inputs = setup_inputs


def setup_inputs(seed=0):
    import zlib

    import numpy as np

    out = dict(_drawn_inputs(seed))
    spreads = {'L0_ffn_router_bias': (0.0, 0.1)}
    factors = {}
    for name, (base, spread) in spreads.items():
        noise = np.random.default_rng([zlib.crc32(name.encode()), seed]).standard_normal(out[name].shape)
        drawn = base * np.exp(spread * noise) if base else spread * noise
        out[name] = jnp.asarray(drawn.astype(out[name].dtype))
    for name, factor in factors.items():
        out[name] = (out[name] * factor).astype(out[name].dtype)
    return out
```

```python
from contextlib import ExitStack

import numpy as np

import concourse.bass as bass
from concourse import mybir

F32 = mybir.dt.float32
BF16 = mybir.dt.bfloat16
I32 = mybir.dt.int32
U32 = mybir.dt.uint32
ALU = mybir.AluOpType
ACT = mybir.ActivationFunctionType
AX = mybir.AxisListType

P = 128
BATCH, SEQ, D = 16, 512, 256
NT = SEQ // P
KC = D // P
NH, DH = 16, 16
NG, GH = 4, 4
E, TOPK, HE, HS = 32, 4, 128, 512
NM = HS // P
TOKENS = BATCH * SEQ
NPART = 3
Q_PART = [0, 0, 0, 1, 1, 2]
K_PART = [0, 1, 2, 0, 1, 0]
NSTACK = len(Q_PART)
KROWS = NSTACK * DH
MROWS = KROWS + NPART
SCALE = DH ** -0.5
NEG = -1e30
REGION = TOKENS
NBLOCK = TOKENS * TOPK // P + E
TABLE = E * REGION + NBLOCK * P
N_CONSTS = 22
SKIP = 1 << 24
EPS = 1e-5
MAGIC = float(0x5F3759DF)

MAX_UNITS = [(0, 0, 4, 4), (1, 0, 4, 2), (2, 0, 2, 1), (2, 2, 2, 1), (3, 0, 2, 1), (3, 2, 2, 1)]
NU1 = len(MAX_UNITS)
NU2 = GH + 1


def hold(eng, passed):
    eng.sem_inc(passed, 1)


def attention_steps(with_next):
    s = [("ffn", 0), ("ffn", 1)]
    s += [("s1", 0, 0), ("s1", 0, 1), ("route",), ("s1", 0, 2), ("ffn", 2), ("s1", 0, 3), ("s1", 0, 4), ("s1", 0, 5),
          ("negsplit", 0)]
    s += [("ffn", 3), ("negT", 0), ("s1", 1, 0), ("s1", 1, 1), ("rank",)]
    if with_next:
        s += [("ln",)]
    nxt = {1: [], 2: [], 3: [], 4: []}
    if with_next:
        nxt = {1: [("xT", 0), ("xT", 1), ("xT", 2), ("xT", 3)],
               2: [("qkv", 0), ("qkv", 1)], 3: [("partsT", 0), ("qkv", 2)],
               4: [("partsT", 1), ("qkv", 3)]}
    for g in range(1, NG):
        if g > 1:
            s += [("s1", g, 0), ("negT", g - 1), ("s1", g, 1)]
        fill = list(nxt[g])
        for u in range(2, NU1):
            s += [("s1", g, u)]
            if u == 3 and fill:
                s += [fill.pop(0)]
            s += [("s2", g - 1, u - 2)]
            if u == 2 and g > 1:
                s += [("av", g - 2)]
            if u == 4 and fill:
                s += [fill.pop(0)]
            if u == 4 and g > 1:
                s += [("avT", g - 2)]
        s += [("negsplit", g), ("s2", g - 1, 4)] + fill
    s += nxt[4][:1]
    s += [("negT", NG - 1), ("av", NG - 2)] + nxt[4][1:] + [("s2", NG - 1, 0), ("s2", NG - 1, 1), ("avT", NG - 2),
          ("s2", NG - 1, 2), ("s2", NG - 1, 3), ("s2", NG - 1, 4)]
    if with_next:
        s += [("partsT", 2)]
    s += [("av", NG - 1), ("down",)]
    if with_next:
        s += [("partsT", 3), ("stack",)]
    s += [("avT", NG - 1), ("aT", 0), ("aT", 1), ("oproj", 0), ("oproj", 1)]
    return s


FIRST_STEPS = [("ln",)] + [("xT", t) for t in range(NT)] + [("qkv", 0), ("qkv", 1)] + \
    [("partsT", 0), ("qkv", 2), ("partsT", 1), ("qkv", 3), ("partsT", 2), ("partsT", 3), ("stack",)]

BANKS_OF = {"ffn": ("hidden", "hidden"), "negT": ("neg_t",), "avT": ("attn",), "xT": ("xn_t",), "qkv": ("rope", "logits"),
            "partsT": ("q_t", "k_t"), "aT": ("attn_t",), "rank": ("slots",)}
NEXT_STEPS = ("ln", "xT", "qkv", "partsT", "stack")
TIMES = {"hidden": NM, "neg_t": NG, "attn": NG, "xn_t": NT, "rope": NT, "logits": NT, "q_t": NT, "k_t": NT,
         "attn_t": 2, "slots": 1, "row_max": NG * NU1, "probs": NG * NU2, "sums": 2}


def bank_plan(steps, nbanks=3):
    plan, last, seen, n = {}, [None] * nbanks, {}, 0
    for step in steps:
        for k, name in enumerate(BANKS_OF.get(step[0], ())):
            b = n % nbanks
            n += 1
            plan[step, k] = (b, last[b])
            idx = step[1] if len(step) > 1 else 0
            last[b] = (name, idx, step[0] in NEXT_STEPS)
    return plan


def unit_plan(steps):
    plan, last, n = {}, [None, None], 0
    for step in steps:
        if step[0] in ("s1", "s2", "down"):
            u = n % 2
            n += 1
            plan[step] = (u, last[u])
            last[u] = {"s1": lambda: ("row_max", step[1] * NU1 + step[2]), "s2": lambda: ("probs", step[1] * NU2 + step[2]),
                       "down": lambda: ("sums", 1)}[step[0]]()
    return plan


def block_kernel(nc, x, wqkvr, wo, wgu_s, wd_s, bias, wgu_e, wd_e, rope_cos, rope_sin, out):
    xn_dram = nc.dram_tensor("xn_dram", (TOKENS, D), F32, kind="Internal").ap()
    sum_dram = nc.dram_tensor("sum_dram", (TOKENS, D), F32, kind="Internal").ap()
    table = nc.dram_tensor("table", (TABLE, 4), I32, kind="Internal").ap()
    y_dram = nc.dram_tensor("y_dram", (TOKENS * TOPK, D), F32, kind="Internal").ap()

    ctx = ExitStack()
    with ctx:
        def sb(name, shape, dt=F32, where=None):
            return (where or ctx).enter_context(nc.sbuf_tensor(name, shape, dt))

        def sem(name):
            return ctx.enter_context(nc.semaphore(name))

        ident = sb("ident", [P, P])
        identb = sb("identb", [P, P], BF16)
        iota_e = sb("iota_e", [P, E])
        counts = sb("counts", [P, E])
        ps_g = [ctx.enter_context(nc.psum_tensor(f"ps_g{i}", [P, 512], F32)) for i in range(3)]
        ps_u = [ctx.enter_context(nc.psum_tensor(f"ps_u{i}", [P, 2, 512], F32)) for i in range(2)]
        ps_av = ctx.enter_context(nc.psum_tensor("ps_av", [P, 512], F32))

        phase_a(nc, sb, sem, ident, identb, iota_e, counts, ps_g, ps_u, ps_av, x, wqkvr, wo, wgu_s, wd_s, bias,
                rope_cos, rope_sin, xn_dram, sum_dram, table)
        phase_bcd(nc, sb, sem, ident, iota_e, counts, ps_g, ps_u, ps_av, wgu_e, wd_e, xn_dram, sum_dram, table,
                  y_dram, out)


def phase_a(nc, sb_, sem, ident, identb, iota_e, counts, ps_g, ps_u, ps_av, x, wqkvr, wo, wgu_s, wd_s, bias,
            rope_cos, rope_sin, xn_dram, sum_dram, table):
    stack = ExitStack()
    with stack:
        def sb(name, shape, dt=F32):
            return sb_(name, shape, dt, stack)

        w_qkvr = sb("w_qkvr", [P, KC, 3 * D + E])
        w_o = sb("w_o", [P, KC, D])
        w_gu = sb("w_gu", [P, KC, 2 * HS])
        w_d = sb("w_d", [P, NM, D])
        bias_bc = sb("bias_bc", [P, E])
        cos = sb("cos", [P, NT, P])
        sin = sb("sin", [P, NT, P])
        mask_qk = sb("mask_qk", [P, P], BF16)
        mask_kq = sb("mask_kq", [P, P], BF16)
        before = sb("before", [P, P], BF16)
        ones = sb("ones", [P, P], BF16)
        tri_f = sb("tri_f", [P, P])

        xin = sb("xin", [P, NT, D])
        stats = sb("stats", [P, NT, 6])
        mv = sb("mv", [P, NT, 2])
        ve = sb("ve", [P, NT])
        rs = sb("rs", [P, NT])
        rs_t = sb("rs_t", [P, NT])
        xn = sb("xn", [P, NT, D])
        xn_t = sb("xn_t", [P, KC, SEQ])
        rp1 = sb("rp1", [P, 2, 2 * D])
        rp2 = sb("rp2", [P, 2, 2 * D])
        rqk = sb("rqk", [P, 2 * D])
        rres = sb("rres", [P, 2 * D])
        parts = sb("parts", [P, 2, NPART, 2 * D], BF16)
        q_t = sb("q_t", [P, NPART, KC, SEQ], BF16)
        k_t = sb("k_t", [P, NPART, KC, SEQ], BF16)
        v_new = sb("v_new", [P, NT, D])
        logits = sb("logits", [P, NT, E])

        q_st = sb("q_st", [P, NH, SEQ], BF16)
        k_st = sb("k_st", [P, NH, SEQ], BF16)
        v_pad = sb("v_pad", [P, NT, NH, 2 * DH])
        neg = sb("neg", [P, 2, NT, GH])
        neg_r = sb("neg_r", [P, NT, GH])
        neg_p = sb("neg_p", [P, 2, NT, NPART, GH], BF16)
        neg_t = sb("neg_t", [NPART * GH, 2, SEQ], BF16)
        probs = [sb(f"probs{i}", [P, NU2, 1024]) for i in range(2)]
        av = sb("av", [P, SEQ])
        rden = sb("rden", [P, NT, GH])
        attn = sb("attn", [P, NT, D])
        attn_t = sb("attn_t", [P, KC, SEQ])
        th = sb("th", [P, 2, SEQ])
        gth = sb("gth", [P, SEQ])
        hid = sb("hid", [P, NM, SEQ])
        xres = sb("xres", [P, NT, D])
        osum = sb("osum", [P, NT, D])
        lg = sb("lg", [P, NT, E])
        top_v = sb("top_v", [P, NT, 8])
        top_i = sb("top_i", [P, NT, 8], U32)
        top_f = sb("top_f", [P, NT, TOPK])
        onehot = sb("onehot", [P, NT, TOPK, E])
        chosen = sb("chosen", [P, NT, E], BF16)
        ex = sb("ex", [P, NT, E + TOPK])
        exo = sb("exo", [P, NT, E + TOPK])
        zs = sb("zs", [P, 4, NT])
        pr4 = sb("pr4", [P, NT, TOPK])
        base = sb("base", [P, E])
        region = sb("region", [P, E])
        pos = sb("pos", [P, NT, E])
        slotf = sb("slotf", [P, NT * TOPK])
        slot = sb("slot", [P, NT * TOPK], I32)
        token_f = sb("token_f", [P, NT * TOPK])
        dest_f = sb("dest_f", [P, NT * TOPK])
        entry = sb("entry", [P, NT * TOPK, 4], I32)

        S = {n: sem(n) for n in TIMES}
        consts, weights, inited, table_set = sem("consts"), sem("weights"), sem("inited"), sem("table_set")
        x_in, x_res, xn_out, sum_out = sem("x_in"), sem("x_res"), sem("xn_out"), sem("sum_out")
        stacked = [sem("stacked0"), sem("stacked1")]
        neg_rows = [sem("neg_rows0"), sem("neg_rows1")]
        scattered = sem("scattered")
        xn_ready, parts_ready, v_placed = sem("xn_ready"), sem("parts_ready"), sem("v_placed")
        v_ready = sem("v_ready")
        passed_pool, passed_dve, passed_sp = sem("passed_pool"), sem("passed_dve"), sem("passed_sp")
        neg_parts, tanh_done, av_out, exps, chosen_ready = \
            sem("neg_parts"), sem("tanh_done"), sem("av_out"), sem("exps"), sem("chosen_ready")
        pe = {n: sem("pe_" + n) for n in ("xT", "qk", "vr", "qT", "kT", "gate", "up", "s1", "negT", "s2", "av", "avT",
                                          "aT", "sum", "rank")}
        dve_front, dve_chain, pool_chain, ex_ready, rope1 = \
            sem("dve_front"), sem("dve_chain"), sem("pool_chain"), sem("ex_ready"), sem("rope1")

        STACK_DMAS = NSTACK * 2

        def done(name, b, k):
            return b * TIMES[name] + k + 1

        block = stack.enter_context(nc.Block())
        body = attention_steps(True)
        tail = attention_steps(False)

        def run(eng, handlers, per=None):
            def steps(order, b, nb, first):
                bp, up = bank_plan(order), unit_plan(order)
                for step in order:
                    if step[0] in handlers:
                        handlers[step[0]](nb if step[0] in NEXT_STEPS else b, step, (bp, up, b, first))
            steps(FIRST_STEPS, 0, 0, True)
            steps(body, 0, 1, False)
            with eng.Fori(1, BATCH - 1) as b:
                steps(body, b, b + 1, False)
            steps(tail, BATCH - 1, None, False)

        class Chain:

            def __init__(self, eng, s, per, passed):
                self.eng, self.s, self.per, self.passed, self.k = eng, s, per, passed, 0

            def link(self, b, ins, apart=False):
                ins.then_inc(self.s, 1)
                self.k = self.k % self.per + 1
                self.eng.wait_ge(self.s, b * self.per + self.k)
                if apart:
                    hold(self.eng, self.passed)

            def closed(self):
                assert self.k == self.per, (self.k, self.per)

        @block.sync
        def _(sp):
            sp.dma_start(w_qkvr[:, :, :], wqkvr.rearrange("(c p) n -> p c n", p=P)).then_inc(weights, 16)
            sp.dma_start(cos[:, :, :], rope_cos.rearrange("(t p) c -> p t c", p=P)).then_inc(weights, 16)
            sp.dma_start(sin[:, :, :], rope_sin.rearrange("(t p) c -> p t c", p=P)).then_inc(weights, 16)
            sp.dma_start(bias_bc[:, :], bias.partition_broadcast(P)).then_inc(weights, 16)
            sp.dma_start(w_gu[:, :, :], wgu_s.rearrange("(c p) n -> p c n", p=P)).then_inc(weights, 16)
            sp.dma_start(w_d[:, :, :], wd_s.rearrange("(c p) n -> p c n", p=P)).then_inc(weights, 16)
            sp.dma_start(w_o[:, :, :], wo.rearrange("(c p) n -> p c n", p=P)).then_inc(weights, 16)

            def tokens(dram, b):
                return dram[bass.ds(b * SEQ, SEQ), :].rearrange("(t p) d -> p t d", p=P)

            def ln(nb, step, env):
                sp.wait_ge(xn_ready, NT * nb + NT)
                sp.dma_start(tokens(xn_dram, nb), xn[:, :, :]).then_inc(xn_out, 16)

            def stack_rows(nb, step, env):
                sp.wait_ge(S["q_t"], done("q_t", nb, NT - 1))
                sp.wait_ge(S["k_t"], done("k_t", nb, NT - 1))
                for c in range(KC):
                    if not env[3]:
                        sp.wait_ge(pe["s2"], nb * NG * NU2 - (KC - 1 - c) * 2 * NU2)
                    for dst, src, which in ((q_st, q_t, Q_PART), (k_st, k_t, K_PART)):
                        for s in range(NSTACK):
                            sp.dma_start(dst[DH * s:DH * (s + 1), 8 * c:8 * c + 8, :],
                                         src[:, which[s], c, :]
                                         ).then_inc(stacked[c], 16)

            def x_load(nb):
                sp.wait_ge(xn_ready, NT * nb)
                sp.dma_start(xin[:, :, :], tokens(x, nb)).then_inc(x_in, 16)

            def ffn(b, step, env):
                if step[1] == 0:
                    sp.wait_ge(S["sums"], 2 * b)
                    sp.dma_start(xres[:, :, :], tokens(x, b)).then_inc(x_res, 16)
                    if env[0].get((("xT", 0), 0)):
                        x_load(b + 1)

            def neg_store(b, step, env):
                g = step[1]
                sp.wait_ge(S["neg_t"], done("neg_t", b, g))
                for p_ in range(NPART):
                    sp.dma_start(q_st[KROWS + p_:KROWS + p_ + 1, GH * g:GH * g + GH, :],
                                 neg_t[GH * p_:GH * p_ + GH, g % 2, :]).then_inc(neg_rows[g % 2], 16)

            def store(b, step, env):
                if step[1] == 1:
                    sp.wait_ge(S["sums"], 2 * b + 2)
                    sp.dma_start(tokens(sum_dram, b), osum[:, :, :]).then_inc(sum_out, 16)

            x_load_first = sp.dma_start(xin[:, :, :], tokens(x, 0)).then_inc(x_in, 16)
            sp.wait_ge(inited, 1)
            rows = TABLE // P // 4
            for k in range(4):
                sp.dma_start(table[k * P * rows:(k + 1) * P * rows, :].rearrange("(p r) c -> p (r c)", p=P),
                             probs[0][:, :, :].rearrange("p u n -> p (u n)")[:, 0:rows * 4].bitcast(I32)
                             ).then_inc(table_set, 16)
            run(sp, {"ln": ln, "stack": stack_rows, "ffn": ffn, "negT": neg_store, "oproj": store})
            sp.wait_ge(xn_out, 16 * BATCH)
            sp.wait_ge(sum_out, 16 * BATCH)

        @block.gpsimd
        def _(pool):
            blank = probs[0][:, :, :].rearrange("p u n -> p (u n)")[:, 0:TABLE // P].bitcast(I32)
            chain = Chain(pool, pool_chain, 4 * NT, passed_pool)
            made = [0]

            def const(ins):
                made[0] += 1
                ins.then_inc(consts, 1)
                pool.wait_ge(consts, made[0])

            def zeros_kept(value, base, mult, step):
                const(pool.memset(tri_f[:], 0.0))
                const(pool.affine_select(out=tri_f[:], in_=tri_f[:], compare_op=ALU.is_ge, fill=value, base=base,
                                         pattern=[[step, P]], channel_multiplier=mult))

            const(pool.memset(blank, 0))
            pool.memset(blank.rearrange("p (r c) -> p r c", c=4)[:, :, 1:2], SKIP).then_inc(inited, 1)
            pool.wait_ge(inited, 1)
            const(pool.memset(ident[:], 0.0))
            const(pool.affine_select(out=ident[:], in_=ident[:], compare_op=ALU.not_equal, fill=1.0, base=0,
                                     pattern=[[-1, P]], channel_multiplier=1))
            const(pool.tensor_copy(identb[:], ident[:]))
            const(pool.memset(v_pad[:], 0.0))
            const(pool.memset(v_pad[:, :, :, DH:DH + 1], 1.0))
            const(pool.memset(k_st[KROWS:MROWS, :, :], 1.0))
            const(pool.memset(ones[:], 1.0))
            const(pool.memset(counts[:], 0.0))
            const(pool.memset(entry[:], 0))
            const(pool.iota(iota_e[:], pattern=[[1, E]], base=0, channel_multiplier=0,
                            allow_small_or_imprecise_dtypes=True))
            const(pool.iota(token_f[:], pattern=[[P, NT], [0, TOPK]], base=0, channel_multiplier=1,
                            allow_small_or_imprecise_dtypes=True))
            const(pool.iota(dest_f[:], pattern=[[P * TOPK, NT], [1, TOPK]], base=0, channel_multiplier=TOPK,
                            allow_small_or_imprecise_dtypes=True))
            zeros_kept(NEG, 0, 1, -1)
            const(pool.tensor_copy(mask_qk[:], tri_f[:]))
            zeros_kept(NEG, 0, -1, 1)
            const(pool.tensor_copy(mask_kq[:], tri_f[:]))
            zeros_kept(1.0, 0, 1, -1)
            const(pool.tensor_copy(before[:], tri_f[:]))
            assert made[0] == N_CONSTS

            def qkv(nb, step, env):
                t = step[1]
                pool.wait_ge(S["rope"], done("rope", nb, t))
                chain.link(nb, pool.tensor_tensor(rqk[:], rp1[:, t % 2, :], rp2[:, t % 2, :], ALU.add))
                if not (env[3] and t < 2):
                    pool.wait_ge(pe["kT"], NT * nb + t - 1)
                hold(pool, passed_pool)
                chain.link(nb, pool.tensor_copy(parts[:, t % 2, 0, :], rqk[:]))
                pool.wait_ge(parts_ready, NT * nb + t)
                chain.link(nb, pool.tensor_tensor(rres[:], rqk[:], parts[:, t % 2, 0, :], ALU.subtract), apart=True)
                chain.link(nb, pool.tensor_copy(parts[:, t % 2, 1, :], rres[:]))
                pool.tensor_tensor(parts[:, t % 2, 2, :], rres[:], parts[:, t % 2, 1, :],
                                   ALU.subtract).then_inc(parts_ready, 1)
                if t == NT - 1:
                    chain.closed()

            def place_v(b, step, env):
                if step[1] == 1:
                    pool.wait_ge(v_ready, NT * (b + 1))
                    pool.wait_ge(pe["av"], NG * b)
                    hold(pool, passed_pool)
                    pool.tensor_copy(v_pad[:, :, :, 0:DH], v_new[:].rearrange("p t (h r) -> p t h r", r=DH)
                                     ).then_inc(v_placed, 1)

            def scatter(b, step, env):
                pool.wait_ge(S["slots"], b + 1)
                hold(pool, passed_pool)
                for k in range(NT * TOPK):
                    pool.indirect_dma_start(table[:, :], bass.IndirectOffsetOnAxis(ap=slot[:, k:k + 1], axis=0),
                                            entry[:, k, :], None).then_inc(scattered, 16)

            pool.wait_ge(table_set, 64)
            run(pool, {"qkv": qkv, "ffn": place_v, "rank": scatter})
            pool.wait_ge(scattered, 16 * NT * TOPK * BATCH)

        @block.scalar
        def _(act):
            def xT(nb, step, env):
                t, bank = step[1], env[0][step, 0][0]
                act.wait_ge(pe["xT"], NT * nb + t + 1)
                if t == 0 and not env[3]:
                    act.wait_ge(pe["up"], NM * nb)
                nc.scalar.activation(xn_t[:, :, t * P:(t + 1) * P],
                                     ps_g[bank][:, 0:D].rearrange("p (c n) -> p c n", c=KC), ACT.Copy
                                     ).then_inc(S["xn_t"], 1)

            def qkv(nb, step, env):
                t, bank = step[1], env[0][step, 1][0]
                act.wait_ge(pe["vr"], NT * nb + t + 1)
                if t == 0:
                    act.wait_ge(v_placed, nb)
                    if not env[3]:
                        act.wait_ge(chosen_ready, nb)
                nc.scalar.activation(v_new[:, t, :], ps_g[bank][:, 0:D], ACT.Copy).then_inc(v_ready, 1)
                nc.scalar.activation(logits[:, t, :], ps_g[bank][:, D:D + E], ACT.Copy).then_inc(S["logits"], 1)

            def partsT(nb, step, env):
                t = step[1]
                for k, (dst, p_, n) in enumerate(((q_t, "qT", "q_t"), (k_t, "kT", "k_t"))):
                    bank = env[0][step, k][0]
                    act.wait_ge(pe[p_], NT * nb + t + 1)
                    if t == 0 and k == 0:
                        for c in range(KC):
                            act.wait_ge(stacked[c], 16 * STACK_DMAS * nb)
                    nc.scalar.activation(
                        dst[:, :, :, t * P:(t + 1) * P].rearrange("p a c n -> p (a c) n"),
                        ps_g[bank][:, :].bitcast(BF16)[:, 0:NPART * D].rearrange("p (a n) -> p a n", n=P), ACT.Copy
                    ).then_inc(S[n], 1)

            def ffn(b, step, env):
                m = step[1]
                act.wait_ge(pe["gate"], NM * b + m + 1)
                if m >= 2:
                    act.wait_ge(S["hidden"], done("hidden", b, m - 2))
                else:
                    act.wait_ge(S["hidden"], NM * b)
                nc.scalar.activation(th[:, m % 2, :], ps_g[env[0][step, 0][0]][:, :], ACT.Tanh, scale=0.5
                                     ).then_inc(tanh_done, 1)

            def negT(b, step, env):
                g, bank = step[1], env[0][step, 0][0]
                act.wait_ge(pe["negT"], NG * b + g + 1)
                if g >= 2:
                    act.wait_ge(neg_rows[g % 2], 16 * NPART * (2 * b + g // 2))
                else:
                    act.wait_ge(neg_rows[g % 2], 16 * NPART * 2 * b)
                nc.scalar.activation(neg_t[:, g % 2, :], ps_g[bank][:, :].bitcast(BF16)[0:NPART * GH, 0:SEQ],
                                     ACT.Copy).then_inc(S["neg_t"], 1)

            def s2(b, step, env):
                _, g, u = step
                act.wait_ge(pe["s2"], NG * NU2 * b + NU2 * g + u + 1)
                if u == 0:
                    act.wait_ge(pe["av"], NG * b + (g - 1 if g >= 2 else 0))
                nc.scalar.activation(probs[g % 2][:, u, :], ps_u[env[1][step][0]][:, :, :].rearrange("p a n -> p (a n)"),
                                     ACT.Exp, scale=SCALE).then_inc(S["probs"], 1)

            def out_av(b, step, env):
                g = step[1]
                act.wait_ge(pe["av"], NG * b + g + 1)
                act.wait_ge(pe["avT"], NG * b + g)
                nc.scalar.activation(av[:, :], ps_av[:, :], ACT.Copy).then_inc(av_out, 1)

            def aT(b, step, env):
                p_, bank = step[1], env[0][step, 0][0]
                act.wait_ge(pe["aT"], 2 * b + p_ + 1)
                act.wait_ge(pe["sum"], 2 * b)
                nc.scalar.activation(
                    attn_t[:, :, 2 * p_ * P:2 * (p_ + 1) * P].rearrange("p c (t n) -> p t c n", t=2),
                    ps_g[bank][:, :].rearrange("p (t c n) -> p t c n", t=2, c=KC), ACT.Copy).then_inc(S["attn_t"], 1)

            def rank(b, step, env):
                act.wait_ge(ex_ready, b + 1)
                nc.scalar.activation(exo[:, :, :], ex[:, :, :], ACT.Exp).then_inc(exps, 1)

            act.wait_ge(table_set, 64)
            run(act, {"xT": xT, "qkv": qkv, "partsT": partsT, "ffn": ffn, "negT": negT, "s2": s2, "av": out_av, "aT": aT,
                      "rank": rank})

        @block.vector
        def _(dve):
            front = Chain(dve, dve_front, 2 + 3 + 3 * 4, passed_dve)
            back = Chain(dve, dve_chain, NM + 3 * NG + NG + 6 + 14, passed_dve)

            def ln(nb, step, env):
                dve.wait_ge(x_in, 16 * (nb + 1))
                dve.wait_ge(xn_ready, NT * nb)
                for t in range(NT):
                    ins = nc.vector.bn_stats(stats[:, t, :], xin[:, t, :])
                front.link(nb, ins, apart=True)
                for t in range(NT):
                    ins = nc.vector.bn_aggr(mv[:, t, :], stats[:, t, :])
                front.link(nb, ins)
                front.link(nb, nc.vector.tensor_scalar(ve[:], mv[:, :, 1], EPS, None, ALU.add))
                front.link(nb, nc.vector.tensor_scalar(rs_t[:].bitcast(I32), ve[:].bitcast(I32), 1, None,
                                                       ALU.arith_shift_right))
                front.link(nb, nc.vector.tensor_scalar(rs[:].bitcast(I32), rs_t[:].bitcast(I32), -1.0, MAGIC,
                                                       ALU.mult, ALU.add))
                for _ in range(4):
                    front.link(nb, nc.vector.scalar_tensor_tensor(out=rs_t[:], in0=rs[:], scalar=-0.5, in1=rs[:],
                                                                  op0=ALU.mult, op1=ALU.mult))
                    front.link(nb, nc.vector.tensor_tensor(rs_t[:], rs_t[:], ve[:], ALU.mult))
                    front.link(nb, nc.vector.scalar_tensor_tensor(out=rs[:], in0=rs_t[:], scalar=1.5, in1=rs[:],
                                                                  op0=ALU.add, op1=ALU.mult))
                front.closed()
                dve.wait_ge(xn_out, 16 * nb)
                dve.wait_ge(pe["xT"], NT * nb)
                for t in range(NT):
                    nc.vector.tensor_scalar(xn[:, t, :], xin[:, t, :], mv[:, t, 0:1], rs[:, t:t + 1], ALU.subtract,
                                            ALU.mult).then_inc(xn_ready, 1)

            def qkv(nb, step, env):
                t, bank = step[1], env[0][step, 0][0]
                dve.wait_ge(pe["qk"], NT * nb + t + 1)
                if not (env[3] and t < 2):
                    dve.wait_ge(parts_ready, NT * nb + t - 1)
                def halves(a):
                    return a.rearrange("p (g s c) -> p g s c", g=2 * KC, s=2)
                nc.vector.tensor_tensor(rp1[:, t % 2, :].rearrange("p (g c) -> p g c", c=P),
                                        ps_g[bank][:, :].rearrange("p (g c) -> p g c", c=P),
                                        cos[:, t:t + 1, :].broadcast_to([P, 2 * KC, P]), ALU.mult).then_inc(rope1, 1)
                nc.vector.tensor_tensor(halves(rp2[:, t % 2, :]), halves(ps_g[bank][:, :])[:, :, ::-1, :],
                                        sin[:, t:t + 1, :].rearrange("p o (s c) -> p o s c", s=2
                                                                     ).broadcast_to([P, 2 * KC, 2, P // 2]), ALU.mult
                                        ).then_inc(S["rope"], 1)

            def ffn(b, step, env):
                m = step[1]
                dve.wait_ge(tanh_done, NM * b + m + 1)
                dve.wait_ge(S["hidden"], NM * b + m)
                back.link(b, nc.vector.scalar_tensor_tensor(out=gth[:], in0=th[:, m % 2, :], scalar=1.0,
                                                            in1=ps_g[env[0][step, 0][0]][:, :], op0=ALU.add,
                                                            op1=ALU.mult))
                dve.wait_ge(pe["up"], NM * b + m + 1)
                dve.wait_ge(pe["sum"], 2 * b)
                nc.vector.scalar_tensor_tensor(out=hid[:, m, :], in0=gth[:], scalar=0.5,
                                               in1=ps_g[env[0][step, 1][0]][:, :], op0=ALU.mult, op1=ALU.mult
                                               ).then_inc(S["hidden"], 1)

            def s1(b, step, env):
                _, g, u = step
                i, h0, nh, per_bank = MAX_UNITS[u]
                ps = ps_u[env[1][step][0]]
                n = (i + 1) * P
                if u == 0:
                    dve.wait_ge(neg_parts, NG * b + max(0, g - 1))
                dve.wait_ge(pe["s1"], NG * NU1 * b + NU1 * g + u + 1)
                if per_bank > 1:
                    src = ps[:, 0:nh // per_bank, :].rearrange("p a (h n) -> p (a h) n", n=n)
                else:
                    src = ps[:, :, 0:n]
                nc.vector.tensor_reduce(neg[:, g % 2, i, h0:h0 + nh], src, AX.X, ALU.max, negate=True
                                        ).then_inc(S["row_max"], 1)

            def negsplit(b, step, env):
                g = step[1]
                dve.wait_ge(S["row_max"], done("row_max", b, NU1 * g + NU1 - 1))
                dve.wait_ge(pe["negT"], NG * b + max(0, g - 1))
                dve.wait_ge(neg_parts, NG * b + g)
                n_, np_ = neg[:, g % 2, :, :], neg_p[:, g % 2, :, :, :]
                back.link(b, nc.vector.tensor_copy(np_[:, :, 0, :], n_))
                back.link(b, nc.vector.tensor_tensor(neg_r[:], n_, np_[:, :, 0, :], ALU.subtract))
                back.link(b, nc.vector.tensor_copy(np_[:, :, 1, :], neg_r[:]))
                nc.vector.tensor_tensor(np_[:, :, 2, :], neg_r[:], np_[:, :, 1, :], ALU.subtract
                                        ).then_inc(neg_parts, 1)

            def avT(b, step, env):
                g, bank = step[1], env[0][step, 0][0]
                ps = ps_g[bank][:, :].rearrange("p (t h c) -> p t h c", t=NT, c=2 * DH)
                dve.wait_ge(pe["avT"], NG * b + g + 1)
                dve.wait_ge(pe["aT"], 2 * b)
                dve.wait_ge(S["attn"], NG * b + g)
                back.link(b, nc.vector.reciprocal(rden[:], ps[:, :, :, DH]))
                nc.vector.tensor_tensor(
                    attn[:, :, g * GH * DH:(g + 1) * GH * DH].rearrange("p t (h c) -> p t h c", c=DH),
                    ps[:, :, :, 0:DH], rden[:].rearrange("p t (h o) -> p t h o", o=1).broadcast_to([P, NT, GH, DH]),
                    ALU.mult).then_inc(S["attn"], 1)

            def oproj(b, step, env):
                p_, u = step[1], env[1][("down",)][0]
                dve.wait_ge(pe["sum"], 2 * b + p_ + 1)
                if p_ == 0:
                    dve.wait_ge(x_res, 16 * (b + 1))
                    dve.wait_ge(sum_out, 16 * b)
                nc.vector.tensor_tensor(osum[:, 2 * p_:2 * p_ + 2, :],
                                        ps_u[u][:, p_, :].rearrange("p (t n) -> p t n", t=2),
                                        xres[:, 2 * p_:2 * p_ + 2, :], ALU.add).then_inc(S["sums"], 1)

            def route(b, step, env):
                dve.wait_ge(S["logits"], done("logits", b, NT - 1))
                dve.wait_ge(exps, b)
                back.link(b, nc.vector.tensor_tensor(
                    lg[:], logits[:], bias_bc[:].rearrange("p (o e) -> p o e", o=1).broadcast_to([P, NT, E]), ALU.add), apart=True)
                for t in range(NT):
                    ins = nc.vector.max(top_v[:, t, :], lg[:, t, :])
                back.link(b, ins, apart=True)
                for t in range(NT):
                    ins = nc.vector.max_index(top_i[:, t, :], top_v[:, t, :], lg[:, t, :])
                back.link(b, ins)
                back.link(b, nc.vector.tensor_copy(top_f[:], top_i[:, :, 0:TOPK]))
                dve.wait_ge(scattered, 16 * NT * TOPK * b)
                back.link(b, nc.vector.tensor_tensor(
                    onehot[:].rearrange("p t j e -> p (t j) e"),
                    iota_e[:].rearrange("p (o e) -> p o e", o=1).broadcast_to([P, NT * TOPK, E]),
                    top_f[:].rearrange("p t (j o) -> p (t j) o", o=1).broadcast_to([P, NT * TOPK, E]), ALU.is_equal))
                dve.wait_ge(pe["rank"], b)
                with nc.allow_low_precision(reason="zeros and ones are exact"):
                    nc.vector.tensor_reduce(chosen[:], onehot[:].rearrange("p t j e -> p t e j"), AX.X, ALU.add
                                            ).then_inc(chosen_ready, 1)
                top1 = top_v[:, :, 0:1]
                nc.vector.tensor_tensor(ex[:, :, 0:E], lg[:], top1.broadcast_to([P, NT, E]), ALU.subtract)
                nc.vector.tensor_tensor(ex[:, :, E:E + TOPK], top_v[:, :, 0:TOPK],
                                        top1.broadcast_to([P, NT, TOPK]), ALU.subtract).then_inc(ex_ready, 1)
                back.link(b, nc.vector.tensor_tensor(base[:], counts[:], region[:], ALU.add))

            def rank(b, step, env):
                bank = env[0][step, 0][0]
                dve.wait_ge(S["slots"], b)
                dve.wait_ge(exps, b + 1)
                back.link(b, nc.vector.tensor_reduce(zs[:, 0, :], exo[:, :, 0:E], AX.X, ALU.add))
                back.link(b, nc.vector.reciprocal(zs[:, 1, :], zs[:, 0, :]))

                def bc(a):
                    return a.rearrange("p (t o) -> p t o", o=1).broadcast_to([P, NT, TOPK])
                back.link(b, nc.vector.tensor_tensor(pr4[:], exo[:, :, E:E + TOPK], bc(zs[:, 1, :]), ALU.mult))
                back.link(b, nc.vector.tensor_reduce(zs[:, 2, :], pr4[:], AX.X, ALU.add))
                back.link(b, nc.vector.tensor_scalar(zs[:, 2, :], zs[:, 2, :], 1e-12, None, ALU.max))
                back.link(b, nc.vector.reciprocal(zs[:, 3, :], zs[:, 2, :]))
                back.link(b, nc.vector.tensor_tensor(
                    entry[:, :, 2].bitcast(F32).rearrange("p (t j) -> p t j", t=NT), pr4[:], bc(zs[:, 3, :]), ALU.mult))
                dve.wait_ge(pe["rank"], b + 1)
                ps = ps_g[bank][:, 0:NT * E].rearrange("p (t e) -> p t e", t=NT)
                back.link(b, nc.vector.tensor_tensor(
                    pos[:], ps, base[:].rearrange("p (o e) -> p o e", o=1).broadcast_to([P, NT, E]), ALU.add))
                back.link(b, nc.vector.tensor_tensor(counts[:], counts[:], ps_g[bank][:, NT * E:(NT + 1) * E], ALU.add))
                for t in range(NT):
                    ins = nc.vector.tensor_tensor(onehot[:, t, :, :], onehot[:, t, :, :],
                                                  pos[:, t:t + 1, :].broadcast_to([P, TOPK, E]), ALU.mult)
                back.link(b, ins)
                back.link(b, nc.vector.tensor_reduce(slotf[:], onehot[:].rearrange("p t j e -> p (t j) e"), AX.X,
                                                     ALU.add))
                back.link(b, nc.vector.tensor_copy(entry[:, :, 0], token_f[:]))
                nc.vector.tensor_copy(entry[:, :, 1], dest_f[:])
                back.link(b, nc.vector.tensor_scalar(token_f[:], token_f[:], float(SEQ), None, ALU.add))
                back.link(b, nc.vector.tensor_scalar(dest_f[:], dest_f[:], float(SEQ * TOPK), None, ALU.add))
                nc.vector.tensor_copy(slot[:], slotf[:]).then_inc(S["slots"], 1)

            dve.wait_ge(consts, N_CONSTS)
            dve.wait_ge(weights, 16 * 7)
            nc.vector.tensor_scalar(region[:], iota_e[:], float(REGION), None, ALU.mult)
            run(dve, {"ln": ln, "qkv": qkv, "ffn": ffn, "s1": s1, "negsplit": negsplit, "avT": avT, "oproj": oproj,
                      "route": route, "rank": rank})
            back.closed()

        @block.tensor
        def _(pe_):
            def bank_of(step, k, env):
                bp, up, b, first = env
                bank, prev = bp[step, k]
                if prev is not None:
                    name, idx, nxt = prev
                    pe_.wait_ge(S[name], done(name, b + 1 if nxt and not first else b, idx))
                elif not first:
                    for name, n in TIMES.items():
                        if name in ("xn_t", "rope", "logits", "q_t", "k_t"):
                            pe_.wait_ge(S[name], n * (b + 1))
                        elif name in ("hidden", "neg_t", "attn", "attn_t", "slots"):
                            pe_.wait_ge(S[name], n * b)
                return ps_g[bank]

            def unit_of(step, env):
                bp, up, b, first = env
                unit, prev = up[step]
                if prev is not None:
                    name, idx = prev
                    pe_.wait_ge(S[name], done(name, b, idx))
                else:
                    for name in ("row_max", "probs", "sums"):
                        pe_.wait_ge(S[name], TIMES[name] * b)
                return ps_u[unit]

            def xT(nb, step, env):
                t = step[1]
                ps = bank_of(step, 0, env)
                pe_.wait_ge(xn_ready, NT * nb + t + 1)
                for c in range(KC):
                    ins = nc.tensor.transpose(ps[:, c * P:(c + 1) * P], xn[:, t, c * P:(c + 1) * P], ident[:])
                ins.then_inc(pe["xT"], 1)

            def qkv(nb, step, env):
                t = step[1]
                pe_.wait_ge(S["xn_t"], done("xn_t", nb, t))
                for k, (name, lo, n) in enumerate((("qk", 0, 2 * D), ("vr", 2 * D, D + E))):
                    ps = bank_of(step, k, env)
                    for c in range(KC):
                        ins = nc.tensor.matmul(ps[:, 0:n], xn_t[:, c, t * P:(t + 1) * P], w_qkvr[:, c, lo:lo + n],
                                               start=(c == 0), stop=(c == KC - 1))
                    ins.then_inc(pe[name], 1)

            def partsT(nb, step, env):
                t = step[1]
                pe_.wait_ge(parts_ready, NT * nb + t + 1)
                for k, name in enumerate(("qT", "kT")):
                    ps = bank_of(step, k, env)[:, :].bitcast(BF16)
                    for a in range(NPART * KC):
                        lo = D * k + P * (a % KC)
                        ins = nc.tensor.transpose(ps[:, a * P:(a + 1) * P], parts[:, t % 2, a // KC, lo:lo + P],
                                                  identb[:])
                    ins.then_inc(pe[name], 1)

            def ffn(b, step, env):
                m = step[1]
                for k, name in enumerate(("gate", "up")):
                    ps = bank_of(step, k, env)
                    for c in range(KC):
                        lo = HS * k + P * m
                        ins = nc.tensor.matmul(ps[:, :], w_gu[:, c, lo:lo + P], xn_t[:, c, :], start=(c == 0),
                                               stop=(c == KC - 1))
                    ins.then_inc(pe[name], 1)

            def s1(b, step, env):
                _, g, u = step
                i, h0, nh, per_bank = MAX_UNITS[u]
                ps = unit_of(step, env)
                if u == 0 and g % 2 == 0:
                    pe_.wait_ge(stacked[g // 2], 16 * STACK_DMAS * (b + 1))
                n = (i + 1) * P
                for a in range(nh // per_bank):
                    for k in range(per_bank):
                        h = GH * g + h0 + a * per_bank + k
                        nc.tensor.matmul(ps[:, a, k * n:(k + 1) * n], q_st[0:KROWS, h, i * P:(i + 1) * P],
                                         k_st[0:KROWS, h, 0:n], start=(k == 0), stop=False, skip_group_check=True)
                    dst = ps[:, a, 0:per_bank * n].rearrange("p (k n) -> p k n", n=n)[:, :, n - P:n]
                    ins = nc.tensor.matmul(dst, identb[:],
                                           mask_qk[:].rearrange("p (o n) -> p o n", o=1).broadcast_to([P, per_bank, P]),
                                           start=False, stop=True, skip_group_check=True)
                ins.then_inc(pe["s1"], 1)

            def negT(b, step, env):
                g = step[1]
                ps = bank_of(step, 0, env)[:, :].bitcast(BF16)
                pe_.wait_ge(neg_parts, NG * b + g + 1)
                for t in range(NT):
                    ins = nc.tensor.transpose(ps[0:NPART * GH, t * P:(t + 1) * P],
                                              neg_p[:, g % 2, t, :, :].rearrange("p a h -> p (a h)"), identb[:])
                ins.then_inc(pe["negT"], 1)

            def s2(b, step, env):
                _, g, u = step
                ps = unit_of(step, env)
                if u == 0:
                    pe_.wait_ge(neg_rows[g % 2], 16 * NPART * (2 * b + g // 2 + 1))
                if u < GH:
                    pieces = [(0, 0, 0, GH * g + u), (1, 0, 1, GH * g + u), (1, 3 * P, 3, GH * g + u)]
                    masks = [(0, SEQ, 1), (1, 3 * P, 2)]
                else:
                    pieces = [(j // 2, (j % 2) * 2 * P, 2, GH * g + j) for j in range(GH)]
                    masks = [(0, 2 * P, 2), (1, 2 * P, 2)]
                for n_, (a, lo, kt, h) in enumerate(pieces):
                    n = SEQ - kt * P
                    nc.tensor.matmul(ps[:, a, lo:lo + n], k_st[0:MROWS, h, kt * P:(kt + 1) * P],
                                     q_st[0:MROWS, h, kt * P:SEQ], start=(lo == 0), stop=False, skip_group_check=True)
                for a, step_, cnt in masks:
                    if cnt == 1:
                        dst, rhs = ps[:, a, 0:P], mask_kq[:]
                    else:
                        if step_ == 3 * P:
                            dst = ps[:, a, :].rearrange("p (k n) -> p k n", n=P)[:, 0:NT:3, :]
                        else:
                            dst = ps[:, a, :].rearrange("p (k n) -> p k n", n=step_)[:, :, 0:P]
                        rhs = mask_kq[:].rearrange("p (o n) -> p o n", o=1).broadcast_to([P, cnt, P])
                    ins = nc.tensor.matmul(dst, identb[:], rhs, start=False, stop=True, skip_group_check=True)
                ins.then_inc(pe["s2"], 1)

            def av_(b, step, env):
                g = step[1]
                pe_.wait_ge(S["probs"], done("probs", b, NU2 * g + NU2 - 1))
                pe_.wait_ge(av_out, NG * b + g)
                if g == 0:
                    pe_.wait_ge(v_placed, b + 1)
                pr = probs[g % 2]
                for kt in range(NT):
                    n = SEQ - kt * P
                    for j in range(GH):
                        if kt == 2:
                            rhs = pr[:, GH, j * 2 * P:j * 2 * P + n]
                        else:
                            lo = {0: 0, 1: SEQ, 3: SEQ + 3 * P}[kt]
                            rhs = pr[:, j, lo:lo + n]
                        ins = nc.tensor.matmul(ps_av[2 * DH * j:2 * DH * (j + 1), kt * P:SEQ],
                                               v_pad[:, kt, GH * g + j, :], rhs, start=(kt == 0), stop=(kt == NT - 1),
                                               skip_group_check=True)
                ins.then_inc(pe["av"], 1)

            def avT(b, step, env):
                g = step[1]
                ps = bank_of(step, 0, env)
                pe_.wait_ge(av_out, NG * b + g + 1)
                for t in range(NT):
                    ins = nc.tensor.transpose(ps[:, t * P:(t + 1) * P], av[:, t * P:(t + 1) * P], ident[:])
                ins.then_inc(pe["avT"], 1)

            def aT(b, step, env):
                p_ = step[1]
                ps = bank_of(step, 0, env)
                pe_.wait_ge(S["attn"], done("attn", b, NG - 1))
                for t in range(2):
                    for c in range(KC):
                        lo = (t * KC + c) * P
                        ins = nc.tensor.transpose(ps[:, lo:lo + P], attn[:, 2 * p_ + t, c * P:(c + 1) * P], ident[:])
                ins.then_inc(pe["aT"], 1)

            def down(b, step, env):
                ps = unit_of(step, env)
                pe_.wait_ge(S["hidden"], done("hidden", b, NM - 1))
                for t in range(NT):
                    for m in range(NM):
                        nc.tensor.matmul(ps[:, t // 2, (t % 2) * D:(t % 2 + 1) * D], hid[:, m, t * P:(t + 1) * P],
                                         w_d[:, m, :], start=(t % 2 == 0 and m == 0), stop=False,
                                         skip_group_check=True)

            def oproj(b, step, env):
                p_ = step[1]
                ps = ps_u[env[1][("down",)][0]]
                pe_.wait_ge(S["attn_t"], done("attn_t", b, p_))
                for t in (2 * p_, 2 * p_ + 1):
                    for c in range(KC):
                        ins = nc.tensor.matmul(ps[:, p_, (t % 2) * D:(t % 2 + 1) * D], attn_t[:, c, t * P:(t + 1) * P],
                                               w_o[:, c, :], start=False, stop=(c == KC - 1), skip_group_check=True)
                ins.then_inc(pe["sum"], 1)

            def rank(b, step, env):
                ps = bank_of(step, 0, env)
                pe_.wait_ge(chosen_ready, b + 1)
                ch = chosen[:].rearrange("p t e -> p (t e)")
                nc.tensor.matmul(ps[:, 0:NT * E], before[:], ch, start=True, stop=False, skip_group_check=True)
                for k in range(1, NT):
                    nc.tensor.matmul(ps[:, k * E:NT * E], ones[:], ch[:, 0:(NT - k) * E], start=False, stop=False,
                                     skip_group_check=True)
                for k in range(NT):
                    ins = nc.tensor.matmul(ps[:, NT * E:(NT + 1) * E], ones[:], ch[:, k * E:(k + 1) * E], start=False,
                                           stop=(k == NT - 1), skip_group_check=True)
                ins.then_inc(pe["rank"], 1)

            pe_.wait_ge(consts, N_CONSTS)
            pe_.wait_ge(weights, 16 * 7)
            run(pe_, {"xT": xT, "qkv": qkv, "partsT": partsT, "ffn": ffn, "s1": s1, "negT": negT, "s2": s2, "av": av_,
                      "avT": avT, "aT": aT, "down": down, "oproj": oproj, "rank": rank})


def phase_bcd(nc, sb_, sem, ident, iota_e, counts, ps_g, ps_u, ps_av, wgu_e, wd_e, xn_dram, sum_dram, table, y_dram,
              out):
    stack = ExitStack()
    with stack:
        def sb(name, shape, dt=F32):
            return sb_(name, shape, dt, stack)

        w_gu = sb("we_gu", [P, E, KC, 2 * HE])
        w_d = sb("we_d", [P, E, D])
        nb_i = sb("nb_i", [P, E], I32)
        nb_f = sb("nb_f", [P, E])
        nb_c = sb("nb_c", [E, 2])
        tri = sb("tri", [E, E])
        one_c = sb("one_c", [E, 1])
        blk_i = sb("blk_i", [E, NBLOCK])
        past = sb("past", [E, NBLOCK])
        row_f = sb("row_f", [1, 2, NBLOCK])
        start_row = sb("start_row", [1, NBLOCK], I32)
        expert = sb("expert", [1, NBLOCK], I32)

        NR = 16
        ent = [sb(f"ent{i}", [P, 4], I32) for i in range(NR)]
        xg = [sb(f"xg{i}", [P, D]) for i in range(NR)]
        x_t = [sb(f"x_t{i}", [P, D]) for i in range(2)]
        tnh = [sb(f"tnh{i}", [P, HE]) for i in range(2)]
        gt = [sb(f"gt{i}", [P, HE]) for i in range(2)]
        hw = [sb(f"hw{i}", [P, HE]) for i in range(2)]
        wh = [sb(f"wh{i}", [P, 1]) for i in range(2)]
        h_t = [sb(f"h_t{i}", [P, HE]) for i in range(2)]
        yb = [sb(f"yb{i}", [P, D]) for i in range(NR)]
        ps_x, ps_gu = [ps_g[0], ps_g[1]], [ps_g[2], ps_av]
        ps_h = [ps_u[0][:, i, :] for i in range(2)]
        ps_y = [ps_u[1][:, i, :] for i in range(2)]

        ws, plan, plan_pe, ready = sem("ws"), sem("plan"), sem("plan_pe"), sem("ready")
        c_pool = sem("c_pool")
        passed, passed_s = sem("passed"), sem("passed_s")
        ent_in = [sem(f"ent_in{i}") for i in range(NR)]
        gathered = [sem(f"gathered{i}") for i in range(NR)]
        y_out = [sem(f"y_out{i}") for i in range(NR)]
        xt_ps, gu_ps, ht_ps, y_ps = sem("xt_ps"), sem("gu_ps"), sem("ht_ps"), sem("y_ps")
        xt_sb, tanh_sb, gate_sb, h_sb, ht_sb, y_sb = [sem(n) for n in
                                                      ("xt_sb", "tanh_sb", "gate_sb", "h_sb", "ht_sb", "y_sb")]
        block = stack.enter_context(nc.Block())
        assert NBLOCK % NR == 0

        def expert_loop(eng, before, stage, after):
            before()
            for n in range(NR):
                stage(n, n, True)
            with eng.Fori(1, NBLOCK // NR) as i:
                for k in range(NR):
                    stage(i * NR + k, k, False)
            after()

        @block.sync
        def _(sp):
            sp.wait_ge(ready, 1)

            def before():
                pass

            def stage(n, k, first):
                row = sp.value_load(start_row[0:1, bass.ds(n, 1)], min_val=0, max_val=TABLE - P)
                if not first:
                    sp.wait_ge(y_out[k], (n - k) * (16 // NR))
                    hold(sp, passed_s)
                sp.dma_start(ent[k][:, :], table[bass.ds(row, P), :]).then_inc(ent_in[k], 16)
            expert_loop(sp, before, stage, lambda: None)

        @block.scalar
        def _(act):
            for q in range(4):
                e0 = q * E // 4
                act.dma_start(w_gu[:, e0:e0 + E // 4, :, :].rearrange("p e c n -> p (e c) n"),
                              wgu_e[e0:e0 + E // 4, :, :].rearrange("e (c p) n -> p (e c) n", p=P)).then_inc(ws, 16)
                act.dma_start(w_d[:, e0:e0 + E // 4, :], wd_e[e0:e0 + E // 4, :, :].rearrange("e p n -> p e n")
                              ).then_inc(ws, 16)

            def stage(n, k, first):
                s = k % 2
                act.wait_ge(gu_ps, n + 1)
                if not (first and k < 2):
                    act.wait_ge(gate_sb, n - 1)
                nc.scalar.activation(tnh[s][:], ps_gu[s][:, 0:HE], ACT.Tanh, scale=0.5).then_inc(tanh_sb, 1)
                act.wait_ge(ht_ps, n + 1)
                if not (first and k < 2):
                    act.wait_ge(y_ps, n - 1)
                nc.scalar.activation(h_t[s][:], ps_h[s][:, 0:P], ACT.Copy).then_inc(ht_sb, 1)
                act.wait_ge(y_ps, n + 1)
                if not first:
                    act.wait_ge(y_out[k], (n - k) * (16 // NR))
                nc.scalar.activation(yb[k][:], ps_y[s][:, 0:D], ACT.Copy).then_inc(y_sb, 1)
            expert_loop(act, lambda: None, stage, lambda: None)

        @block.gpsimd
        def _(pool):
            pool.iota(blk_i[:], pattern=[[1, NBLOCK]], base=0, channel_multiplier=0,
                      allow_small_or_imprecise_dtypes=True).then_inc(c_pool, 1)
            pool.memset(one_c[:], 1.0).then_inc(c_pool, 1)
            pool.memset(tri[:], 0.0).then_inc(c_pool, 1)
            pool.wait_ge(c_pool, 3)
            pool.affine_select(out=tri[:], in_=tri[:], compare_op=ALU.is_ge, fill=1.0, base=-1,
                               pattern=[[-1, E]], channel_multiplier=1).then_inc(c_pool, 1)
            LAG = 8

            def gather(n, k, first):
                pool.wait_ge(ent_in[k], (n - k) * (16 // NR) + 16)
                if not first:
                    pool.wait_ge(xt_ps, n - NR + 1)
                hold(pool, passed)
                pool.indirect_dma_start(xg[k][:, :], None, xn_dram[:, :],
                                        bass.IndirectOffsetOnAxis(ap=ent[k][:, 0:1], axis=0)).then_inc(gathered[k], 16)

            def scatter(n, k):
                pool.wait_ge(y_sb, n + 1)
                hold(pool, passed)
                pool.indirect_dma_start(y_dram[:, :], bass.IndirectOffsetOnAxis(ap=ent[k][:, 1:2], axis=0),
                                        yb[k][:, :], None, bounds_check=TOKENS * TOPK - 1, oob_is_err=False
                                        ).then_inc(y_out[k], 16)

            for n in range(NR):
                gather(n, n, True)
                if n >= LAG:
                    scatter(n - LAG, n - LAG)
            with pool.Fori(1, NBLOCK // NR) as i:
                for k in range(NR):
                    m = i * NR + k - LAG
                    gather(i * NR + k, k, False)
                    scatter(m, (k - LAG) % NR)
            for n in range(NBLOCK - LAG, NBLOCK):
                scatter(n, n % NR)
            for k in range(NR):
                pool.wait_ge(y_out[k], 16 * NBLOCK // NR)

        @block.tensor
        def _(pe):
            pe.wait_ge(plan, 1)
            nc.tensor.transpose(ps_g[0][0:E, 0:P], nb_f[:], ident[:]).then_inc(plan_pe, 1)
            pe.wait_ge(plan, 2)
            pe.wait_ge(c_pool, 4)
            nc.tensor.matmul(ps_g[1][0:E, 0:1], tri[:], nb_c[:, 0:1], start=True, stop=True).then_inc(plan_pe, 1)
            pe.wait_ge(plan, 4)
            nc.tensor.matmul(ps_g[0][0:1, 0:NBLOCK], one_c[:], past[:], start=True, stop=True)
            nc.tensor.matmul(ps_g[2][0:1, 0:NBLOCK], nb_c[:, 0:1], past[:], start=True, stop=True).then_inc(plan_pe, 1)
            pe.wait_ge(ready, 1)
            pe.wait_ge(ws, 16 * 8)

            def xT(n, k, first):
                s = k % 2
                pe.wait_ge(gathered[k], (n - k) * (16 // NR) + 16)
                if not (first and k < 2):
                    pe.wait_ge(xt_sb, n - 1)
                for c in range(KC):
                    ins = nc.tensor.transpose(ps_x[s][:, c * P:(c + 1) * P], xg[k][:, c * P:(c + 1) * P], ident[:])
                ins.then_inc(xt_ps, 1)

            def gu(n, k, first):
                s = k % 2
                e = pe.value_load(expert[0:1, bass.ds(n, 1)], min_val=0, max_val=E - 1)
                pe.wait_ge(xt_sb, n + 1)
                if not (first and k < 2):
                    pe.wait_ge(h_sb, n - 1)
                for c in range(KC):
                    ins = nc.tensor.matmul(ps_gu[s][:, 0:2 * HE], x_t[s][:, c * P:(c + 1) * P],
                                           w_gu[:, bass.ds(e, 1), c, :], start=(c == 0), stop=(c == KC - 1))
                ins.then_inc(gu_ps, 1)

            def hT(n, k, first):
                s = k % 2
                pe.wait_ge(h_sb, n + 1)
                if not (first and k < 2):
                    pe.wait_ge(ht_sb, n - 1)
                nc.tensor.transpose(ps_h[s][:, 0:P], hw[s][:], ident[:]).then_inc(ht_ps, 1)

            def y(n, k, first):
                s = k % 2
                e = pe.value_load(expert[0:1, bass.ds(n, 1)], min_val=0, max_val=E - 1)
                pe.wait_ge(ht_sb, n + 1)
                if not (first and k < 2):
                    pe.wait_ge(y_sb, n - 1)
                nc.tensor.matmul(ps_y[s][:, 0:D], h_t[s][:], w_d[:, bass.ds(e, 1), :], start=True, stop=True
                                 ).then_inc(y_ps, 1)

            xT(0, 0, True)
            for n in range(NR):
                gu(n, n, True)
                if n >= 1:
                    hT(n - 1, n - 1, True)
                xT(n + 1, (n + 1) % NR, n + 1 < NR)
                if n >= 1:
                    y(n - 1, n - 1, True)
            with pe.Fori(1, NBLOCK // NR - 1) as i:
                for k in range(NR):
                    n = i * NR + k
                    gu(n, k, False)
                    hT(n - 1, (k - 1) % NR, False)
                    xT(n + 1, (k + 1) % NR, False)
                    y(n - 1, (k - 1) % NR, False)
            for n in range(NBLOCK - NR, NBLOCK):
                gu(n, n % NR, False)
                hT(n - 1, (n - 1) % NR, False)
                if n + 1 < NBLOCK:
                    xT(n + 1, (n + 1) % NR, False)
                y(n - 1, (n - 1) % NR, False)
            hT(NBLOCK - 1, NR - 1, False)
            y(NBLOCK - 1, NR - 1, False)

        @block.vector
        def _(dve):
            dchain = sem("plan_dve")
            n_ = [0]

            def link(ins):
                n_[0] += 1
                ins.then_inc(dchain, 1)
                dve.wait_ge(dchain, n_[0])
            link(nc.vector.tensor_scalar(nb_f[:], counts[:], float(P - 1), None, ALU.add))
            link(nc.vector.tensor_copy(nb_i[:], nb_f[:]))
            link(nc.vector.tensor_scalar(nb_i[:], nb_i[:], 7, None, ALU.arith_shift_right))
            nc.vector.tensor_copy(nb_f[:], nb_i[:]).then_inc(plan, 1)
            dve.wait_ge(plan_pe, 1)
            nc.vector.tensor_copy(nb_c[:, 0:1], ps_g[0][0:E, 0:1]).then_inc(plan, 1)
            dve.wait_ge(plan_pe, 2)
            nc.vector.tensor_copy(nb_c[:, 1:2], ps_g[1][0:E, 0:1]).then_inc(plan, 1)
            dve.wait_ge(plan, 3)
            dve.wait_ge(c_pool, 4)
            nc.vector.tensor_scalar(past[:], blk_i[:], nb_c[:, 1:2], None, ALU.is_ge).then_inc(plan, 1)
            dve.wait_ge(plan_pe, 3)
            link(nc.vector.tensor_tensor(row_f[:, 0, :], blk_i[0:1, :], ps_g[2][0:1, 0:NBLOCK], ALU.subtract))
            link(nc.vector.tensor_scalar(row_f[:, 0, :], row_f[:, 0, :], float(P), None, ALU.mult))
            link(nc.vector.scalar_tensor_tensor(out=row_f[:, 1, :], in0=ps_g[0][0:1, 0:NBLOCK], scalar=float(REGION),
                                                in1=row_f[:, 0, :], op0=ALU.mult, op1=ALU.add))
            link(nc.vector.tensor_copy(start_row[:], row_f[:, 1, :]))
            link(nc.vector.tensor_scalar(row_f[:, 0, :], ps_g[0][0:1, 0:NBLOCK], float(E - 1), None, ALU.min))
            nc.vector.tensor_copy(expert[:], row_f[:, 0, :]).then_inc(ready, 1)

            def front(n, k, first):
                s = k % 2
                dve.wait_ge(xt_ps, n + 1)
                if not (first and k < 2):
                    dve.wait_ge(gu_ps, n - 1)
                nc.vector.tensor_copy(x_t[s][:], ps_x[s][:, 0:D]).then_inc(xt_sb, 1)

            def stage(n, k, first):
                s = k % 2
                dve.wait_ge(tanh_sb, n + 1)
                if not (first and k < 2):
                    dve.wait_ge(h_sb, n - 1)
                nc.vector.tensor_scalar(wh[s][:], ent[k][:, 2:3].bitcast(F32), 0.5, None, ALU.mult)
                nc.vector.scalar_tensor_tensor(out=gt[s][:], in0=tnh[s][:], scalar=1.0, in1=ps_gu[s][:, 0:HE],
                                               op0=ALU.add, op1=ALU.mult).then_inc(gate_sb, 1)
                dve.wait_ge(gate_sb, n + 1)
                if not (first and k < 2):
                    dve.wait_ge(ht_ps, n - 1)
                nc.vector.scalar_tensor_tensor(out=hw[s][:], in0=gt[s][:], scalar=wh[s][:, 0:1],
                                               in1=ps_gu[s][:, HE:2 * HE], op0=ALU.mult, op1=ALU.mult
                                               ).then_inc(h_sb, 1)
            front(0, 0, True)
            for n in range(NR):
                front(n + 1, (n + 1) % NR, n + 1 < NR)
                stage(n, n, True)
            with dve.Fori(1, NBLOCK // NR - 1) as i:
                for k in range(NR):
                    front(i * NR + k + 1, (k + 1) % NR, False)
                    stage(i * NR + k, k, False)
            for n in range(NBLOCK - NR, NBLOCK):
                if n + 1 < NBLOCK:
                    front(n + 1, (n + 1) % NR, False)
                stage(n, n % NR, False)

    stack = ExitStack()
    with stack:
        NTILE = TOKENS // P
        ND = 4
        ys = [sb_(f"ys{i}", [P, TOPK, D], F32, stack) for i in range(ND)]
        acc = [sb_(f"acc{i}", [P, D], F32, stack) for i in range(ND)]
        red = [sb_(f"red{i}", [P, 2, D], F32, stack) for i in range(ND)]
        res = [sb_(f"res{i}", [P, D], F32, stack) for i in range(ND)]
        y_in = [sem(f"y_in{i}") for i in range(ND)]
        stored = [sem(f"stored{i}") for i in range(ND)]
        half, added = sem("half"), sem("added")
        added_p, half_p = sem("added_p"), sem("half_p")
        block = stack.enter_context(nc.Block())
        y_v = y_dram.rearrange("(n p j) d -> n p j d", p=P, j=TOPK)

        def tiles(eng, stage):
            for n in range(ND):
                stage(n, n, True)
            with eng.Fori(1, NTILE // ND) as i:
                for k in range(ND):
                    stage(i * ND + k, k, False)

        @block.sync
        def _(sp):
            def load(n, k, first):
                if not first:
                    sp.wait_ge(added, n - ND + 1)
                sp.dma_start(ys[k][:, :, :], y_dram[bass.ds(n * (P * TOPK), P * TOPK), :].rearrange(
                    "(p j) d -> p j d", j=TOPK)).then_inc(y_in[k], 16)
                sp.dma_start(acc[k][:, :], sum_dram[bass.ds(n * P, P), :]).then_inc(y_in[k], 16)
            tiles(sp, load)

        @block.scalar
        def _(act):
            def store(n, k, first):
                act.wait_ge(added, n + 1)
                act.dma_start(out[bass.ds(n * P, P), :], res[k][:, :]).then_inc(stored[k], 16)
            tiles(act, store)
            for k in range(ND):
                act.wait_ge(stored[k], 16 * NTILE // ND)

        @block.vector
        def _(dve):
            def add(n, k, first):
                dve.wait_ge(y_in[k], (n - k) * (32 // ND) + 32)
                if not first:
                    dve.wait_ge(added, n - ND + 1)
                nc.vector.tensor_tensor(red[k][:], ys[k][:, 0:2, :], ys[k][:, 2:4, :], ALU.add).then_inc(half, 1)
                dve.wait_ge(half, 2 * n + 1)
                nc.vector.tensor_tensor(red[k][:, 0, :], red[k][:, 0, :], red[k][:, 1, :], ALU.add).then_inc(half, 1)
                dve.wait_ge(half, 2 * n + 2)
                if not first:
                    dve.wait_ge(stored[k], (n - k) * (16 // ND))
                nc.vector.tensor_tensor(res[k][:], red[k][:, 0, :], acc[k][:], ALU.add).then_inc(added, 1)
            tiles(dve, add)


def _rope_tables():
    inv = (1.0 / np.float32(10000.0) ** (np.arange(0, DH, 2, dtype=np.float32) / np.float32(DH))).astype(np.float32)
    ang = np.outer(np.arange(SEQ, dtype=np.float32), inv).astype(np.float32)
    c, s = np.cos(ang).astype(np.float32), np.sin(ang).astype(np.float32)
    per_head = P // DH
    return np.repeat(np.concatenate([c, c], 1), per_head, 1), np.repeat(np.concatenate([-s, s], 1), per_head, 1)


def _dims_first(w):
    return w.reshape(D, KC, P // DH, DH).transpose(0, 1, 3, 2).reshape(D, D)


def kernel(**inputs):
    import concourse.bacc as bacc
    from concourse.bass_utils import run_bass_kernel_spmd

    a = {k: np.asarray(v) for k, v in inputs.items()}
    cos, sin = _rope_tables()
    arrays = {
        "x": a["L0_attn_x"].reshape(TOKENS, D),
        "wqkvr": np.concatenate([_dims_first(a["L0_attn_Wq"].T), _dims_first(a["L0_attn_Wk"].T), a["L0_attn_Wv"].T, a["L0_ffn_router_w"].T], 1),
        "wo": a["L0_attn_Wo"].T,
        "wgu_s": np.concatenate([a["L0_ffn_sgate_w"].T, a["L0_ffn_sup_w"].T], 1),
        "wd_s": a["L0_ffn_sdown_w"].T,
        "bias": a["L0_ffn_router_bias"],
        "wgu_e": np.concatenate([a["L0_ffn_gate_w"].transpose(0, 2, 1), a["L0_ffn_up_w"].transpose(0, 2, 1)], 2),
        "wd_e": a["L0_ffn_down_w"].transpose(0, 2, 1),
        "rope_cos": cos,
        "rope_sin": sin,
    }
    arrays = {k: np.ascontiguousarray(v) for k, v in arrays.items()}
    nc = bacc.Bacc("TRN2", target_bir_lowering=False, num_devices=1)
    args = [nc.dram_tensor(k, v.shape, mybir.dt.from_np(v.dtype), kind="ExternalInput").ap() for k, v in arrays.items()]
    out = nc.dram_tensor("out", (TOKENS, D), F32, kind="ExternalOutput").ap()
    block_kernel(nc, *args, out)
    r = run_bass_kernel_spmd(nc, [arrays], core_ids=[0])
    return r.results[0]["out"].reshape(BATCH, SEQ, D)
```

```python
from contextlib import ExitStack

import numpy as np

import concourse.bass as bass
from concourse import mybir

F32 = mybir.dt.float32
BF16 = mybir.dt.bfloat16
I32 = mybir.dt.int32
U32 = mybir.dt.uint32
ALU = mybir.AluOpType
ACT = mybir.ActivationFunctionType
AX = mybir.AxisListType

P = 128
BATCH, SEQ, D = 16, 512, 256
NT = SEQ // P
KC = D // P
NH, DH = 16, 16
NG, GH = 4, 4
E, TOPK, HE, HS = 32, 4, 128, 512
NM = HS // P
TOKENS = BATCH * SEQ
NPART = 3
Q_PART = [0, 0, 0, 1, 1, 2]
K_PART = [0, 1, 2, 0, 1, 0]
NSTACK = len(Q_PART)
KROWS = NSTACK * DH
MROWS = KROWS + NPART
SCALE = DH ** -0.5
NEG = -1e30
REGION = TOKENS
NBLOCK = TOKENS * TOPK // P + E
TABLE = E * REGION + P
N_CONSTS = 21
SKIP = 1 << 24
EPS = 1e-5
MAGIC = float(0x5F3759DF)

MAX_UNITS = [(0, 0, 4, 4), (1, 0, 4, 2), (2, 0, 2, 1), (2, 2, 2, 1), (3, 0, 2, 1), (3, 2, 2, 1)]
NU1 = len(MAX_UNITS)
NU2 = GH + 1


def hold(eng, passed):
    eng.sem_inc(passed, 1)


def attention_steps(with_next):
    def nxt(*steps):
        return list(steps) if with_next else []

    s = [("gate", 0), ("s1", 0, 0), ("up", 0), ("rankC",), ("placeV",), ("s1", 0, 1), ("gate", 1), ("copy",), ("s1", 0, 2),
         ("up", 1), ("scat", 0), ("s1", 0, 3), ("gate", 2), ("s1", 0, 4)] + nxt(("lnA",)) + [("s1", 0, 5), ("scat", 1),
         ("negsplit", 0)]
    fill = {
        1: [[("up", 2)], [("gate", 3)] + nxt(("lnB",)), [("up", 3)] + nxt(("lnC",)), nxt(("xT", 0), ("xT", 1)),
            nxt(("xT", 2), ("xT", 3)), nxt(("qk", 0)), nxt(("vr", 0), ("part0", 0)), nxt(("qk", 1), ("part1", 0))],
        2: [nxt(("vr", 1)), [("av", 0, 0), ("av", 0, 1)] + nxt(("part0", 1)), [("av", 0, 2), ("av", 0, 3)],
            nxt(("partsT", 0), ("part1", 1)), [("avT", 0)], nxt(("qk", 2)), nxt(("partsT", 1), ("part0", 2)),
            nxt(("qk", 3), ("part1", 2))],
        3: [nxt(("vr", 2)), [("av", 1, 0), ("av", 1, 1)] + nxt(("part0", 3)), [("av", 1, 2), ("av", 1, 3)],
            nxt(("partsT", 2)), [("avT", 1)] + nxt(("part1", 3)), nxt(("vr", 3)), [("scat", 2)] + nxt(("partsT", 3)), []],
    }
    for g in range(1, NG):
        f = fill[g]
        s += f[0] + [("negT", g - 1), ("s1", g, 0)] + f[1] + [("s1", g, 1)] + f[2]
        for u in range(2, NU1):
            s += [("s1", g, u), ("s2", g - 1, u - 2)] + f[u + 1]
        s += [("negsplit", g), ("s2", g - 1, 4)] + f[7]
    s += nxt(("route",)) + [("negT", 3)] + [("av", 2, k) for k in range(NT)] + [("scat", 3)] + nxt(("stack", 0)) + \
        [("s2", 3, 0), ("s2", 3, 1), ("avT", 2), ("s2", 3, 2), ("s2", 3, 3), ("s2", 3, 4)]
    s += nxt(("exps",), ("rank",)) + [("down", 0)] + nxt(("stack", 1), ("rankA",), ("rankB",)) + [("down", 1)] + \
        [("av", 3, k) for k in range(NT)] + [("down", 2), ("avT", 3), ("down", 3), ("aT", 0), ("aT", 1), ("oproj", 0),
                                             ("oproj", 1)]
    return s


FIRST_STEPS = [("lnA",), ("lnB",), ("lnC",)] + [("xT", t) for t in range(NT)] + \
    [("qk", 0), ("vr", 0), ("part0", 0), ("part1", 0), ("qk", 1), ("vr", 1), ("part0", 1), ("part1", 1), ("partsT", 0),
     ("qk", 2), ("vr", 2), ("part0", 2), ("part1", 2), ("partsT", 1), ("qk", 3), ("vr", 3), ("part0", 3), ("part1", 3),
     ("partsT", 2), ("partsT", 3), ("stack", 0), ("stack", 1), ("route",), ("exps",), ("rank",), ("rankA",), ("rankB",)]

BANKS_OF = {"gate": ("hidden",), "up": ("hidden",), "negT": ("neg_t",), "avT": ("attn",), "xT": ("xn_t",), "qk": ("rope",),
            "vr": ("logits",), "partsT": ("q_t", "k_t"), "aT": ("attn_t",), "rank": ("ranked",)}
NEXT_STEPS = ("lnA", "lnB", "lnC", "xT", "qk", "vr", "part0", "part1", "partsT", "stack", "route", "exps", "rank", "rankA",
              "rankB")
TIMES = {"hidden": NM, "neg_t": NG, "attn": NG, "xn_t": NT, "rope": NT, "logits": NT, "q_t": NT, "k_t": NT,
         "attn_t": 2, "ranked": 1, "row_max": NG * NU1, "probs": NG * NU2, "sums": 2}


def plans(steps, last_banks, last_units):
    banks, units, last_banks, last_units = {}, {}, list(last_banks), list(last_units)
    nb = nu = 0
    for step in steps:
        idx, ahead = step[1] if len(step) > 1 else 0, int(step[0] in NEXT_STEPS)
        for k, name in enumerate(BANKS_OF.get(step[0], ())):
            banks[step, k] = (nb, last_banks[nb])
            last_banks[nb] = (name, idx, ahead)
            nb = (nb + 1) % len(last_banks)
        if step[0] in ("s1", "s2") or step == ("down", 0):
            units[step] = (nu, last_units[nu])
            last_units[nu] = {"s1": ("row_max", idx * NU1 + step[-1], 0), "s2": ("probs", idx * NU2 + step[-1], 0),
                              "down": ("sums", 1, 0)}[step[0]]
            nu = (nu + 1) % len(last_units)
    return banks, units, last_banks, last_units


def one_later(last):
    return [u and (u[0], u[1], u[2] - 1) for u in last]


def block_kernel(nc, x, wqkvr, wo, wgu_s, wd_s, bias, wgu_e, wd_e, rope_cos, rope_sin, out):
    values = nc.dram_tensor("values", (E * REGION, D), F32, kind="Internal").ap()
    sum_dram = nc.dram_tensor("sum_dram", (TOKENS, D), F32, kind="Internal").ap()
    table = nc.dram_tensor("table", (TABLE, 2), I32, kind="Internal").ap()
    y_dram = nc.dram_tensor("y_dram", (TOKENS * TOPK, D), F32, kind="Internal").ap()

    ctx = ExitStack()
    with ctx:
        def sb(name, shape, dt=F32, where=None):
            return (where or ctx).enter_context(nc.sbuf_tensor(name, shape, dt))

        def sem(name):
            return ctx.enter_context(nc.semaphore(name))

        ident = sb("ident", [P, P])
        identb = sb("identb", [P, P], BF16)
        iota_e = sb("iota_e", [P, E])
        counts = sb("counts", [P, E])
        ps_g = [ctx.enter_context(nc.psum_tensor(f"ps_g{i}", [P, 512], F32)) for i in range(3)]
        ps_u = [ctx.enter_context(nc.psum_tensor(f"ps_u{i}", [P, 2, 512], F32)) for i in range(2)]
        ps_av = ctx.enter_context(nc.psum_tensor("ps_av", [P, 512], F32))

        phase_a(nc, sb, sem, ident, identb, iota_e, counts, ps_g, ps_u, ps_av, x, wqkvr, wo, wgu_s, wd_s, bias,
                rope_cos, rope_sin, values, sum_dram, table)
        phase_bcd(nc, sb, sem, ident, iota_e, counts, ps_g, ps_u, ps_av, wgu_e, wd_e, values, sum_dram, table,
                  y_dram, out)


def phase_a(nc, sb_, sem, ident, identb, iota_e, counts, ps_g, ps_u, ps_av, x, wqkvr, wo, wgu_s, wd_s, bias,
            rope_cos, rope_sin, values, sum_dram, table):
    stack = ExitStack()
    with stack:
        def sb(name, shape, dt=F32):
            return sb_(name, shape, dt, stack)

        w_qkvr = sb("w_qkvr", [P, KC, 3 * D + E])
        w_o = sb("w_o", [P, KC, D])
        w_gu = sb("w_gu", [P, KC, 2 * HS])
        w_d = sb("w_d", [P, NM, D])
        bias_bc = sb("bias_bc", [P, E])
        cos = sb("cos", [P, NT, P])
        sin = sb("sin", [P, NT, P])
        mask_qk = sb("mask_qk", [P, P], BF16)
        mask_kq = sb("mask_kq", [P, P], BF16)
        before = sb("before", [P, P], BF16)
        ones = sb("ones", [P, P], BF16)
        tri_f = sb("tri_f", [P, P])

        xin = sb("xin", [P, NT, D])
        stats = sb("stats", [P, NT, 6])
        mv = sb("mv", [P, NT, 2])
        ve = sb("ve", [P, NT])
        rs = sb("rs", [P, NT])
        rs_t = sb("rs_t", [P, NT])
        xn = sb("xn", [P, NT, D])
        xn_t = sb("xn_t", [P, KC, SEQ])
        rp1 = sb("rp1", [P, 2, 2 * D])
        rp2 = sb("rp2", [P, 2, 2 * D])
        rqk = sb("rqk", [P, 2 * D])
        rres = sb("rres", [P, 2 * D])
        parts = sb("parts", [P, 2, NPART, 2 * D], BF16)
        q_t = sb("q_t", [P, NPART, KC, SEQ], BF16)
        k_t = sb("k_t", [P, NPART, KC, SEQ], BF16)
        v_new = sb("v_new", [P, NT, D])
        logits = sb("logits", [P, NT, E])

        q_st = sb("q_st", [P, NH, SEQ], BF16)
        k_st = sb("k_st", [P, NH, SEQ], BF16)
        v_pad = sb("v_pad", [P, NT, NH, 2 * DH])
        neg = sb("neg", [P, 2, NT, GH])
        neg_r = sb("neg_r", [P, NT, GH])
        neg_p = sb("neg_p", [P, 2, NT, NPART, GH], BF16)
        neg_t = sb("neg_t", [NPART * GH, 2, SEQ], BF16)
        probs = [sb(f"probs{i}", [P, NU2, 1024]) for i in range(2)]
        av = sb("av", [P, SEQ])
        rden = sb("rden", [P, NT, GH])
        attn = sb("attn", [P, NT, D])
        attn_t = sb("attn_t", [P, KC, SEQ])
        th = sb("th", [P, 2, SEQ])
        gth = sb("gth", [P, SEQ])
        hid = sb("hid", [P, NM, SEQ])
        xres = sb("xres", [P, NT, D])
        osum = sb("osum", [P, NT, D])
        lg = sb("lg", [P, NT, E])
        top_v = sb("top_v", [P, NT, 8])
        top_i = sb("top_i", [P, NT, 8], U32)
        top_f = sb("top_f", [P, NT, TOPK])
        onehot = sb("onehot", [P, NT, TOPK, E])
        chosen = sb("chosen", [P, NT, E], BF16)
        ex = sb("ex", [P, NT, E + TOPK])
        exo = sb("exo", [P, NT, E + TOPK])
        zs = sb("zs", [P, 4, NT])
        pr4 = sb("pr4", [P, NT, TOPK])
        base = sb("base", [P, E])
        region = sb("region", [P, E])
        pos = sb("pos", [P, NT, E])
        slotf = sb("slotf", [P, NT * TOPK])
        slot = sb("slot", [P, NT * TOPK], I32)
        dest_f = sb("dest_f", [P, NT * TOPK])
        entry = sb("entry", [P, NT * TOPK, 2], I32)
        xs = sb("xs", [P, NT, D])

        S = {n: sem(n) for n in TIMES}
        consts, weights, inited, table_set = sem("consts"), sem("weights"), sem("inited"), sem("table_set")
        xs_ready, slots = sem("xs_ready"), sem("slots")
        x_in, x_res, sum_out = sem("x_in"), sem("x_res"), sem("sum_out")
        stacked = [sem("stacked0"), sem("stacked1")]
        neg_rows = [sem("neg_rows0"), sem("neg_rows1")]
        scattered = sem("scattered")
        xn_ready, parts_ready, v_placed = sem("xn_ready"), sem("parts_ready"), sem("v_placed")
        v_ready = sem("v_ready")
        summed, part0_ready, part1_ready = sem("summed"), sem("part0_ready"), sem("part1_ready")
        passed_pool, passed_dve, passed_sp = sem("passed_pool"), sem("passed_dve"), sem("passed_sp")
        neg_parts, tanh_done, av_out, exps, chosen_ready = \
            sem("neg_parts"), sem("tanh_done"), sem("av_out"), sem("exps"), sem("chosen_ready")
        pe = {n: sem("pe_" + n) for n in ("xT", "qk", "vr", "qT", "kT", "gate", "up", "s1", "negT", "s2", "av", "avT",
                                          "aT", "sum", "rank")}
        dve_front, dve_chain, pool_chain, ex_ready, rope1 = \
            sem("dve_front"), sem("dve_chain"), sem("pool_chain"), sem("ex_ready"), sem("rope1")

        STACK_DMAS = NSTACK * 2

        SCATTERS = 2 * 16 * NT * TOPK

        def done(name, b, k):
            return b * TIMES[name] + k + 1

        block = stack.enter_context(nc.Block())
        body = attention_steps(True)
        tail = attention_steps(False)

        def run(eng, handlers):
            def steps(order, b, nb, first, last_banks, last_units):
                bp, up, lb, lu = plans(order, last_banks, last_units)
                for step in order:
                    if step[0] in handlers:
                        handlers[step[0]](nb if step[0] in NEXT_STEPS else b, step, (bp, up, b, first))
                return lb, lu
            lb, lu = steps(FIRST_STEPS, 0, 0, True, [None] * 3, [None] * 2)
            lb, lu = steps(body, 0, 1, False, one_later(lb), lu)
            lb, lu = one_later(lb), one_later(lu)
            with eng.Fori(1, BATCH - 1) as b:
                assert (lb, lu) == tuple(map(one_later, steps(body, b, b + 1, False, lb, lu)))
            steps(tail, BATCH - 1, None, False, lb, lu)

        class Chain:

            def __init__(self, eng, s, per, passed):
                self.eng, self.s, self.per, self.passed, self.k = eng, s, per, passed, 0

            def link(self, b, ins, apart=False):
                ins.then_inc(self.s, 1)
                self.k = self.k % self.per + 1
                self.eng.wait_ge(self.s, b * self.per + self.k)
                if apart:
                    hold(self.eng, self.passed)

            def closed(self):
                assert self.k == self.per, (self.k, self.per)

        @block.sync
        def _(sp):
            sp.dma_start(w_qkvr[:, :, :], wqkvr.rearrange("(c p) n -> p c n", p=P)).then_inc(weights, 16)
            sp.dma_start(cos[:, :, :], rope_cos.rearrange("(t p) c -> p t c", p=P)).then_inc(weights, 16)
            sp.dma_start(sin[:, :, :], rope_sin.rearrange("(t p) c -> p t c", p=P)).then_inc(weights, 16)
            sp.dma_start(bias_bc[:, :], bias.partition_broadcast(P)).then_inc(weights, 16)
            sp.dma_start(w_gu[:, :, :], wgu_s.rearrange("(c p) n -> p c n", p=P)).then_inc(weights, 16)
            sp.dma_start(w_d[:, :, :], wd_s.rearrange("(c p) n -> p c n", p=P)).then_inc(weights, 16)
            sp.dma_start(w_o[:, :, :], wo.rearrange("(c p) n -> p c n", p=P)).then_inc(weights, 16)

            def tokens(dram, b):
                return dram[bass.ds(b * SEQ, SEQ), :].rearrange("(t p) d -> p t d", p=P)

            def stack_rows(nb, step, env):
                sp.wait_ge(S["q_t"], done("q_t", nb, NT - 1))
                sp.wait_ge(S["k_t"], done("k_t", nb, NT - 1))
                c = step[1]
                if not env[3]:
                    sp.wait_ge(pe["s2"], nb * NG * NU2 - (KC - 1 - c) * 2 * NU2)
                for dst, src, which in ((q_st, q_t, Q_PART), (k_st, k_t, K_PART)):
                    for s in range(NSTACK):
                        sp.dma_start(dst[DH * s:DH * (s + 1), 8 * c:8 * c + 8, :], src[:, which[s], c, :]
                                     ).then_inc(stacked[c], 16)

            def x_load(nb):
                sp.wait_ge(xn_ready, NT * nb)
                sp.dma_start(xin[:, :, :], tokens(x, nb)).then_inc(x_in, 16)

            def gate(b, step, env):
                if step[1] == 0:
                    sp.wait_ge(S["sums"], 2 * b)
                    sp.dma_start(xres[:, :, :], tokens(x, b)).then_inc(x_res, 16)
                    if env[0].get((("xT", 0), 0)):
                        x_load(b + 1)

            def neg_store(b, step, env):
                g = step[1]
                sp.wait_ge(S["neg_t"], done("neg_t", b, g))
                sp.dma_start(q_st[KROWS:MROWS, GH * g:GH * g + GH, :],
                             neg_t[:, g % 2, :]).then_inc(neg_rows[g % 2], 16)

            def store(b, step, env):
                if step[1] == 1:
                    sp.wait_ge(S["sums"], 2 * b + 2)
                    sp.dma_start(tokens(sum_dram, b), osum[:, :, :]).then_inc(sum_out, 16)

            sp.dma_start(xin[:, :, :], tokens(x, 0)).then_inc(x_in, 16)
            sp.wait_ge(inited, 1)
            sp.dma_start(table.rearrange("(p r) c -> p (r c)", p=P),
                         probs[0][:, :, :].rearrange("p u n -> p (u n)")[:, 0:2 * TABLE // P].bitcast(I32)
                         ).then_inc(table_set, 16)
            run(sp, {"stack": stack_rows, "gate": gate, "negT": neg_store, "oproj": store})
            sp.wait_ge(sum_out, 16 * BATCH)

        @block.gpsimd
        def _(pool):
            blank = probs[0][:, :, :].rearrange("p u n -> p (u n)")[:, 0:2 * TABLE // P].bitcast(I32)
            chain = Chain(pool, pool_chain, NT, passed_pool)
            made = [0]

            def const(ins):
                made[0] += 1
                ins.then_inc(consts, 1)
                pool.wait_ge(consts, made[0])

            def zeros_kept(value, base, mult, step):
                const(pool.memset(tri_f[:], 0.0))
                const(pool.affine_select(out=tri_f[:], in_=tri_f[:], compare_op=ALU.is_ge, fill=value, base=base,
                                         pattern=[[step, P]], channel_multiplier=mult))

            const(pool.memset(blank, 0))
            pool.memset(blank.rearrange("p (r c) -> p r c", c=2)[:, :, 0:1], SKIP).then_inc(inited, 1)
            pool.wait_ge(inited, 1)
            const(pool.memset(ident[:], 0.0))
            const(pool.affine_select(out=ident[:], in_=ident[:], compare_op=ALU.not_equal, fill=1.0, base=0,
                                     pattern=[[-1, P]], channel_multiplier=1))
            const(pool.tensor_copy(identb[:], ident[:]))
            const(pool.memset(v_pad[:], 0.0))
            const(pool.memset(v_pad[:, :, :, DH:DH + 1], 1.0))
            const(pool.memset(k_st[KROWS:MROWS, :, :], 1.0))
            const(pool.memset(ones[:], 1.0))
            const(pool.memset(counts[:], 0.0))
            const(pool.memset(entry[:], 0))
            const(pool.iota(iota_e[:], pattern=[[1, E]], base=0, channel_multiplier=0,
                            allow_small_or_imprecise_dtypes=True))
            const(pool.iota(dest_f[:], pattern=[[P * TOPK, NT], [1, TOPK]], base=0, channel_multiplier=TOPK,
                            allow_small_or_imprecise_dtypes=True))
            zeros_kept(NEG, 0, 1, -1)
            const(pool.tensor_copy(mask_qk[:], tri_f[:]))
            zeros_kept(NEG, 0, -1, 1)
            const(pool.tensor_copy(mask_kq[:], tri_f[:]))
            zeros_kept(1.0, 0, 1, -1)
            const(pool.tensor_copy(before[:], tri_f[:]))
            assert made[0] == N_CONSTS

            def qkv(nb, step, env):
                t = step[1]
                pool.wait_ge(S["rope"], done("rope", nb, t))
                if not (env[3] and t < 1):
                    pool.wait_ge(parts_ready, NT * nb + t)
                hold(pool, passed_pool)
                pool.tensor_tensor(rqk[:], rp1[:, t % 2, :], rp2[:, t % 2, :], ALU.add).then_inc(summed, 1)
                pool.wait_ge(part0_ready, NT * nb + t + 1)
                chain.link(nb, pool.tensor_tensor(rres[:], rqk[:], parts[:, t % 2, 0, :], ALU.subtract))
                pool.wait_ge(part1_ready, NT * nb + t + 1)
                pool.tensor_tensor(parts[:, t % 2, 2, :], rres[:], parts[:, t % 2, 1, :],
                                   ALU.subtract).then_inc(parts_ready, 1)
                if t == NT - 1:
                    chain.closed()

            def scatter(b, step, env):
                t = step[1]
                pool.wait_ge(xs_ready, NT * b + NT)
                pool.wait_ge(slots, b + 1)
                hold(pool, passed_pool)
                for k in range(TOPK * t, TOPK * (t + 1)):
                    pool.indirect_dma_start(table[:, :], bass.IndirectOffsetOnAxis(ap=slot[:, k:k + 1], axis=0),
                                            entry[:, k, :], None).then_inc(scattered, 16)
                    pool.indirect_dma_start(values[:, :], bass.IndirectOffsetOnAxis(ap=slot[:, k:k + 1], axis=0),
                                            xs[:, k // TOPK, :], None).then_inc(scattered, 16)

            pool.wait_ge(table_set, 16)
            run(pool, {"qk": qkv, "scat": scatter})
            pool.wait_ge(scattered, SCATTERS * BATCH)

        @block.scalar
        def _(act):
            def xT(nb, step, env):
                t, bank = step[1], env[0][step, 0][0]
                act.wait_ge(pe["xT"], NT * nb + t + 1)
                if t == 0 and not env[3]:
                    act.wait_ge(pe["up"], NM * nb)
                nc.scalar.activation(xn_t[:, :, t * P:(t + 1) * P],
                                     ps_g[bank][:, 0:D].rearrange("p (c n) -> p c n", c=KC), ACT.Copy
                                     ).then_inc(S["xn_t"], 1)

            def qkv(nb, step, env):
                t, bank = step[1], env[0][step, 0][0]
                act.wait_ge(pe["vr"], NT * nb + t + 1)
                if t == 0:
                    act.wait_ge(v_placed, nb)
                    if not env[3]:
                        act.wait_ge(chosen_ready, nb)
                nc.scalar.activation(v_new[:, t, :], ps_g[bank][:, 0:D], ACT.Copy).then_inc(v_ready, 1)
                nc.scalar.activation(logits[:, t, :], ps_g[bank][:, D:D + E], ACT.Copy).then_inc(S["logits"], 1)

            def part0(nb, step, env):
                t = step[1]
                act.wait_ge(summed, NT * nb + t + 1)
                if not (env[3] and t < 2):
                    act.wait_ge(pe["kT"], NT * nb + t - 1)
                nc.scalar.activation(parts[:, t % 2, 0, :], rqk[:], ACT.Copy).then_inc(part0_ready, 1)

            def part1(nb, step, env):
                t = step[1]
                act.wait_ge(pool_chain, NT * nb + t + 1)
                nc.scalar.activation(parts[:, t % 2, 1, :], rres[:], ACT.Copy).then_inc(part1_ready, 1)

            def place_v(b, step, env):
                act.wait_ge(v_ready, NT * (b + 1))
                act.wait_ge(pe["av"], NG * b)
                nc.scalar.activation(v_pad[:, :, :, 0:DH], v_new[:].rearrange("p t (h r) -> p t h r", r=DH), ACT.Copy
                                     ).then_inc(v_placed, 1)

            def partsT(nb, step, env):
                t = step[1]
                for k, (dst, p_, n) in enumerate(((q_t, "qT", "q_t"), (k_t, "kT", "k_t"))):
                    bank = env[0][step, k][0]
                    act.wait_ge(pe[p_], NT * nb + t + 1)
                    if t == 0 and k == 0:
                        for c in range(KC):
                            act.wait_ge(stacked[c], 16 * STACK_DMAS * nb)
                    nc.scalar.activation(
                        dst[:, :, :, t * P:(t + 1) * P].rearrange("p a c n -> p (a c) n"),
                        ps_g[bank][:, :].bitcast(BF16)[:, 0:NPART * D].rearrange("p (a n) -> p a n", n=P), ACT.Copy
                    ).then_inc(S[n], 1)

            def gate(b, step, env):
                m = step[1]
                act.wait_ge(pe["gate"], NM * b + m + 1)
                if m >= 2:
                    act.wait_ge(S["hidden"], done("hidden", b, m - 2))
                else:
                    act.wait_ge(S["hidden"], NM * b)
                nc.scalar.activation(th[:, m % 2, :], ps_g[env[0][step, 0][0]][:, :], ACT.Tanh, scale=0.5
                                     ).then_inc(tanh_done, 1)

            def copy(b, step, env):
                act.wait_ge(xn_ready, NT * (b + 1))
                act.wait_ge(scattered, SCATTERS * b)
                for t in range(NT):
                    nc.scalar.activation(xs[:, t, :], xn[:, t, :], ACT.Copy).then_inc(xs_ready, 1)

            def negT(b, step, env):
                g, bank = step[1], env[0][step, 0][0]
                act.wait_ge(pe["negT"], NG * b + g + 1)
                if g >= 2:
                    act.wait_ge(neg_rows[g % 2], 16 * (2 * b + g // 2))
                else:
                    act.wait_ge(neg_rows[g % 2], 16 * 2 * b)
                nc.scalar.activation(neg_t[:, g % 2, :], ps_g[bank][:, :].bitcast(BF16)[0:NPART * GH, 0:SEQ],
                                     ACT.Copy).then_inc(S["neg_t"], 1)

            def s2(b, step, env):
                _, g, u = step
                act.wait_ge(pe["s2"], NG * NU2 * b + NU2 * g + u + 1)
                if u == 0:
                    act.wait_ge(pe["av"], NG * b + (g - 1 if g >= 2 else 0))
                nc.scalar.activation(probs[g % 2][:, u, :], ps_u[env[1][step][0]][:, :, :].rearrange("p a n -> p (a n)"),
                                     ACT.Exp, scale=SCALE).then_inc(S["probs"], 1)

            def out_av(b, step, env):
                g = step[1]
                if step[2] < NT - 1:
                    return
                act.wait_ge(pe["av"], NG * b + g + 1)
                act.wait_ge(pe["avT"], NG * b + g)
                nc.scalar.activation(av[:, :], ps_av[:, :], ACT.Copy).then_inc(av_out, 1)

            def aT(b, step, env):
                p_, bank = step[1], env[0][step, 0][0]
                act.wait_ge(pe["aT"], 2 * b + p_ + 1)
                act.wait_ge(pe["sum"], 2 * b)
                nc.scalar.activation(
                    attn_t[:, :, 2 * p_ * P:2 * (p_ + 1) * P].rearrange("p c (t n) -> p t c n", t=2),
                    ps_g[bank][:, :].rearrange("p (t c n) -> p t c n", t=2, c=KC), ACT.Copy).then_inc(S["attn_t"], 1)

            def exponentials(b, step, env):
                act.wait_ge(ex_ready, b + 1)
                nc.scalar.activation(exo[:, :, :], ex[:, :, :], ACT.Exp).then_inc(exps, 1)

            act.wait_ge(table_set, 16)
            run(act, {"xT": xT, "vr": qkv, "partsT": partsT, "gate": gate, "copy": copy, "part0": part0, "part1": part1,
                      "placeV": place_v, "negT": negT, "s2": s2,
                      "av": out_av, "aT": aT, "exps": exponentials})

        @block.vector
        def _(dve):
            front = Chain(dve, dve_front, 2 + 3 + 3 * 3 + 6 + 7, passed_dve)
            back = Chain(dve, dve_chain, NM + 3 * NG + NG + 4, passed_dve)

            def ln_a(nb, step, env):
                dve.wait_ge(x_in, 16 * (nb + 1))
                dve.wait_ge(xn_ready, NT * nb)
                for t in range(NT):
                    ins = nc.vector.bn_stats(stats[:, t, :], xin[:, t, :])
                front.link(nb, ins, apart=True)
                for t in range(NT):
                    ins = nc.vector.bn_aggr(mv[:, t, :], stats[:, t, :])
                front.link(nb, ins)
                front.link(nb, nc.vector.tensor_scalar(ve[:], mv[:, :, 1], EPS, None, ALU.add))

            def ln_b(nb, step, env):
                front.link(nb, nc.vector.tensor_scalar(rs_t[:].bitcast(I32), ve[:].bitcast(I32), 1, None,
                                                       ALU.arith_shift_right))
                front.link(nb, nc.vector.tensor_scalar(rs[:].bitcast(I32), rs_t[:].bitcast(I32), -1.0, MAGIC,
                                                       ALU.mult, ALU.add))
                for _ in range(3):
                    front.link(nb, nc.vector.scalar_tensor_tensor(out=rs_t[:], in0=rs[:], scalar=-0.5, in1=rs[:],
                                                                  op0=ALU.mult, op1=ALU.mult))
                    front.link(nb, nc.vector.tensor_tensor(rs_t[:], rs_t[:], ve[:], ALU.mult))
                    front.link(nb, nc.vector.scalar_tensor_tensor(out=rs[:], in0=rs_t[:], scalar=1.5, in1=rs[:],
                                                                  op0=ALU.add, op1=ALU.mult))

            def ln_c(nb, step, env):
                dve.wait_ge(xs_ready, NT * nb)
                dve.wait_ge(pe["xT"], NT * nb)
                for t in range(NT):
                    nc.vector.tensor_scalar(xn[:, t, :], xin[:, t, :], mv[:, t, 0:1], rs[:, t:t + 1], ALU.subtract,
                                            ALU.mult).then_inc(xn_ready, 1)

            def qkv(nb, step, env):
                t, bank = step[1], env[0][step, 0][0]
                dve.wait_ge(pe["qk"], NT * nb + t + 1)
                if not (env[3] and t < 2):
                    dve.wait_ge(parts_ready, NT * nb + t - 1)
                def halves(a):
                    return a.rearrange("p (g s c) -> p g s c", g=2 * KC, s=2)
                nc.vector.tensor_tensor(rp1[:, t % 2, :].rearrange("p (g c) -> p g c", c=P),
                                        ps_g[bank][:, :].rearrange("p (g c) -> p g c", c=P),
                                        cos[:, t:t + 1, :].broadcast_to([P, 2 * KC, P]), ALU.mult).then_inc(rope1, 1)
                nc.vector.tensor_tensor(halves(rp2[:, t % 2, :]), halves(ps_g[bank][:, :])[:, :, ::-1, :],
                                        sin[:, t:t + 1, :].rearrange("p o (s c) -> p o s c", s=2
                                                                     ).broadcast_to([P, 2 * KC, 2, P // 2]), ALU.mult
                                        ).then_inc(S["rope"], 1)

            def ffn(b, step, env):
                m = step[1]
                (g_bank, _), (u_bank, _) = env[0][("gate", m), 0], env[0][step, 0]
                dve.wait_ge(tanh_done, NM * b + m + 1)
                dve.wait_ge(S["hidden"], NM * b + m)
                back.link(b, nc.vector.scalar_tensor_tensor(out=gth[:], in0=th[:, m % 2, :], scalar=1.0,
                                                            in1=ps_g[g_bank][:, :], op0=ALU.add,
                                                            op1=ALU.mult))
                dve.wait_ge(pe["up"], NM * b + m + 1)
                dve.wait_ge(pe["sum"], 2 * b)
                nc.vector.scalar_tensor_tensor(out=hid[:, m, :], in0=gth[:], scalar=0.5,
                                               in1=ps_g[u_bank][:, :], op0=ALU.mult, op1=ALU.mult
                                               ).then_inc(S["hidden"], 1)

            def s1(b, step, env):
                _, g, u = step
                i, h0, nh, per_bank = MAX_UNITS[u]
                ps = ps_u[env[1][step][0]]
                n = (i + 1) * P
                if u == 0:
                    dve.wait_ge(neg_parts, NG * b + max(0, g - 1))
                dve.wait_ge(pe["s1"], NG * NU1 * b + NU1 * g + u + 1)
                if per_bank > 1:
                    src = ps[:, 0:nh // per_bank, :].rearrange("p a (h n) -> p (a h) n", n=n)
                else:
                    src = ps[:, :, 0:n]
                nc.vector.tensor_reduce(neg[:, g % 2, i, h0:h0 + nh], src, AX.X, ALU.max, negate=True
                                        ).then_inc(S["row_max"], 1)

            def negsplit(b, step, env):
                g = step[1]
                dve.wait_ge(S["row_max"], done("row_max", b, NU1 * g + NU1 - 1))
                dve.wait_ge(pe["negT"], NG * b + max(0, g - 1))
                dve.wait_ge(neg_parts, NG * b + g)
                n_, np_ = neg[:, g % 2, :, :], neg_p[:, g % 2, :, :, :]
                back.link(b, nc.vector.tensor_copy(np_[:, :, 0, :], n_))
                back.link(b, nc.vector.tensor_tensor(neg_r[:], n_, np_[:, :, 0, :], ALU.subtract))
                back.link(b, nc.vector.tensor_copy(np_[:, :, 1, :], neg_r[:]))
                nc.vector.tensor_tensor(np_[:, :, 2, :], neg_r[:], np_[:, :, 1, :], ALU.subtract
                                        ).then_inc(neg_parts, 1)

            def avT(b, step, env):
                g, bank = step[1], env[0][step, 0][0]
                ps = ps_g[bank][:, :].rearrange("p (t h c) -> p t h c", t=NT, c=2 * DH)
                dve.wait_ge(pe["avT"], NG * b + g + 1)
                dve.wait_ge(pe["aT"], 2 * b)
                dve.wait_ge(S["attn"], NG * b + g)
                back.link(b, nc.vector.reciprocal(rden[:], ps[:, :, :, DH]))
                nc.vector.tensor_tensor(
                    attn[:, :, g * GH * DH:(g + 1) * GH * DH].rearrange("p t (h c) -> p t h c", c=DH),
                    ps[:, :, :, 0:DH], rden[:].rearrange("p t (h o) -> p t h o", o=1).broadcast_to([P, NT, GH, DH]),
                    ALU.mult).then_inc(S["attn"], 1)

            def oproj(b, step, env):
                p_, u = step[1], env[1][("down", 0)][0]
                dve.wait_ge(pe["sum"], 2 * b + p_ + 1)
                if p_ == 0:
                    dve.wait_ge(x_res, 16 * (b + 1))
                    dve.wait_ge(sum_out, 16 * b)
                nc.vector.tensor_tensor(osum[:, 2 * p_:2 * p_ + 2, :],
                                        ps_u[u][:, p_, :].rearrange("p (t n) -> p t n", t=2),
                                        xres[:, 2 * p_:2 * p_ + 2, :], ALU.add).then_inc(S["sums"], 1)

            def route(b, step, env):
                dve.wait_ge(S["logits"], done("logits", b, NT - 1))
                dve.wait_ge(exps, b)
                dve.wait_ge(slots, b)
                front.link(b, nc.vector.tensor_tensor(
                    lg[:], logits[:], bias_bc[:].rearrange("p (o e) -> p o e", o=1).broadcast_to([P, NT, E]), ALU.add), apart=True)
                for t in range(NT):
                    ins = nc.vector.max(top_v[:, t, :], lg[:, t, :])
                front.link(b, ins, apart=True)
                for t in range(NT):
                    ins = nc.vector.max_index(top_i[:, t, :], top_v[:, t, :], lg[:, t, :])
                front.link(b, ins)
                front.link(b, nc.vector.tensor_copy(top_f[:], top_i[:, :, 0:TOPK]))
                front.link(b, nc.vector.tensor_tensor(
                    onehot[:].rearrange("p t j e -> p (t j) e"),
                    iota_e[:].rearrange("p (o e) -> p o e", o=1).broadcast_to([P, NT * TOPK, E]),
                    top_f[:].rearrange("p t (j o) -> p (t j) o", o=1).broadcast_to([P, NT * TOPK, E]), ALU.is_equal))
                dve.wait_ge(pe["rank"], b)
                with nc.allow_low_precision(reason="zeros and ones are exact"):
                    nc.vector.tensor_reduce(chosen[:], onehot[:].rearrange("p t j e -> p t e j"), AX.X, ALU.add
                                            ).then_inc(chosen_ready, 1)
                top1 = top_v[:, :, 0:1]
                nc.vector.tensor_tensor(ex[:, :, 0:E], lg[:], top1.broadcast_to([P, NT, E]), ALU.subtract)
                nc.vector.tensor_tensor(ex[:, :, E:E + TOPK], top_v[:, :, 0:TOPK],
                                        top1.broadcast_to([P, NT, TOPK]), ALU.subtract).then_inc(ex_ready, 1)
                dve.wait_ge(S["ranked"], b)
                front.link(b, nc.vector.tensor_tensor(base[:], counts[:], region[:], ALU.add))

            def rank_a(b, step, env):
                dve.wait_ge(exps, b + 1)
                front.link(b, nc.vector.tensor_reduce(zs[:, 0, :], exo[:, :, 0:E], AX.X, ALU.add))
                front.link(b, nc.vector.reciprocal(zs[:, 1, :], zs[:, 0, :]))

                def bc(a):
                    return a.rearrange("p (t o) -> p t o", o=1).broadcast_to([P, NT, TOPK])
                front.link(b, nc.vector.tensor_tensor(pr4[:], exo[:, :, E:E + TOPK], bc(zs[:, 1, :]), ALU.mult))
                front.link(b, nc.vector.tensor_reduce(zs[:, 2, :], pr4[:], AX.X, ALU.add))
                front.link(b, nc.vector.tensor_scalar(zs[:, 2, :], zs[:, 2, :], 1e-12, None, ALU.max))
                front.link(b, nc.vector.reciprocal(zs[:, 3, :], zs[:, 2, :]))

            def rank_b(b, step, env):
                bank = env[0][("rank",), 0][0]
                dve.wait_ge(pe["rank"], b + 1)
                ps = ps_g[bank][:, 0:NT * E].rearrange("p (t e) -> p t e", t=NT)
                front.link(b, nc.vector.tensor_tensor(
                    pos[:], ps, base[:].rearrange("p (o e) -> p o e", o=1).broadcast_to([P, NT, E]), ALU.add))
                nc.vector.tensor_tensor(counts[:], counts[:], ps_g[bank][:, NT * E:(NT + 1) * E], ALU.add
                                        ).then_inc(S["ranked"], 1)
                front.closed()

            def rank_c(b, step, env):
                dve.wait_ge(S["ranked"], b + 1)
                dve.wait_ge(scattered, SCATTERS * b)
                nc.vector.tensor_tensor(
                    entry[:, :, 1].bitcast(F32).rearrange("p (t j) -> p t j", t=NT), pr4[:],
                    zs[:, 3, :].rearrange("p (t o) -> p t o", o=1).broadcast_to([P, NT, TOPK]), ALU.mult)
                for t in range(NT):
                    ins = nc.vector.tensor_tensor(onehot[:, t, :, :], onehot[:, t, :, :],
                                                  pos[:, t:t + 1, :].broadcast_to([P, TOPK, E]), ALU.mult)
                back.link(b, ins)
                back.link(b, nc.vector.tensor_reduce(slotf[:], onehot[:].rearrange("p t j e -> p (t j) e"), AX.X,
                                                     ALU.add))
                back.link(b, nc.vector.tensor_copy(entry[:, :, 0], dest_f[:]))
                back.link(b, nc.vector.tensor_scalar(dest_f[:], dest_f[:], float(SEQ * TOPK), None, ALU.add))
                nc.vector.tensor_copy(slot[:], slotf[:]).then_inc(slots, 1)

            dve.wait_ge(consts, N_CONSTS)
            dve.wait_ge(weights, 16 * 7)
            nc.vector.tensor_scalar(region[:], iota_e[:], float(REGION), None, ALU.mult)
            run(dve, {"lnA": ln_a, "lnB": ln_b, "lnC": ln_c, "qk": qkv, "up": ffn, "s1": s1, "negsplit": negsplit,
                      "avT": avT, "oproj": oproj, "route": route, "rankA": rank_a, "rankB": rank_b, "rankC": rank_c})
            back.closed()

        @block.tensor
        def _(pe_):
            def bank_of(step, k, env):
                bp, up, b, first = env
                bank, prev = bp[step, k]
                if prev is not None:
                    name, idx, ahead = prev
                    pe_.wait_ge(S[name], done(name, b + ahead - int(first), idx))
                return ps_g[bank]

            def unit_of(step, env):
                bp, up, b, first = env
                unit, prev = up[step]
                if prev is not None:
                    name, idx, ahead = prev
                    pe_.wait_ge(S[name], done(name, b + ahead - int(first), idx))
                return ps_u[unit]

            def xT(nb, step, env):
                t = step[1]
                ps = bank_of(step, 0, env)
                pe_.wait_ge(xn_ready, NT * nb + t + 1)
                for c in range(KC):
                    ins = nc.tensor.transpose(ps[:, c * P:(c + 1) * P], xn[:, t, c * P:(c + 1) * P], ident[:])
                ins.then_inc(pe["xT"], 1)

            def project(name, lo, n):
                def handler(nb, step, env):
                    t = step[1]
                    pe_.wait_ge(S["xn_t"], done("xn_t", nb, t))
                    ps = bank_of(step, 0, env)
                    for c in range(KC):
                        ins = nc.tensor.matmul(ps[:, 0:n], xn_t[:, c, t * P:(t + 1) * P], w_qkvr[:, c, lo:lo + n],
                                               start=(c == 0), stop=(c == KC - 1))
                    ins.then_inc(pe[name], 1)
                return handler

            def partsT(nb, step, env):
                t = step[1]
                pe_.wait_ge(parts_ready, NT * nb + t + 1)
                for k, name in enumerate(("qT", "kT")):
                    ps = bank_of(step, k, env)[:, :].bitcast(BF16)
                    for a in range(NPART * KC):
                        lo = D * k + P * (a % KC)
                        ins = nc.tensor.transpose(ps[:, a * P:(a + 1) * P], parts[:, t % 2, a // KC, lo:lo + P],
                                                  identb[:])
                    ins.then_inc(pe[name], 1)

            def hidden_part(name, k):
                def handler(b, step, env):
                    m = step[1]
                    ps = bank_of(step, 0, env)
                    for c in range(KC):
                        lo = HS * k + P * m
                        ins = nc.tensor.matmul(ps[:, :], w_gu[:, c, lo:lo + P], xn_t[:, c, :], start=(c == 0),
                                               stop=(c == KC - 1))
                    ins.then_inc(pe[name], 1)
                return handler

            def s1(b, step, env):
                _, g, u = step
                i, h0, nh, per_bank = MAX_UNITS[u]
                ps = unit_of(step, env)
                if u == 0 and g % 2 == 0:
                    pe_.wait_ge(stacked[g // 2], 16 * STACK_DMAS * (b + 1))
                n = (i + 1) * P
                for a in range(nh // per_bank):
                    for k in range(per_bank):
                        h = GH * g + h0 + a * per_bank + k
                        nc.tensor.matmul(ps[:, a, k * n:(k + 1) * n], q_st[0:KROWS, h, i * P:(i + 1) * P],
                                         k_st[0:KROWS, h, 0:n], start=(k == 0), stop=False, skip_group_check=True)
                    dst = ps[:, a, 0:per_bank * n].rearrange("p (k n) -> p k n", n=n)[:, :, n - P:n]
                    ins = nc.tensor.matmul(dst, identb[:],
                                           mask_qk[:].rearrange("p (o n) -> p o n", o=1).broadcast_to([P, per_bank, P]),
                                           start=False, stop=True, skip_group_check=True)
                ins.then_inc(pe["s1"], 1)

            def negT(b, step, env):
                g = step[1]
                ps = bank_of(step, 0, env)[:, :].bitcast(BF16)
                pe_.wait_ge(neg_parts, NG * b + g + 1)
                for t in range(NT):
                    ins = nc.tensor.transpose(ps[0:NPART * GH, t * P:(t + 1) * P],
                                              neg_p[:, g % 2, t, :, :].rearrange("p a h -> p (a h)"), identb[:])
                ins.then_inc(pe["negT"], 1)

            def s2(b, step, env):
                _, g, u = step
                ps = unit_of(step, env)
                if u == 0:
                    pe_.wait_ge(neg_rows[g % 2], 16 * (2 * b + g // 2 + 1))
                if u < GH:
                    pieces = [(0, 0, 0, GH * g + u), (1, 0, 1, GH * g + u), (1, 3 * P, 3, GH * g + u)]
                    masks = [(0, SEQ, 1), (1, 3 * P, 2)]
                else:
                    pieces = [(j // 2, (j % 2) * 2 * P, 2, GH * g + j) for j in range(GH)]
                    masks = [(0, 2 * P, 2), (1, 2 * P, 2)]
                for n_, (a, lo, kt, h) in enumerate(pieces):
                    n = SEQ - kt * P
                    nc.tensor.matmul(ps[:, a, lo:lo + n], k_st[0:MROWS, h, kt * P:(kt + 1) * P],
                                     q_st[0:MROWS, h, kt * P:SEQ], start=(lo == 0), stop=False, skip_group_check=True)
                for a, step_, cnt in masks:
                    if cnt == 1:
                        dst, rhs = ps[:, a, 0:P], mask_kq[:]
                    else:
                        if step_ == 3 * P:
                            dst = ps[:, a, :].rearrange("p (k n) -> p k n", n=P)[:, 0:NT:3, :]
                        else:
                            dst = ps[:, a, :].rearrange("p (k n) -> p k n", n=step_)[:, :, 0:P]
                        rhs = mask_kq[:].rearrange("p (o n) -> p o n", o=1).broadcast_to([P, cnt, P])
                    ins = nc.tensor.matmul(dst, identb[:], rhs, start=False, stop=True, skip_group_check=True)
                ins.then_inc(pe["s2"], 1)

            def av_(b, step, env):
                _, g, kt = step
                if kt == 0:
                    pe_.wait_ge(S["probs"], done("probs", b, NU2 * g + NU2 - 1))
                    pe_.wait_ge(av_out, NG * b + g)
                    if g == 0:
                        pe_.wait_ge(v_placed, b + 1)
                pr = probs[g % 2]
                n = SEQ - kt * P
                for j in range(GH):
                    if kt == 2:
                        rhs = pr[:, GH, j * 2 * P:j * 2 * P + n]
                    else:
                        lo = {0: 0, 1: SEQ, 3: SEQ + 3 * P}[kt]
                        rhs = pr[:, j, lo:lo + n]
                    ins = nc.tensor.matmul(ps_av[2 * DH * j:2 * DH * (j + 1), kt * P:SEQ], v_pad[:, kt, GH * g + j, :],
                                           rhs, start=(kt == 0), stop=(kt == NT - 1), skip_group_check=True)
                if kt == NT - 1:
                    ins.then_inc(pe["av"], 1)

            def avT(b, step, env):
                g = step[1]
                ps = bank_of(step, 0, env)
                pe_.wait_ge(av_out, NG * b + g + 1)
                for t in range(NT):
                    ins = nc.tensor.transpose(ps[:, t * P:(t + 1) * P], av[:, t * P:(t + 1) * P], ident[:])
                ins.then_inc(pe["avT"], 1)

            def aT(b, step, env):
                p_ = step[1]
                ps = bank_of(step, 0, env)
                pe_.wait_ge(S["attn"], done("attn", b, NG - 1))
                for t in range(2):
                    for c in range(KC):
                        lo = (t * KC + c) * P
                        ins = nc.tensor.transpose(ps[:, lo:lo + P], attn[:, 2 * p_ + t, c * P:(c + 1) * P], ident[:])
                ins.then_inc(pe["aT"], 1)

            def down(b, step, env):
                t = step[1]
                if t == 0:
                    unit_of(step, env)
                    pe_.wait_ge(S["hidden"], done("hidden", b, NM - 1))
                ps = ps_u[env[1][("down", 0)][0]]
                for m in range(NM):
                    nc.tensor.matmul(ps[:, t // 2, (t % 2) * D:(t % 2 + 1) * D], hid[:, m, t * P:(t + 1) * P],
                                     w_d[:, m, :], start=(t % 2 == 0 and m == 0), stop=False, skip_group_check=True)

            def oproj(b, step, env):
                p_ = step[1]
                ps = ps_u[env[1][("down", 0)][0]]
                pe_.wait_ge(S["attn_t"], done("attn_t", b, p_))
                for t in (2 * p_, 2 * p_ + 1):
                    for c in range(KC):
                        ins = nc.tensor.matmul(ps[:, p_, (t % 2) * D:(t % 2 + 1) * D], attn_t[:, c, t * P:(t + 1) * P],
                                               w_o[:, c, :], start=False, stop=(c == KC - 1), skip_group_check=True)
                ins.then_inc(pe["sum"], 1)

            def rank(b, step, env):
                ps = bank_of(step, 0, env)
                pe_.wait_ge(chosen_ready, b + 1)
                ch = chosen[:].rearrange("p t e -> p (t e)")
                nc.tensor.matmul(ps[:, 0:NT * E], before[:], ch, start=True, stop=False, skip_group_check=True)
                for k in range(1, NT):
                    nc.tensor.matmul(ps[:, k * E:NT * E], ones[:], ch[:, 0:(NT - k) * E], start=False, stop=False,
                                     skip_group_check=True)
                for k in range(NT):
                    ins = nc.tensor.matmul(ps[:, NT * E:(NT + 1) * E], ones[:], ch[:, k * E:(k + 1) * E], start=False,
                                           stop=(k == NT - 1), skip_group_check=True)
                ins.then_inc(pe["rank"], 1)

            pe_.wait_ge(consts, N_CONSTS)
            pe_.wait_ge(weights, 16 * 7)
            run(pe_, {"xT": xT, "qk": project("qk", 0, 2 * D), "vr": project("vr", 2 * D, D + E), "partsT": partsT,
                      "gate": hidden_part("gate", 0), "up": hidden_part("up", 1), "s1": s1, "negT": negT, "s2": s2, "av": av_,
                      "avT": avT, "aT": aT, "down": down, "oproj": oproj, "rank": rank})


def phase_bcd(nc, sb_, sem, ident, iota_e, counts, ps_g, ps_u, ps_av, wgu_e, wd_e, values, sum_dram, table, y_dram,
              out):
    stack = ExitStack()
    with stack:
        def sb(name, shape, dt=F32):
            return sb_(name, shape, dt, stack)

        w_gu = sb("we_gu", [P, E, KC, 2 * HE])
        w_d = sb("we_d", [P, E, D])
        nb_i = sb("nb_i", [P, E], I32)
        nb_f = sb("nb_f", [P, E])
        nb_c = sb("nb_c", [E, 2])
        tri = sb("tri", [E, E])
        one_c = sb("one_c", [E, 1])
        blk_i = sb("blk_i", [E, NBLOCK])
        past = sb("past", [E, NBLOCK])
        row_f = sb("row_f", [1, 2, NBLOCK])
        place = sb("place", [1, NBLOCK], I32)
        zeros = sb("zeros", [P, D])
        row_p = sb("row_p", [P, 1])
        fill_f = sb("fill_f", [P, 2, E])
        fill_row = sb("fill_row", [P, E], I32)
        expert = sb("expert", [1, NBLOCK], I32)

        NR = 16
        ent = [sb(f"ent{i}", [P, 2], I32) for i in range(NR)]
        xg = [sb(f"xg{i}", [P, D]) for i in range(NR)]
        x_t = [sb(f"x_t{i}", [P, D]) for i in range(2)]
        tnh = [sb(f"tnh{i}", [P, HE]) for i in range(2)]
        gt = [sb(f"gt{i}", [P, HE]) for i in range(2)]
        hw = [sb(f"hw{i}", [P, HE]) for i in range(2)]
        wh = [sb(f"wh{i}", [P, 1]) for i in range(2)]
        h_t = [sb(f"h_t{i}", [P, HE]) for i in range(2)]
        yb = [sb(f"yb{i}", [P, D]) for i in range(NR)]
        ps_x, ps_gu = [ps_g[0], ps_g[1]], [ps_g[2], ps_av]
        ps_h = [ps_u[0][:, i, :] for i in range(2)]
        ps_y = [ps_u[1][:, i, :] for i in range(2)]

        ws, plan, plan_pe, ready = sem("ws"), sem("plan"), sem("plan_pe"), sem("ready")
        c_pool, fill_ready = sem("c_pool"), sem("fill_ready")
        passed, passed_s = sem("passed"), sem("passed_s")
        filled = sem("filled")
        block_in = [sem(f"block_in{i}") for i in range(NR)]
        y_out = [sem(f"y_out{i}") for i in range(NR)]
        xt_ps, gu_ps, ht_ps, y_ps = sem("xt_ps"), sem("gu_ps"), sem("ht_ps"), sem("y_ps")
        xt_sb, tanh_sb, gate_sb, h_sb, ht_sb, y_sb = [sem(n) for n in
                                                      ("xt_sb", "tanh_sb", "gate_sb", "h_sb", "ht_sb", "y_sb")]
        block = stack.enter_context(nc.Block())
        BODY = 2 * NR
        LOOPS = (NBLOCK - 2 * NR) // BODY
        assert NBLOCK == 2 * NR + LOOPS * BODY

        def expert_loop(eng, stage):
            for n in range(NR):
                stage(n, n, True)
            with eng.Fori(0, LOOPS) as i:
                for k in range(BODY):
                    stage(i * BODY + NR + k, k % NR, False)
            for n in range(NBLOCK - NR, NBLOCK):
                stage(n, n % NR, False)

        table_v = table.rearrange("(n p) c -> n p c", p=P)
        values_v = values.rearrange("(n p) c -> n p c", p=P)

        @block.sync
        def _(sp):
            sp.wait_ge(filled, 16 * E)
            sp.wait_ge(ready, 1)

            def stage(n, k, first):
                if k % 4:
                    return
                _, places = nc.values_load_multi_w_load_instructions(
                    place[0:1, bass.ds(n, 4)], engines=(mybir.EngineType.SP,), min_val=0, max_val=TABLE // P - 1)
                v_places = [at % (E * REGION // P) for at in places]
                for q in range(4):
                    if not first:
                        sp.wait_ge(y_out[k + q], (n + q - (k + q)) * (16 // NR))
                        hold(sp, passed_s)
                    sp.dma_start(ent[k + q][:, :], table_v[bass.ds(places[q], 1), :, :]).then_inc(block_in[k + q], 16)
                    sp.dma_start(xg[k + q][:, :], values_v[bass.ds(v_places[q], 1), :, :]
                                 ).then_inc(block_in[k + q], 16)
            expert_loop(sp, stage)

        @block.scalar
        def _(act):
            for q in range(4):
                e0 = q * E // 4
                act.dma_start(w_gu[:, e0:e0 + E // 4, :, :].rearrange("p e c n -> p (e c) n"),
                              wgu_e[e0:e0 + E // 4, :, :].rearrange("e (c p) n -> p (e c) n", p=P)).then_inc(ws, 16)
                act.dma_start(w_d[:, e0:e0 + E // 4, :], wd_e[e0:e0 + E // 4, :, :].rearrange("e p n -> p e n")
                              ).then_inc(ws, 16)

            def tanh(n, k, first):
                s = k % 2
                act.wait_ge(gu_ps, n + 1)
                if not (first and k < 2):
                    act.wait_ge(gate_sb, n - 1)
                nc.scalar.activation(tnh[s][:], ps_gu[s][:, 0:HE], ACT.Tanh, scale=0.5).then_inc(tanh_sb, 1)

            def hidden(n, k, first):
                s = k % 2
                act.wait_ge(ht_ps, n + 1)
                if not (first and k < 2):
                    act.wait_ge(y_ps, n - 1)
                nc.scalar.activation(h_t[s][:], ps_h[s][:, 0:P], ACT.Copy).then_inc(ht_sb, 1)

            def result(n, k, first):
                s = k % 2
                act.wait_ge(y_ps, n + 1)
                if not first:
                    act.wait_ge(y_out[k], (n - k) * (16 // NR))
                nc.scalar.activation(yb[k][:], ps_y[s][:, 0:D], ACT.Copy).then_inc(y_sb, 1)

            def iteration(n, k, first):
                tanh(n, k, first)
                if not first or n >= 1:
                    hidden(n - 1, (k - 1) % NR, first)
                if not first or n >= 2:
                    result(n - 2, (k - 2) % NR, first)

            for n in range(NR):
                iteration(n, n, True)
            for n in range(NR, NR + 2):
                tanh(n, n - NR, False)
                hidden(n - 1, (n - 1) % NR, False)
                result(n - 2, n - 2, True)
            for n in range(NR + 2, 2 * NR):
                iteration(n, n % NR, False)
            with act.Fori(0, LOOPS) as i:
                for k in range(BODY):
                    iteration(i * BODY + 2 * NR + k, k % NR, False)
            hidden(NBLOCK - 1, NR - 1, False)
            result(NBLOCK - 2, NR - 2, False)
            result(NBLOCK - 1, NR - 1, False)

        @block.gpsimd
        def _(pool):
            pool.iota(blk_i[:], pattern=[[1, NBLOCK]], base=0, channel_multiplier=0,
                      allow_small_or_imprecise_dtypes=True).then_inc(c_pool, 1)
            pool.memset(one_c[:], 1.0).then_inc(c_pool, 1)
            pool.memset(tri[:], 0.0).then_inc(c_pool, 1)
            pool.wait_ge(c_pool, 3)
            pool.affine_select(out=tri[:], in_=tri[:], compare_op=ALU.is_ge, fill=1.0, base=-1,
                               pattern=[[-1, E]], channel_multiplier=1).then_inc(c_pool, 1)
            pool.wait_ge(c_pool, 4)
            pool.memset(zeros[:], 0.0).then_inc(c_pool, 1)
            pool.wait_ge(c_pool, 5)
            pool.iota(row_p[:], pattern=[[0, 1]], base=0, channel_multiplier=1,
                      allow_small_or_imprecise_dtypes=True).then_inc(c_pool, 1)
            pool.wait_ge(c_pool, 6)
            pool.wait_ge(fill_ready, 1)
            for e in range(E):
                pool.indirect_dma_start(values[:, :], bass.IndirectOffsetOnAxis(ap=fill_row[:, e:e + 1], axis=0),
                                        zeros[:, :], None, bounds_check=E * REGION - 1, oob_is_err=False
                                        ).then_inc(filled, 16)

            def scatter(n, k, first):
                pool.wait_ge(y_sb, n + 1)
                hold(pool, passed)
                pool.indirect_dma_start(y_dram[:, :], bass.IndirectOffsetOnAxis(ap=ent[k][:, 0:1], axis=0),
                                        yb[k][:, :], None, bounds_check=TOKENS * TOPK - 1, oob_is_err=False
                                        ).then_inc(y_out[k], 16)
            expert_loop(pool, scatter)
            for k in range(NR):
                pool.wait_ge(y_out[k], 16 * NBLOCK // NR)

        @block.tensor
        def _(pe):
            pe.wait_ge(plan, 1)
            nc.tensor.transpose(ps_g[0][0:E, 0:P], nb_f[:], ident[:]).then_inc(plan_pe, 1)
            pe.wait_ge(plan, 2)
            pe.wait_ge(c_pool, 4)
            nc.tensor.matmul(ps_g[1][0:E, 0:1], tri[:], nb_c[:, 0:1], start=True, stop=True).then_inc(plan_pe, 1)
            pe.wait_ge(plan, 4)
            nc.tensor.matmul(ps_g[0][0:1, 0:NBLOCK], one_c[:], past[:], start=True, stop=True)
            nc.tensor.matmul(ps_g[2][0:1, 0:NBLOCK], nb_c[:, 0:1], past[:], start=True, stop=True).then_inc(plan_pe, 1)
            pe.wait_ge(ready, 1)
            pe.wait_ge(ws, 16 * 8)

            def xT(n, k, first):
                s = k % 2
                pe.wait_ge(block_in[k], (n - k) * (32 // NR) + 32)
                if not (first and k < 2):
                    pe.wait_ge(xt_sb, n - 1)
                for c in range(KC):
                    ins = nc.tensor.transpose(ps_x[s][:, c * P:(c + 1) * P], xg[k][:, c * P:(c + 1) * P], ident[:])
                ins.then_inc(xt_ps, 1)

            def expert_of(n):
                return pe.value_load(expert[0:1, bass.ds(n, 1)], min_val=0, max_val=E - 1)

            def gu(n, k, first, e):
                s = k % 2
                pe.wait_ge(xt_sb, n + 1)
                if not (first and k < 2):
                    pe.wait_ge(h_sb, n - 1)
                for c in range(KC):
                    ins = nc.tensor.matmul(ps_gu[s][:, 0:2 * HE], x_t[s][:, c * P:(c + 1) * P],
                                           w_gu[:, bass.ds(e, 1), c, :], start=(c == 0), stop=(c == KC - 1))
                ins.then_inc(gu_ps, 1)

            def hT(n, k, first):
                s = k % 2
                pe.wait_ge(h_sb, n + 1)
                if not (first and k < 2):
                    pe.wait_ge(ht_sb, n - 1)
                nc.tensor.transpose(ps_h[s][:, 0:P], hw[s][:], ident[:]).then_inc(ht_ps, 1)

            def y(n, k, first, e):
                s = k % 2
                pe.wait_ge(ht_sb, n + 1)
                if not (first and k < 2):
                    pe.wait_ge(y_sb, n - 1)
                nc.tensor.matmul(ps_y[s][:, 0:D], h_t[s][:], w_d[:, bass.ds(e, 1), :], start=True, stop=True
                                 ).then_inc(y_ps, 1)

            def iterations(n0, count, first):
                e = {k: expert_of(n0 + k) for k in (range(1) if first else range(-2, 1))}
                for k in range(count):
                    n = n0 + k
                    if not (isinstance(n, int) and n + 1 == NBLOCK):
                        xT(n + 1, (k + 1) % NR, first and k + 1 < NR)
                    gu(n, k % NR, first, e[k])
                    if k + 1 < count:
                        e[k + 1] = expert_of(n + 1)
                    if not first or k >= 1:
                        hT(n - 1, (k - 1) % NR, first)
                    if not first or k >= 2:
                        y(n - 2, (k - 2) % NR, first, e[k - 2])

            xT(0, 0, True)
            iterations(0, NR, True)
            with pe.Fori(0, LOOPS) as i:
                iterations(i * BODY + NR, BODY, False)
            iterations(NBLOCK - NR, NR, False)
            e = [expert_of(NBLOCK - 2), expert_of(NBLOCK - 1)]
            hT(NBLOCK - 1, NR - 1, False)
            y(NBLOCK - 2, NR - 2, False, e[0])
            y(NBLOCK - 1, NR - 1, False, e[1])

        @block.vector
        def _(dve):
            dchain = sem("plan_dve")
            n_ = [0]

            def link(ins):
                n_[0] += 1
                ins.then_inc(dchain, 1)
                dve.wait_ge(dchain, n_[0])
            dve.wait_ge(c_pool, 6)
            link(nc.vector.tensor_scalar(fill_f[:, 0, :], counts[:], row_p[:, 0:1], None, ALU.add))
            link(nc.vector.tensor_scalar(fill_f[:, 1, :], fill_f[:, 0, :], float(REGION), float(SKIP), ALU.is_ge,
                                         ALU.mult))
            link(nc.vector.tensor_tensor(fill_f[:, 0, :], fill_f[:, 0, :], fill_f[:, 1, :], ALU.add))
            link(nc.vector.scalar_tensor_tensor(out=fill_f[:, 1, :], in0=iota_e[:], scalar=float(REGION),
                                                in1=fill_f[:, 0, :], op0=ALU.mult, op1=ALU.add))
            nc.vector.tensor_copy(fill_row[:], fill_f[:, 1, :]).then_inc(fill_ready, 1)
            link(nc.vector.tensor_scalar(nb_f[:], counts[:], float(P - 1), None, ALU.add))
            link(nc.vector.tensor_copy(nb_i[:], nb_f[:]))
            link(nc.vector.tensor_scalar(nb_i[:], nb_i[:], 7, None, ALU.arith_shift_right))
            nc.vector.tensor_copy(nb_f[:], nb_i[:]).then_inc(plan, 1)
            dve.wait_ge(plan_pe, 1)
            nc.vector.tensor_copy(nb_c[:, 0:1], ps_g[0][0:E, 0:1]).then_inc(plan, 1)
            dve.wait_ge(plan_pe, 2)
            nc.vector.tensor_copy(nb_c[:, 1:2], ps_g[1][0:E, 0:1]).then_inc(plan, 1)
            dve.wait_ge(plan, 3)
            dve.wait_ge(c_pool, 4)
            nc.vector.tensor_scalar(past[:], blk_i[:], nb_c[:, 1:2], None, ALU.is_ge).then_inc(plan, 1)
            dve.wait_ge(plan_pe, 3)
            link(nc.vector.tensor_tensor(row_f[:, 0, :], blk_i[0:1, :], ps_g[2][0:1, 0:NBLOCK], ALU.subtract))
            link(nc.vector.scalar_tensor_tensor(out=row_f[:, 1, :], in0=ps_g[0][0:1, 0:NBLOCK],
                                                scalar=float(REGION // P), in1=row_f[:, 0, :], op0=ALU.mult,
                                                op1=ALU.add))
            link(nc.vector.tensor_scalar(row_f[:, 1, :], row_f[:, 1, :], float(E * REGION // P), None, ALU.min))
            link(nc.vector.tensor_copy(place[:], row_f[:, 1, :]))
            link(nc.vector.tensor_scalar(row_f[:, 0, :], ps_g[0][0:1, 0:NBLOCK], float(E - 1), None, ALU.min))
            nc.vector.tensor_copy(expert[:], row_f[:, 0, :]).then_inc(ready, 1)

            def front(n, k, first):
                s = k % 2
                dve.wait_ge(xt_ps, n + 1)
                if not (first and k < 2):
                    dve.wait_ge(gu_ps, n - 1)
                nc.vector.tensor_copy(x_t[s][:], ps_x[s][:, 0:D]).then_inc(xt_sb, 1)

            def stage(n, k, first):
                s = k % 2
                dve.wait_ge(tanh_sb, n + 1)
                if not (first and k < 2):
                    dve.wait_ge(h_sb, n - 1)
                nc.vector.tensor_scalar(wh[s][:], ent[k][:, 1:2].bitcast(F32), 0.5, None, ALU.mult)
                nc.vector.scalar_tensor_tensor(out=gt[s][:], in0=tnh[s][:], scalar=1.0, in1=ps_gu[s][:, 0:HE],
                                               op0=ALU.add, op1=ALU.mult).then_inc(gate_sb, 1)
                dve.wait_ge(gate_sb, n + 1)
                if not (first and k < 2):
                    dve.wait_ge(ht_ps, n - 1)
                nc.vector.scalar_tensor_tensor(out=hw[s][:], in0=gt[s][:], scalar=wh[s][:, 0:1],
                                               in1=ps_gu[s][:, HE:2 * HE], op0=ALU.mult, op1=ALU.mult
                                               ).then_inc(h_sb, 1)
            front(0, 0, True)
            for n in range(NR):
                front(n + 1, (n + 1) % NR, n + 1 < NR)
                stage(n, n, True)
            with dve.Fori(0, LOOPS) as i:
                for k in range(BODY):
                    front(i * BODY + NR + k + 1, (k + 1) % NR, False)
                    stage(i * BODY + NR + k, k % NR, False)
            for n in range(NBLOCK - NR, NBLOCK):
                if n + 1 < NBLOCK:
                    front(n + 1, (n + 1) % NR, False)
                stage(n, n % NR, False)

    stack = ExitStack()
    with stack:
        NTILE = TOKENS // P
        ND = 4
        ys = [sb_(f"ys{i}", [P, TOPK, D], F32, stack) for i in range(ND)]
        acc = [sb_(f"acc{i}", [P, D], F32, stack) for i in range(ND)]
        red = [sb_(f"red{i}", [P, 2, D], F32, stack) for i in range(ND)]
        res = [sb_(f"res{i}", [P, D], F32, stack) for i in range(ND)]
        y_in = [sem(f"y_in{i}") for i in range(ND)]
        stored = [sem(f"stored{i}") for i in range(ND)]
        half, added = sem("half"), sem("added")
        added_p, half_p = sem("added_p"), sem("half_p")
        block = stack.enter_context(nc.Block())
        y_v = y_dram.rearrange("(n p j) d -> n p j d", p=P, j=TOPK)

        def tiles(eng, stage):
            for n in range(ND):
                stage(n, n, True)
            with eng.Fori(1, NTILE // ND) as i:
                for k in range(ND):
                    stage(i * ND + k, k, False)

        @block.sync
        def _(sp):
            def load(n, k, first):
                if not first:
                    sp.wait_ge(added, n - ND + 1)
                sp.dma_start(ys[k][:, :, :], y_dram[bass.ds(n * (P * TOPK), P * TOPK), :].rearrange(
                    "(p j) d -> p j d", j=TOPK)).then_inc(y_in[k], 16)
                sp.dma_start(acc[k][:, :], sum_dram[bass.ds(n * P, P), :]).then_inc(y_in[k], 16)
            tiles(sp, load)

        @block.scalar
        def _(act):
            def store(n, k, first):
                act.wait_ge(added, n + 1)
                act.dma_start(out[bass.ds(n * P, P), :], res[k][:, :]).then_inc(stored[k], 16)
            tiles(act, store)
            for k in range(ND):
                act.wait_ge(stored[k], 16 * NTILE // ND)

        @block.vector
        def _(dve):
            def add(n, k, first):
                dve.wait_ge(y_in[k], (n - k) * (32 // ND) + 32)
                if not first:
                    dve.wait_ge(added, n - ND + 1)
                nc.vector.tensor_tensor(red[k][:], ys[k][:, 0:2, :], ys[k][:, 2:4, :], ALU.add).then_inc(half, 1)
                dve.wait_ge(half, 2 * n + 1)
                nc.vector.tensor_tensor(red[k][:, 0, :], red[k][:, 0, :], red[k][:, 1, :], ALU.add).then_inc(half, 1)
                dve.wait_ge(half, 2 * n + 2)
                if not first:
                    dve.wait_ge(stored[k], (n - k) * (16 // ND))
                nc.vector.tensor_tensor(res[k][:], red[k][:, 0, :], acc[k][:], ALU.add).then_inc(added, 1)
            tiles(dve, add)


def _rope_tables():
    inv = (1.0 / np.float32(10000.0) ** (np.arange(0, DH, 2, dtype=np.float32) / np.float32(DH))).astype(np.float32)
    ang = np.outer(np.arange(SEQ, dtype=np.float32), inv).astype(np.float32)
    c, s = np.cos(ang).astype(np.float32), np.sin(ang).astype(np.float32)
    per_head = P // DH
    return np.repeat(np.concatenate([c, c], 1), per_head, 1), np.repeat(np.concatenate([-s, s], 1), per_head, 1)


def _dims_first(w):
    return w.reshape(D, KC, P // DH, DH).transpose(0, 1, 3, 2).reshape(D, D)


def kernel(**inputs):
    import concourse.bacc as bacc
    from concourse.bass_utils import run_bass_kernel_spmd

    a = {k: np.asarray(v) for k, v in inputs.items()}
    cos, sin = _rope_tables()
    arrays = {
        "x": a["L0_attn_x"].reshape(TOKENS, D),
        "wqkvr": np.concatenate([_dims_first(a["L0_attn_Wq"].T), _dims_first(a["L0_attn_Wk"].T), a["L0_attn_Wv"].T, a["L0_ffn_router_w"].T], 1),
        "wo": a["L0_attn_Wo"].T,
        "wgu_s": np.concatenate([a["L0_ffn_sgate_w"].T, a["L0_ffn_sup_w"].T], 1),
        "wd_s": a["L0_ffn_sdown_w"].T,
        "bias": a["L0_ffn_router_bias"],
        "wgu_e": np.concatenate([a["L0_ffn_gate_w"].transpose(0, 2, 1), a["L0_ffn_up_w"].transpose(0, 2, 1)], 2),
        "wd_e": a["L0_ffn_down_w"].transpose(0, 2, 1),
        "rope_cos": cos,
        "rope_sin": sin,
    }
    arrays = {k: np.ascontiguousarray(v) for k, v in arrays.items()}
    nc = bacc.Bacc("TRN2", target_bir_lowering=False, num_devices=1)
    args = [nc.dram_tensor(k, v.shape, mybir.dt.from_np(v.dtype), kind="ExternalInput").ap() for k, v in arrays.items()]
    out = nc.dram_tensor("out", (TOKENS, D), F32, kind="ExternalOutput").ap()
    block_kernel(nc, *args, out)
    r = run_bass_kernel_spmd(nc, [arrays], core_ids=[0])
    return r.results[0]["out"].reshape(BATCH, SEQ, D)
```

```python
from contextlib import ExitStack

import numpy as np

import concourse.bass as bass
from concourse import mybir

F32 = mybir.dt.float32
BF16 = mybir.dt.bfloat16
I32 = mybir.dt.int32
U32 = mybir.dt.uint32
ALU = mybir.AluOpType
ACT = mybir.ActivationFunctionType
AX = mybir.AxisListType

P = 128
BATCH, SEQ, D = 16, 512, 256
NT = SEQ // P
KC = D // P
NH, DH = 16, 16
NG, GH = 4, 4
E, TOPK, HE, HS = 32, 4, 128, 512
NM = HS // P
TOKENS = BATCH * SEQ
NPART = 3
Q_PART = [0, 0, 0, 1, 1, 2]
K_PART = [0, 1, 2, 0, 1, 0]
NSTACK = len(Q_PART)
KROWS = NSTACK * DH
MROWS = KROWS + NPART
SCALE = DH ** -0.5
NEG = -1e30
REGION = TOKENS
NBLOCK = TOKENS * TOPK // P + E
TABLE = E * REGION + P
N_CONSTS, N_EARLY, N_IDENT = 23, 21, 3
SKIP = 1 << 24
EPS = 1e-5
MAGIC = float(0x5F3759DF)

MAX_UNITS = [(0, 0, 4, 4), (1, 0, 4, 2), (2, 0, 2, 1), (2, 2, 2, 1), (3, 0, 2, 1), (3, 2, 2, 1)]
NU1 = len(MAX_UNITS)
NU2 = GH + 1


def hold(eng, passed):
    eng.sem_inc(passed, 1)


ORDER = [
    ("rankC",), ("gate", 0), ("placeV",), ("s1", 0, 0), ("gth", 0), ("up", 0), ("s1", 0, 1), ("copy",), ("s1", 0, 2),
    ("gate", 1), ("s1", 0, 3), ("s1", 0, 4), ("gth", 1), ("scat", 0), ("up", 1), ("lnA",), ("gate", 2), ("s1", 0, 5),
    ("negsplit", 0), ("gth", 2), ("scat", 1), ("s1", 1, 0), ("up", 2), ("s1", 1, 1), ("negT", 0), ("gate", 3),
    ("lnB",), ("lnC",), ("gth", 3), ("up", 3), ("s2", 0, 0), ("s2", 0, 1), ("s2", 0, 2), ("s1", 1, 2), ("xT", 0),
    ("xT", 1), ("xT", 2), ("s1", 1, 3), ("s1", 1, 4), ("qk", 0), ("s2", 0, 3), ("vr", 0), ("xT", 3), ("vr", 1),
    ("part0", 0), ("s1", 1, 5), ("negsplit", 1), ("s2", 0, 4), ("qk", 1), ("part1", 0), ("negT", 1), ("s1", 2, 0),
    ("s1", 2, 1), ("part0", 1), ("av", 0, 0), ("av", 0, 1), ("s1", 2, 2), ("s2", 1, 0), ("av", 0, 2), ("av", 0, 3),
    ("s1", 2, 3), ("partsT", 0), ("s1", 2, 4), ("s1", 2, 5), ("part1", 1), ("avT", 0), ("qk", 2), ("s2", 1, 1),
    ("s2", 1, 2), ("negsplit", 2), ("partsT", 1), ("s2", 1, 3), ("part0", 2), ("qk", 3), ("s2", 1, 4), ("negT", 2),
    ("part1", 2), ("vr", 2), ("s1", 3, 0), ("s1", 3, 1), ("part0", 3), ("av", 1, 0), ("av", 1, 1), ("av", 1, 2),
    ("av", 1, 3), ("s1", 3, 2), ("s2", 2, 0), ("partsT", 2), ("s1", 3, 3), ("part1", 3), ("s1", 3, 4), ("s2", 2, 1),
    ("avT", 1), ("s2", 2, 2), ("s2", 2, 3), ("vr", 3), ("s1", 3, 5), ("negsplit", 3), ("route",), ("partsT", 3),
    ("scat", 2), ("s2", 2, 4), ("negT", 3), ("av", 2, 0), ("av", 2, 1), ("av", 2, 2), ("av", 2, 3), ("s2", 3, 0),
    ("scat", 3), ("s2", 3, 1), ("avT", 2), ("stack", 0), ("s2", 3, 2), ("s2", 3, 3), ("rank",), ("s2", 3, 4),
    ("exps",), ("stack", 1), ("down", 0), ("down", 1), ("rankA",), ("av", 3, 0), ("av", 3, 1), ("av", 3, 2),
    ("av", 3, 3), ("rankB",), ("down", 2), ("avT", 3), ("down", 3), ("aT", 0), ("aT", 1), ("oproj", 0), ("oproj", 1),
]


def attention_steps(with_next):
    return [s for s in ORDER if with_next or s[0] not in NEXT_STEPS]


def last_steps(order):
    s, piece = [], 0
    for step in order:
        s.append(step)
        if step == ("rankC",):
            s.append(("fill_rows",))
        if step == ("scat", NT - 1):
            s.append(("fill",))
        if step[0] == "s2" and step[1:] != (0, 0) and piece < GU_PIECES:
            s.append(("load_gu", piece))
            piece += 1
        if step == ("s2", NG - 1, NU2 - 1):
            s += [("load_d", k) for k in range(D_PIECES)]
    assert piece == GU_PIECES
    return s


GU_PIECES, D_PIECES = 16, 4
FIRST_STEPS = [("lnA",), ("lnB",), ("lnC",)] + [("xT", t) for t in range(NT)] + \
    [("loaded", 0), ("qk", 0), ("vr", 0), ("part0", 0), ("part1", 0), ("qk", 1), ("vr", 1), ("part0", 1), ("part1", 1), ("partsT", 0),
     ("qk", 2), ("vr", 2), ("part0", 2), ("part1", 2), ("partsT", 1), ("qk", 3), ("vr", 3), ("part0", 3), ("part1", 3),
     ("partsT", 2), ("partsT", 3), ("stack", 0), ("stack", 1), ("loaded", 1), ("route",), ("exps",),
     ("rank",), ("rankA",), ("rankB",)]

BANKS_OF = {"gate": ("gated",), "up": ("hidden",), "negT": ("neg_t",), "avT": ("attn",), "xT": ("xn_t",), "qk": ("rope",),
            "vr": ("logits",), "partsT": ("q_t", "k_t"), "aT": ("attn_t",), "rank": ("ranked",)}
NEXT_STEPS = ("lnA", "lnB", "lnC", "xT", "qk", "vr", "part0", "part1", "partsT", "stack", "route", "exps", "rank", "rankA",
              "rankB")
TIMES = {"gated": NM, "hidden": NM, "neg_t": NG, "attn": NG, "xn_t": NT, "rope": NT, "logits": NT, "q_t": NT, "k_t": NT,
         "attn_t": 2, "ranked": 1, "row_max": NG * NU1, "probs": NG * NU2, "sums": 2}


def plans(steps, last_banks, last_units):
    banks, units, last_banks, last_units = {}, {}, list(last_banks), list(last_units)
    nb = nu = 0
    for step in steps:
        idx, ahead = step[1] if len(step) > 1 else 0, int(step[0] in NEXT_STEPS)
        for k, name in enumerate(BANKS_OF.get(step[0], ())):
            banks[step, k] = (nb, last_banks[nb])
            last_banks[nb] = (name, idx, ahead)
            nb = (nb + 1) % len(last_banks)
        if step[0] in ("s1", "s2") or step == ("down", 0):
            units[step] = (nu, last_units[nu])
            last_units[nu] = {"s1": ("row_max", idx * NU1 + step[-1], 0), "s2": ("probs", idx * NU2 + step[-1], 0),
                              "down": ("sums", 1, 0)}[step[0]]
            nu = (nu + 1) % len(last_units)
    return banks, units, last_banks, last_units


def one_later(last):
    return [u and (u[0], u[1], u[2] - 1) for u in last]


def block_kernel(nc, x, wqkvr, wo, wgu_s, wd_s, bias, wgu_e, wd_e, rope_cos, rope_sin, out):
    values = nc.dram_tensor("values", (E * REGION, D), F32, kind="Internal").ap()
    sum_dram = nc.dram_tensor("sum_dram", (TOKENS, D), F32, kind="Internal").ap()
    table = nc.dram_tensor("table", (TABLE, 2), I32, kind="Internal").ap()
    y_dram = nc.dram_tensor("y_dram", (TOKENS * TOPK, D), F32, kind="Internal").ap()

    ctx = ExitStack()
    with ctx:
        def sb(name, shape, dt=F32, where=None):
            return (where or ctx).enter_context(nc.sbuf_tensor(name, shape, dt))

        def sem(name):
            return ctx.enter_context(nc.semaphore(name))

        ident = sb("ident", [P, P])
        identb = sb("identb", [P, P], BF16)
        iota_e = sb("iota_e", [P, E])
        counts = sb("counts", [P, E])
        we_gu = sb("we_gu", [P, E * KC * 2 * HE])
        we_d = sb("we_d", [P, E * D])
        ps_g = [ctx.enter_context(nc.psum_tensor(f"ps_g{i}", [P, 512], F32)) for i in range(3)]
        ps_u = [ctx.enter_context(nc.psum_tensor(f"ps_u{i}", [P, 2, 512], F32)) for i in range(2)]
        ps_av = ctx.enter_context(nc.psum_tensor("ps_av", [P, 512], F32))

        phase_a(nc, sb, sem, ident, identb, iota_e, counts, we_gu, we_d, ps_g, ps_u, ps_av, x, wqkvr, wgu_e, wd_e, wo, wgu_s, wd_s, bias,
                rope_cos, rope_sin, values, sum_dram, table)
        phase_bcd(nc, sb, sem, ident, iota_e, counts, we_gu, we_d, ps_g, ps_u, ps_av, values, sum_dram, table,
                  y_dram, out)


def phase_a(nc, sb_, sem, ident, identb, iota_e, counts, we_gu, we_d, ps_g, ps_u, ps_av, x, wqkvr, wgu_e, wd_e, wo, wgu_s, wd_s, bias,
            rope_cos, rope_sin, values, sum_dram, table):
    stack = ExitStack()
    with stack:
        def sb(name, shape, dt=F32):
            return sb_(name, shape, dt, stack)

        def carve(space):
            used = [0]

            def take(shape, dt=F32):
                n = int(np.prod(shape[1:])) * (2 if dt == BF16 else 4) // 4
                used[0] += n
                ap = space[:, used[0] - n:used[0]]
                ap = ap.bitcast(BF16) if dt == BF16 else ap
                assert used[0] <= space.shape[1]
                names = ["d%d" % i for i in range(len(shape) - 1)]
                if len(names) == 1:
                    return ap
                return ap.rearrange("p (%s) -> p %s" % (" ".join(names), " ".join(names)),
                                    **dict(zip(names[1:], shape[2:])))
            return take
        in_gu, in_d = carve(we_gu), carve(we_d)

        w_qkvr = in_gu([P, KC, 3 * D + E])
        w_o = sb("w_o", [P, KC, D])
        w_gu = in_gu([P, KC, 2 * HS])
        w_d = sb("w_d", [P, NM, D])
        bias_bc = sb("bias_bc", [P, E])
        cos = sb("cos", [P, NT, P])
        sin = sb("sin", [P, NT, P])
        mask_qk = sb("mask_qk", [P, P], BF16)
        mask_kq = sb("mask_kq", [P, P], BF16)
        before = sb("before", [P, P], BF16)
        ones = sb("ones", [P, P], BF16)
        tri_f = sb("tri_f", [P, P])

        zeros = sb("zeros", [P, D])
        row_p = sb("row_p", [P, 1])
        fill_f = sb("fill_f", [P, 2, E])
        fill_row = sb("fill_row", [P, E], I32)

        xin = in_gu([P, NT, D])
        stats = sb("stats", [P, NT, 6])
        mv = sb("mv", [P, NT, 2])
        ve = sb("ve", [P, NT])
        rs = sb("rs", [P, NT])
        rs_t = sb("rs_t", [P, NT])
        xn = in_gu([P, NT, D])
        xn_t = in_gu([P, KC, SEQ])
        rp1 = in_gu([P, 2, 2 * D])
        rp2 = in_gu([P, 2, 2 * D])
        rqk = sb("rqk", [P, 2 * D])
        rres = in_gu([P, 2 * D])
        parts = in_gu([P, 2, NPART, 2 * D], BF16)
        q_t = in_gu([P, NPART, KC, SEQ], BF16)
        k_t = in_gu([P, NPART, KC, SEQ], BF16)
        v_new = in_gu([P, NT, D])
        logits = sb("logits", [P, NT, E])

        q_st = in_d([P, NH, SEQ], BF16)
        k_st = in_d([P, NH, SEQ], BF16)
        v_pad = sb("v_pad", [P, NT, NH, 2 * DH])
        neg = sb("neg", [P, 2, NT, GH])
        neg_r = sb("neg_r", [P, NT, GH])
        neg_p = sb("neg_p", [P, 2, NT, NPART, GH], BF16)
        neg_t = sb("neg_t", [NPART * GH, 2, SEQ], BF16)
        probs = [sb(f"probs{i}", [P, NU2, 1024]) for i in range(2)]
        av = sb("av", [P, SEQ])
        rden = sb("rden", [P, NT, GH])
        attn = sb("attn", [P, NT, D])
        attn_t = sb("attn_t", [P, KC, SEQ])
        th = in_gu([P, 2, SEQ])
        gth = sb("gth", [P, SEQ])
        hid = sb("hid", [P, NM, SEQ])
        xres = sb("xres", [P, NT, D])
        osum = sb("osum", [P, NT, D])
        lg = sb("lg", [P, NT, E])
        top_v = sb("top_v", [P, NT, 8])
        top_i = sb("top_i", [P, NT, 8], U32)
        top_f = sb("top_f", [P, NT, TOPK])
        onehot = sb("onehot", [P, NT, TOPK, E])
        chosen = sb("chosen", [P, NT, E], BF16)
        ex = sb("ex", [P, NT, E + TOPK])
        exo = sb("exo", [P, NT, E + TOPK])
        zs = sb("zs", [P, 4, NT])
        pr4 = sb("pr4", [P, NT, TOPK])
        base = sb("base", [P, E])
        region = sb("region", [P, E])
        pos = sb("pos", [P, NT, E])
        slotf = sb("slotf", [P, NT * TOPK])
        slot = sb("slot", [P, NT * TOPK], I32)
        dest_f = sb("dest_f", [P, NT * TOPK])
        entry = sb("entry", [P, NT * TOPK, 2], I32)
        xs = sb("xs", [P, NT, D])

        S = {n: sem(n) for n in TIMES}
        consts, w_front, weights, inited, table_set = sem("consts"), sem("w_front"), sem("weights"), sem("inited"), sem("table_set")
        xs_ready, slots = sem("xs_ready"), sem("slots")
        x_in, x_res, sum_out = sem("x_in"), sem("x_res"), sem("sum_out")
        stacked = [sem("stacked0"), sem("stacked1")]
        neg_rows = [sem("neg_rows0"), sem("neg_rows1")]
        scattered = sem("scattered")
        xn_ready, parts_ready, v_placed = sem("xn_ready"), sem("parts_ready"), sem("v_placed")
        v_ready = sem("v_ready")
        summed, part0_ready, part1_ready = sem("summed"), sem("part0_ready"), sem("part1_ready")
        passed_pool, passed_dve, passed_sp = sem("passed_pool"), sem("passed_dve"), sem("passed_sp")
        we_in, fill_chain, fill_ready, filled = sem("we_in"), sem("fill_chain"), sem("fill_ready"), sem("filled")
        neg_parts, tanh_done, av_out, exps, chosen_ready = \
            sem("neg_parts"), sem("tanh_done"), sem("av_out"), sem("exps"), sem("chosen_ready")
        pe = {n: sem("pe_" + n) for n in ("xT", "qk", "vr", "qT", "kT", "gate", "up", "s1", "negT", "s2", "av", "avT",
                                          "aT", "sum", "rank")}
        dve_front, dve_chain, pool_chain, ex_ready, rope1 = \
            sem("dve_front"), sem("dve_chain"), sem("pool_chain"), sem("ex_ready"), sem("rope1")

        STACK_DMAS = NSTACK * 2

        SCATTERS = 2 * 16 * NT * TOPK

        def done(name, b, k):
            return b * TIMES[name] + k + 1

        block = stack.enter_context(nc.Block())
        body = attention_steps(True)
        tail = last_steps(attention_steps(False))

        def run(eng, handlers):
            def steps(order, b, nb, first, last_banks, last_units):
                bp, up, lb, lu = plans(order, last_banks, last_units)
                for step in order:
                    if step[0] in handlers:
                        handlers[step[0]](nb if step[0] in NEXT_STEPS else b, step, (bp, up, b, first))
                return lb, lu
            lb, lu = steps(FIRST_STEPS, 0, 0, True, [None] * 3, [None] * 2)
            lb, lu = steps(body, 0, 1, False, one_later(lb), lu)
            lb, lu = one_later(lb), one_later(lu)
            with eng.Fori(1, BATCH - 1) as b:
                assert (lb, lu) == tuple(map(one_later, steps(body, b, b + 1, False, lb, lu)))
            steps(tail, BATCH - 1, None, False, lb, lu)

        class Chain:

            def __init__(self, eng, s, per, passed):
                self.eng, self.s, self.per, self.passed, self.k = eng, s, per, passed, 0

            def link(self, b, ins, apart=False):
                ins.then_inc(self.s, 1)
                self.k = self.k % self.per + 1
                self.eng.wait_ge(self.s, b * self.per + self.k)
                if apart:
                    hold(self.eng, self.passed)

            def closed(self):
                assert self.k == self.per, (self.k, self.per)

        @block.sync
        def _(sp):
            def tokens(dram, b):
                return dram[bass.ds(b * SEQ, SEQ), :].rearrange("(t p) d -> p t d", p=P)

            sp.dma_start(xin[:, :, :], tokens(x, 0)).then_inc(x_in, 16)
            sp.dma_start(w_qkvr[:, :, :], wqkvr.rearrange("(c p) n -> p c n", p=P)).then_inc(w_front, 16)
            sp.dma_start(cos[:, :, :], rope_cos.rearrange("(t p) c -> p t c", p=P)).then_inc(w_front, 16)
            sp.dma_start(sin[:, :, :], rope_sin.rearrange("(t p) c -> p t c", p=P)).then_inc(w_front, 16)
            sp.dma_start(bias_bc[:, :], bias.partition_broadcast(P)).then_inc(weights, 16)
            sp.dma_start(w_gu[:, :, :], wgu_s.rearrange("(c p) n -> p c n", p=P)).then_inc(weights, 16)
            sp.dma_start(w_d[:, :, :], wd_s.rearrange("(c p) n -> p c n", p=P)).then_inc(weights, 16)
            sp.dma_start(w_o[:, :, :], wo.rearrange("(c p) n -> p c n", p=P)).then_inc(weights, 16)

            def stack_rows(nb, step, env):
                sp.wait_ge(S["q_t"], done("q_t", nb, NT - 1))
                sp.wait_ge(S["k_t"], done("k_t", nb, NT - 1))
                c = step[1]
                if not env[3]:
                    sp.wait_ge(pe["s2"], nb * NG * NU2 - (KC - 1 - c) * 2 * NU2)
                for dst, src, which in ((q_st, q_t, Q_PART), (k_st, k_t, K_PART)):
                    for s in range(NSTACK):
                        sp.dma_start(dst[DH * s:DH * (s + 1), 8 * c:8 * c + 8, :], src[:, which[s], c, :]
                                     ).then_inc(stacked[c], 16)

            def x_load(nb):
                sp.wait_ge(xn_ready, NT * nb)
                sp.dma_start(xin[:, :, :], tokens(x, nb)).then_inc(x_in, 16)

            def gate(b, step, env):
                if step[1] == 0:
                    sp.wait_ge(S["sums"], 2 * b)
                    sp.dma_start(xres[:, :, :], tokens(x, b)).then_inc(x_res, 16)
                    if env[0].get((("xT", 0), 0)):
                        x_load(b + 1)

            def neg_store(b, step, env):
                g = step[1]
                sp.wait_ge(S["neg_t"], done("neg_t", b, g))
                sp.dma_start(q_st[KROWS:MROWS, GH * g:GH * g + GH, :],
                             neg_t[:, g % 2, :]).then_inc(neg_rows[g % 2], 16)

            def store(b, step, env):
                if step[1] == 1:
                    sp.wait_ge(S["sums"], 2 * b + 2)
                    sp.dma_start(tokens(sum_dram, b), osum[:, :, :]).then_inc(sum_out, 16)

            def loaded(b, step, env):
                if step[1] == 1:
                    sp.wait_ge(inited, 1)
                    sp.dma_start(table.rearrange("(p r) c -> p (r c)", p=P),
                                 probs[0][:, :, :].rearrange("p u n -> p (u n)")[:, 0:2 * TABLE // P].bitcast(I32)
                                 ).then_inc(table_set, 16)

            run(sp, {"loaded": loaded, "stack": stack_rows, "gate": gate, "negT": neg_store, "oproj": store})
            sp.wait_ge(sum_out, 16 * BATCH)

        @block.gpsimd
        def _(pool):
            blank = probs[0][:, :, :].rearrange("p u n -> p (u n)")[:, 0:2 * TABLE // P].bitcast(I32)
            chain = Chain(pool, pool_chain, NT, passed_pool)
            made = [0]

            def const(ins):
                made[0] += 1
                ins.then_inc(consts, 1)
                pool.wait_ge(consts, made[0])

            def zeros_kept(value, base, mult, step):
                const(pool.memset(tri_f[:], 0.0))
                const(pool.affine_select(out=tri_f[:], in_=tri_f[:], compare_op=ALU.is_ge, fill=value, base=base,
                                         pattern=[[step, P]], channel_multiplier=mult))

            const(pool.memset(ident[:], 0.0))
            const(pool.affine_select(out=ident[:], in_=ident[:], compare_op=ALU.not_equal, fill=1.0, base=0,
                                     pattern=[[-1, P]], channel_multiplier=1))
            const(pool.tensor_copy(identb[:], ident[:]))
            assert made[0] == N_IDENT
            const(pool.memset(v_pad[:], 0.0))
            const(pool.memset(v_pad[:, :, :, DH:DH + 1], 1.0))
            const(pool.memset(ones[:], 1.0))
            const(pool.memset(zeros[:], 0.0))
            const(pool.iota(row_p[:], pattern=[[0, 1]], base=0, channel_multiplier=1,
                            allow_small_or_imprecise_dtypes=True))
            const(pool.memset(counts[:], 0.0))
            const(pool.memset(entry[:], 0))
            const(pool.iota(iota_e[:], pattern=[[1, E]], base=0, channel_multiplier=0,
                            allow_small_or_imprecise_dtypes=True))
            const(pool.iota(dest_f[:], pattern=[[P * TOPK, NT], [1, TOPK]], base=0, channel_multiplier=TOPK,
                            allow_small_or_imprecise_dtypes=True))
            zeros_kept(NEG, 0, 1, -1)
            const(pool.tensor_copy(mask_qk[:], tri_f[:]))
            zeros_kept(NEG, 0, -1, 1)
            const(pool.tensor_copy(mask_kq[:], tri_f[:]))
            zeros_kept(1.0, 0, 1, -1)
            const(pool.tensor_copy(before[:], tri_f[:]))
            assert made[0] == N_EARLY

            def qkv(nb, step, env):
                t = step[1]
                pool.wait_ge(S["rope"], done("rope", nb, t))
                if not (env[3] and t < 1):
                    pool.wait_ge(parts_ready, NT * nb + t)
                hold(pool, passed_pool)
                pool.tensor_tensor(rqk[:], rp1[:, t % 2, :], rp2[:, t % 2, :], ALU.add).then_inc(summed, 1)
                pool.wait_ge(part0_ready, NT * nb + t + 1)
                chain.link(nb, pool.tensor_tensor(rres[:], rqk[:], parts[:, t % 2, 0, :], ALU.subtract))
                pool.wait_ge(part1_ready, NT * nb + t + 1)
                pool.tensor_tensor(parts[:, t % 2, 2, :], rres[:], parts[:, t % 2, 1, :],
                                   ALU.subtract).then_inc(parts_ready, 1)
                if t == NT - 1:
                    chain.closed()

            def scatter(b, step, env):
                t = step[1]
                pool.wait_ge(xs_ready, NT * b + NT)
                pool.wait_ge(slots, b + 1)
                hold(pool, passed_pool)
                for k in range(TOPK * t, TOPK * (t + 1)):
                    pool.indirect_dma_start(table[:, :], bass.IndirectOffsetOnAxis(ap=slot[:, k:k + 1], axis=0),
                                            entry[:, k, :], None).then_inc(scattered, 16)
                    pool.indirect_dma_start(values[:, :], bass.IndirectOffsetOnAxis(ap=slot[:, k:k + 1], axis=0),
                                            xs[:, k // TOPK, :], None).then_inc(scattered, 16)

            def fill(b, step, env):
                pool.wait_ge(fill_ready, 1)
                for e in range(E):
                    pool.indirect_dma_start(values[:, :], bass.IndirectOffsetOnAxis(ap=fill_row[:, e:e + 1], axis=0),
                                            zeros[:, :], None, bounds_check=E * REGION - 1, oob_is_err=False
                                            ).then_inc(filled, 16)

            def loaded(b, step, env):
                if step[1] == 1:
                    pool.wait_ge(parts_ready, NT)
                    const(pool.memset(k_st[KROWS:MROWS, :, :], 1.0))
                    const(pool.memset(blank, 0))
                    pool.memset(blank.rearrange("p (r c) -> p r c", c=2)[:, :, 0:1], SKIP).then_inc(inited, 1)
                    assert made[0] == N_CONSTS
                    pool.wait_ge(table_set, 16)

            run(pool, {"loaded": loaded, "qk": qkv, "scat": scatter, "fill": fill})
            pool.wait_ge(filled, 16 * E)
            pool.wait_ge(scattered, SCATTERS * BATCH)

        @block.scalar
        def _(act):
            def xT(nb, step, env):
                t, bank = step[1], env[0][step, 0][0]
                act.wait_ge(pe["xT"], NT * nb + t + 1)
                if t == 0 and not env[3]:
                    act.wait_ge(pe["up"], NM * nb)
                nc.scalar.activation(xn_t[:, :, t * P:(t + 1) * P],
                                     ps_g[bank][:, 0:D].rearrange("p (c n) -> p c n", c=KC), ACT.Copy
                                     ).then_inc(S["xn_t"], 1)

            def qkv(nb, step, env):
                t, bank = step[1], env[0][step, 0][0]
                act.wait_ge(pe["vr"], NT * nb + t + 1)
                if t == 0:
                    act.wait_ge(v_placed, nb)
                    if not env[3]:
                        act.wait_ge(chosen_ready, nb)
                nc.scalar.activation(v_new[:, t, :], ps_g[bank][:, 0:D], ACT.Copy).then_inc(v_ready, 1)
                nc.scalar.activation(logits[:, t, :], ps_g[bank][:, D:D + E], ACT.Copy).then_inc(S["logits"], 1)

            def part0(nb, step, env):
                t = step[1]
                act.wait_ge(summed, NT * nb + t + 1)
                if not (env[3] and t < 2):
                    act.wait_ge(pe["kT"], NT * nb + t - 1)
                nc.scalar.activation(parts[:, t % 2, 0, :], rqk[:], ACT.Copy).then_inc(part0_ready, 1)

            def part1(nb, step, env):
                t = step[1]
                act.wait_ge(pool_chain, NT * nb + t + 1)
                nc.scalar.activation(parts[:, t % 2, 1, :], rres[:], ACT.Copy).then_inc(part1_ready, 1)

            def place_v(b, step, env):
                act.wait_ge(v_ready, NT * (b + 1))
                act.wait_ge(pe["av"], NG * b)
                nc.scalar.activation(v_pad[:, :, :, 0:DH], v_new[:].rearrange("p t (h r) -> p t h r", r=DH), ACT.Copy
                                     ).then_inc(v_placed, 1)

            def partsT(nb, step, env):
                t = step[1]
                for k, (dst, p_, n) in enumerate(((q_t, "qT", "q_t"), (k_t, "kT", "k_t"))):
                    bank = env[0][step, k][0]
                    act.wait_ge(pe[p_], NT * nb + t + 1)
                    if t == 0 and k == 0:
                        for c in range(KC):
                            act.wait_ge(stacked[c], 16 * STACK_DMAS * nb)
                    nc.scalar.activation(
                        dst[:, :, :, t * P:(t + 1) * P].rearrange("p a c n -> p (a c) n"),
                        ps_g[bank][:, :].bitcast(BF16)[:, 0:NPART * D].rearrange("p (a n) -> p a n", n=P), ACT.Copy
                    ).then_inc(S[n], 1)

            def gate(b, step, env):
                m = step[1]
                act.wait_ge(pe["gate"], NM * b + m + 1)
                if m >= 2:
                    act.wait_ge(S["hidden"], done("hidden", b, m - 2))
                else:
                    act.wait_ge(S["hidden"], NM * b)
                nc.scalar.activation(th[:, m % 2, :], ps_g[env[0][step, 0][0]][:, :], ACT.Tanh, scale=0.5
                                     ).then_inc(tanh_done, 1)

            def copy(b, step, env):
                act.wait_ge(xn_ready, NT * (b + 1))
                act.wait_ge(scattered, SCATTERS * b)
                for t in range(NT):
                    nc.scalar.activation(xs[:, t, :], xn[:, t, :], ACT.Copy).then_inc(xs_ready, 1)

            def negT(b, step, env):
                g, bank = step[1], env[0][step, 0][0]
                act.wait_ge(pe["negT"], NG * b + g + 1)
                if g >= 2:
                    act.wait_ge(neg_rows[g % 2], 16 * (2 * b + g // 2))
                else:
                    act.wait_ge(neg_rows[g % 2], 16 * 2 * b)
                nc.scalar.activation(neg_t[:, g % 2, :], ps_g[bank][:, :].bitcast(BF16)[0:NPART * GH, 0:SEQ],
                                     ACT.Copy).then_inc(S["neg_t"], 1)

            def s2(b, step, env):
                _, g, u = step
                act.wait_ge(pe["s2"], NG * NU2 * b + NU2 * g + u + 1)
                if isinstance(b, int) and (b, g, u) == (0, 0, 0):
                    act.wait_ge(table_set, 16)
                if u == 0:
                    act.wait_ge(pe["av"], NG * b + (g - 1 if g >= 2 else 0))
                nc.scalar.activation(probs[g % 2][:, u, :], ps_u[env[1][step][0]][:, :, :].rearrange("p a n -> p (a n)"),
                                     ACT.Exp, scale=SCALE).then_inc(S["probs"], 1)

            def out_av(b, step, env):
                g = step[1]
                if step[2] < NT - 1:
                    return
                act.wait_ge(pe["av"], NG * b + g + 1)
                act.wait_ge(pe["avT"], NG * b + g)
                nc.scalar.activation(av[:, :], ps_av[:, :], ACT.Copy).then_inc(av_out, 1)

            def aT(b, step, env):
                p_, bank = step[1], env[0][step, 0][0]
                act.wait_ge(pe["aT"], 2 * b + p_ + 1)
                act.wait_ge(pe["sum"], 2 * b)
                nc.scalar.activation(
                    attn_t[:, :, 2 * p_ * P:2 * (p_ + 1) * P].rearrange("p c (t n) -> p t c n", t=2),
                    ps_g[bank][:, :].rearrange("p (t c n) -> p t c n", t=2, c=KC), ACT.Copy).then_inc(S["attn_t"], 1)

            def exponentials(b, step, env):
                act.wait_ge(ex_ready, b + 1)
                nc.scalar.activation(exo[:, :, :], ex[:, :, :], ACT.Exp).then_inc(exps, 1)

            def load_gu(b, step, env):
                k, n = step[1], E // GU_PIECES
                if k == 0:
                    act.wait_ge(xn_ready, NT * BATCH)
                    act.wait_ge(xs_ready, NT * BATCH)
                    act.wait_ge(pe["kT"], NT * BATCH)
                    act.wait_ge(parts_ready, NT * BATCH)
                    act.wait_ge(v_placed, BATCH)
                    act.wait_ge(S["hidden"], NM * BATCH)
                    for c in range(KC):
                        act.wait_ge(stacked[c], 16 * STACK_DMAS * BATCH)
                act.dma_start(we_gu[:, k * n * KC * 2 * HE:(k + 1) * n * KC * 2 * HE].rearrange("p (e n) -> p e n", n=2 * HE),
                              wgu_e[k * n:(k + 1) * n, :, :].rearrange("e (c p) n -> p (e c) n", p=P)).then_inc(we_in, 16)

            def load_d(b, step, env):
                k, n = step[1], E // D_PIECES
                act.wait_ge(pe["s2"], NG * NU2 * BATCH)
                act.dma_start(we_d[:, k * n * D:(k + 1) * n * D].rearrange("p (e n) -> p e n", n=D),
                              wd_e[k * n:(k + 1) * n, :, :].rearrange("e p n -> p e n")).then_inc(we_in, 16)

            def loaded(b, step, env):
                if step[1] == 1:
                    act.wait_ge(consts, N_EARLY)

            run(act, {"loaded": loaded, "xT": xT, "vr": qkv, "partsT": partsT, "gate": gate, "copy": copy, "part0": part0, "part1": part1,
                      "placeV": place_v, "negT": negT, "s2": s2,
                      "av": out_av, "aT": aT, "exps": exponentials, "load_gu": load_gu, "load_d": load_d})
            act.wait_ge(we_in, 16 * (GU_PIECES + D_PIECES))

        @block.vector
        def _(dve):
            front = Chain(dve, dve_front, 2 + 3 + 3 * 3 + 6 + 7, passed_dve)
            back = Chain(dve, dve_chain, 3 * NG + NG + 4, passed_dve)

            def ln_a(nb, step, env):
                dve.wait_ge(x_in, 16 * (nb + 1))
                dve.wait_ge(xn_ready, NT * nb)
                for t in range(NT):
                    ins = nc.vector.bn_stats(stats[:, t, :], xin[:, t, :])
                front.link(nb, ins, apart=True)
                for t in range(NT):
                    ins = nc.vector.bn_aggr(mv[:, t, :], stats[:, t, :])
                front.link(nb, ins)
                front.link(nb, nc.vector.tensor_scalar(ve[:], mv[:, :, 1], EPS, None, ALU.add))

            def ln_b(nb, step, env):
                front.link(nb, nc.vector.tensor_scalar(rs_t[:].bitcast(I32), ve[:].bitcast(I32), 1, None,
                                                       ALU.arith_shift_right))
                front.link(nb, nc.vector.tensor_scalar(rs[:].bitcast(I32), rs_t[:].bitcast(I32), -1.0, MAGIC,
                                                       ALU.mult, ALU.add))
                for _ in range(3):
                    front.link(nb, nc.vector.scalar_tensor_tensor(out=rs_t[:], in0=rs[:], scalar=-0.5, in1=rs[:],
                                                                  op0=ALU.mult, op1=ALU.mult))
                    front.link(nb, nc.vector.tensor_tensor(rs_t[:], rs_t[:], ve[:], ALU.mult))
                    front.link(nb, nc.vector.scalar_tensor_tensor(out=rs[:], in0=rs_t[:], scalar=1.5, in1=rs[:],
                                                                  op0=ALU.add, op1=ALU.mult))

            def ln_c(nb, step, env):
                dve.wait_ge(xs_ready, NT * nb)
                dve.wait_ge(pe["xT"], NT * nb)
                for t in range(NT):
                    nc.vector.tensor_scalar(xn[:, t, :], xin[:, t, :], mv[:, t, 0:1], rs[:, t:t + 1], ALU.subtract,
                                            ALU.mult).then_inc(xn_ready, 1)

            def qkv(nb, step, env):
                t, bank = step[1], env[0][step, 0][0]
                dve.wait_ge(pe["qk"], NT * nb + t + 1)
                if not (env[3] and t < 2):
                    dve.wait_ge(parts_ready, NT * nb + t - 1)
                def halves(a):
                    return a.rearrange("p (g s c) -> p g s c", g=2 * KC, s=2)
                nc.vector.tensor_tensor(rp1[:, t % 2, :].rearrange("p (g c) -> p g c", c=P),
                                        ps_g[bank][:, :].rearrange("p (g c) -> p g c", c=P),
                                        cos[:, t:t + 1, :].broadcast_to([P, 2 * KC, P]), ALU.mult).then_inc(rope1, 1)
                nc.vector.tensor_tensor(halves(rp2[:, t % 2, :]), halves(ps_g[bank][:, :])[:, :, ::-1, :],
                                        sin[:, t:t + 1, :].rearrange("p o (s c) -> p o s c", s=2
                                                                     ).broadcast_to([P, 2 * KC, 2, P // 2]), ALU.mult
                                        ).then_inc(S["rope"], 1)

            def gated(b, step, env):
                m = step[1]
                bank = env[0][("gate", m), 0][0]
                dve.wait_ge(tanh_done, NM * b + m + 1)
                dve.wait_ge(S["hidden"], NM * b + m)
                nc.vector.scalar_tensor_tensor(out=gth[:], in0=th[:, m % 2, :], scalar=1.0, in1=ps_g[bank][:, :],
                                               op0=ALU.add, op1=ALU.mult).then_inc(S["gated"], 1)

            def hidden(b, step, env):
                m, bank = step[1], env[0][step, 0][0]
                dve.wait_ge(S["gated"], done("gated", b, m))
                dve.wait_ge(pe["up"], NM * b + m + 1)
                dve.wait_ge(pe["sum"], 2 * b)
                nc.vector.scalar_tensor_tensor(out=hid[:, m, :], in0=gth[:], scalar=0.5,
                                               in1=ps_g[bank][:, :], op0=ALU.mult, op1=ALU.mult
                                               ).then_inc(S["hidden"], 1)

            def s1(b, step, env):
                _, g, u = step
                i, h0, nh, per_bank = MAX_UNITS[u]
                ps = ps_u[env[1][step][0]]
                n = (i + 1) * P
                if u == 0:
                    dve.wait_ge(neg_parts, NG * b + max(0, g - 1))
                dve.wait_ge(pe["s1"], NG * NU1 * b + NU1 * g + u + 1)
                if per_bank > 1:
                    src = ps[:, 0:nh // per_bank, :].rearrange("p a (h n) -> p (a h) n", n=n)
                else:
                    src = ps[:, :, 0:n]
                nc.vector.tensor_reduce(neg[:, g % 2, i, h0:h0 + nh], src, AX.X, ALU.max, negate=True
                                        ).then_inc(S["row_max"], 1)

            def negsplit(b, step, env):
                g = step[1]
                dve.wait_ge(S["row_max"], done("row_max", b, NU1 * g + NU1 - 1))
                dve.wait_ge(pe["negT"], NG * b + max(0, g - 1))
                dve.wait_ge(neg_parts, NG * b + g)
                n_, np_ = neg[:, g % 2, :, :], neg_p[:, g % 2, :, :, :]
                back.link(b, nc.vector.tensor_copy(np_[:, :, 0, :], n_))
                back.link(b, nc.vector.tensor_tensor(neg_r[:], n_, np_[:, :, 0, :], ALU.subtract))
                back.link(b, nc.vector.tensor_copy(np_[:, :, 1, :], neg_r[:]))
                nc.vector.tensor_tensor(np_[:, :, 2, :], neg_r[:], np_[:, :, 1, :], ALU.subtract
                                        ).then_inc(neg_parts, 1)

            def avT(b, step, env):
                g, bank = step[1], env[0][step, 0][0]
                ps = ps_g[bank][:, :].rearrange("p (t h c) -> p t h c", t=NT, c=2 * DH)
                dve.wait_ge(pe["avT"], NG * b + g + 1)
                dve.wait_ge(pe["aT"], 2 * b)
                dve.wait_ge(S["attn"], NG * b + g)
                back.link(b, nc.vector.reciprocal(rden[:], ps[:, :, :, DH]))
                nc.vector.tensor_tensor(
                    attn[:, :, g * GH * DH:(g + 1) * GH * DH].rearrange("p t (h c) -> p t h c", c=DH),
                    ps[:, :, :, 0:DH], rden[:].rearrange("p t (h o) -> p t h o", o=1).broadcast_to([P, NT, GH, DH]),
                    ALU.mult).then_inc(S["attn"], 1)

            def oproj(b, step, env):
                p_, u = step[1], env[1][("down", 0)][0]
                dve.wait_ge(pe["sum"], 2 * b + p_ + 1)
                if p_ == 0:
                    dve.wait_ge(x_res, 16 * (b + 1))
                    dve.wait_ge(sum_out, 16 * b)
                nc.vector.tensor_tensor(osum[:, 2 * p_:2 * p_ + 2, :],
                                        ps_u[u][:, p_, :].rearrange("p (t n) -> p t n", t=2),
                                        xres[:, 2 * p_:2 * p_ + 2, :], ALU.add).then_inc(S["sums"], 1)

            def route(b, step, env):
                dve.wait_ge(S["logits"], done("logits", b, NT - 1))
                dve.wait_ge(exps, b)
                dve.wait_ge(slots, b)
                front.link(b, nc.vector.tensor_tensor(
                    lg[:], logits[:], bias_bc[:].rearrange("p (o e) -> p o e", o=1).broadcast_to([P, NT, E]), ALU.add), apart=True)
                for t in range(NT):
                    ins = nc.vector.max(top_v[:, t, :], lg[:, t, :])
                front.link(b, ins, apart=True)
                for t in range(NT):
                    ins = nc.vector.max_index(top_i[:, t, :], top_v[:, t, :], lg[:, t, :])
                front.link(b, ins)
                front.link(b, nc.vector.tensor_copy(top_f[:], top_i[:, :, 0:TOPK]))
                front.link(b, nc.vector.tensor_tensor(
                    onehot[:].rearrange("p t j e -> p (t j) e"),
                    iota_e[:].rearrange("p (o e) -> p o e", o=1).broadcast_to([P, NT * TOPK, E]),
                    top_f[:].rearrange("p t (j o) -> p (t j) o", o=1).broadcast_to([P, NT * TOPK, E]), ALU.is_equal))
                dve.wait_ge(pe["rank"], b)
                with nc.allow_low_precision(reason="zeros and ones are exact"):
                    nc.vector.tensor_reduce(chosen[:], onehot[:].rearrange("p t j e -> p t e j"), AX.X, ALU.add
                                            ).then_inc(chosen_ready, 1)
                top1 = top_v[:, :, 0:1]
                nc.vector.tensor_tensor(ex[:, :, 0:E], lg[:], top1.broadcast_to([P, NT, E]), ALU.subtract)
                nc.vector.tensor_tensor(ex[:, :, E:E + TOPK], top_v[:, :, 0:TOPK],
                                        top1.broadcast_to([P, NT, TOPK]), ALU.subtract).then_inc(ex_ready, 1)
                dve.wait_ge(S["ranked"], b)
                front.link(b, nc.vector.tensor_tensor(base[:], counts[:], region[:], ALU.add))

            def rank_a(b, step, env):
                dve.wait_ge(exps, b + 1)
                front.link(b, nc.vector.tensor_reduce(zs[:, 0, :], exo[:, :, 0:E], AX.X, ALU.add))
                front.link(b, nc.vector.reciprocal(zs[:, 1, :], zs[:, 0, :]))

                def bc(a):
                    return a.rearrange("p (t o) -> p t o", o=1).broadcast_to([P, NT, TOPK])
                front.link(b, nc.vector.tensor_tensor(pr4[:], exo[:, :, E:E + TOPK], bc(zs[:, 1, :]), ALU.mult))
                front.link(b, nc.vector.tensor_reduce(zs[:, 2, :], pr4[:], AX.X, ALU.add))
                front.link(b, nc.vector.tensor_scalar(zs[:, 2, :], zs[:, 2, :], 1e-12, None, ALU.max))
                front.link(b, nc.vector.reciprocal(zs[:, 3, :], zs[:, 2, :]))

            def rank_b(b, step, env):
                bank = env[0][("rank",), 0][0]
                dve.wait_ge(pe["rank"], b + 1)
                ps = ps_g[bank][:, 0:NT * E].rearrange("p (t e) -> p t e", t=NT)
                front.link(b, nc.vector.tensor_tensor(
                    pos[:], ps, base[:].rearrange("p (o e) -> p o e", o=1).broadcast_to([P, NT, E]), ALU.add))
                nc.vector.tensor_tensor(counts[:], counts[:], ps_g[bank][:, NT * E:(NT + 1) * E], ALU.add
                                        ).then_inc(S["ranked"], 1)
                front.closed()

            def rank_c(b, step, env):
                dve.wait_ge(S["ranked"], b + 1)
                dve.wait_ge(scattered, SCATTERS * b)
                nc.vector.tensor_tensor(
                    entry[:, :, 1].bitcast(F32).rearrange("p (t j) -> p t j", t=NT), pr4[:],
                    zs[:, 3, :].rearrange("p (t o) -> p t o", o=1).broadcast_to([P, NT, TOPK]), ALU.mult)
                for t in range(NT):
                    ins = nc.vector.tensor_tensor(onehot[:, t, :, :], onehot[:, t, :, :],
                                                  pos[:, t:t + 1, :].broadcast_to([P, TOPK, E]), ALU.mult)
                back.link(b, ins)
                back.link(b, nc.vector.tensor_reduce(slotf[:], onehot[:].rearrange("p t j e -> p (t j) e"), AX.X,
                                                     ALU.add))
                back.link(b, nc.vector.tensor_copy(entry[:, :, 0], dest_f[:]))
                back.link(b, nc.vector.tensor_scalar(dest_f[:], dest_f[:], float(SEQ * TOPK), None, ALU.add))
                nc.vector.tensor_copy(slot[:], slotf[:]).then_inc(slots, 1)

            def fill_rows(b, step, env):
                nc.vector.tensor_scalar(fill_f[:, 0, :], counts[:], row_p[:, 0:1], None, ALU.add).then_inc(fill_chain, 1)
                dve.wait_ge(fill_chain, 1)
                nc.vector.tensor_scalar(fill_f[:, 1, :], fill_f[:, 0, :], float(REGION), float(SKIP), ALU.is_ge,
                                        ALU.mult).then_inc(fill_chain, 1)
                dve.wait_ge(fill_chain, 2)
                nc.vector.tensor_tensor(fill_f[:, 0, :], fill_f[:, 0, :], fill_f[:, 1, :], ALU.add).then_inc(fill_chain, 1)
                dve.wait_ge(fill_chain, 3)
                nc.vector.scalar_tensor_tensor(out=fill_f[:, 1, :], in0=iota_e[:], scalar=float(REGION),
                                               in1=fill_f[:, 0, :], op0=ALU.mult, op1=ALU.add).then_inc(fill_chain, 1)
                dve.wait_ge(fill_chain, 4)
                nc.vector.tensor_copy(fill_row[:], fill_f[:, 1, :]).then_inc(fill_ready, 1)

            def loaded(b, step, env):
                if step[1] == 0:
                    dve.wait_ge(w_front, 16 * 3)
                else:
                    dve.wait_ge(weights, 16 * 4)
                    dve.wait_ge(consts, N_EARLY)
                    nc.vector.tensor_scalar(region[:], iota_e[:], float(REGION), None, ALU.mult)

            run(dve, {"lnA": ln_a, "lnB": ln_b, "lnC": ln_c, "qk": qkv, "gth": gated, "up": hidden, "s1": s1, "negsplit": negsplit,
                      "avT": avT, "oproj": oproj, "route": route, "rankA": rank_a, "rankB": rank_b, "rankC": rank_c,
                      "fill_rows": fill_rows, "loaded": loaded})
            back.closed()

        @block.tensor
        def _(pe_):
            def bank_of(step, k, env):
                bp, up, b, first = env
                bank, prev = bp[step, k]
                if prev is not None:
                    name, idx, ahead = prev
                    pe_.wait_ge(S[name], done(name, b + ahead - int(first), idx))
                return ps_g[bank]

            def unit_of(step, env):
                bp, up, b, first = env
                unit, prev = up[step]
                if prev is not None:
                    name, idx, ahead = prev
                    pe_.wait_ge(S[name], done(name, b + ahead - int(first), idx))
                return ps_u[unit]

            def xT(nb, step, env):
                t = step[1]
                ps = bank_of(step, 0, env)
                pe_.wait_ge(xn_ready, NT * nb + t + 1)
                for c in range(KC):
                    ins = nc.tensor.transpose(ps[:, c * P:(c + 1) * P], xn[:, t, c * P:(c + 1) * P], ident[:])
                ins.then_inc(pe["xT"], 1)

            def project(name, lo, n):
                def handler(nb, step, env):
                    t = step[1]
                    pe_.wait_ge(S["xn_t"], done("xn_t", nb, t))
                    ps = bank_of(step, 0, env)
                    for c in range(KC):
                        ins = nc.tensor.matmul(ps[:, 0:n], xn_t[:, c, t * P:(t + 1) * P], w_qkvr[:, c, lo:lo + n],
                                               start=(c == 0), stop=(c == KC - 1))
                    ins.then_inc(pe[name], 1)
                return handler

            def partsT(nb, step, env):
                t = step[1]
                pe_.wait_ge(parts_ready, NT * nb + t + 1)
                for k, name in enumerate(("qT", "kT")):
                    ps = bank_of(step, k, env)[:, :].bitcast(BF16)
                    for a in range(NPART * KC):
                        lo = D * k + P * (a % KC)
                        ins = nc.tensor.transpose(ps[:, a * P:(a + 1) * P], parts[:, t % 2, a // KC, lo:lo + P],
                                                  identb[:])
                    ins.then_inc(pe[name], 1)

            def hidden_part(name, k):
                def handler(b, step, env):
                    m = step[1]
                    ps = bank_of(step, 0, env)
                    for c in range(KC):
                        lo = HS * k + P * m
                        ins = nc.tensor.matmul(ps[:, :], w_gu[:, c, lo:lo + P], xn_t[:, c, :], start=(c == 0),
                                               stop=(c == KC - 1))
                    ins.then_inc(pe[name], 1)
                return handler

            def s1(b, step, env):
                _, g, u = step
                i, h0, nh, per_bank = MAX_UNITS[u]
                ps = unit_of(step, env)
                if u == 0 and g % 2 == 0:
                    pe_.wait_ge(stacked[g // 2], 16 * STACK_DMAS * (b + 1))
                n = (i + 1) * P
                for a in range(nh // per_bank):
                    for k in range(per_bank):
                        h = GH * g + h0 + a * per_bank + k
                        nc.tensor.matmul(ps[:, a, k * n:(k + 1) * n], q_st[0:KROWS, h, i * P:(i + 1) * P],
                                         k_st[0:KROWS, h, 0:n], start=(k == 0), stop=False, skip_group_check=True)
                    dst = ps[:, a, 0:per_bank * n].rearrange("p (k n) -> p k n", n=n)[:, :, n - P:n]
                    ins = nc.tensor.matmul(dst, identb[:],
                                           mask_qk[:].rearrange("p (o n) -> p o n", o=1).broadcast_to([P, per_bank, P]),
                                           start=False, stop=True, skip_group_check=True)
                ins.then_inc(pe["s1"], 1)

            def negT(b, step, env):
                g = step[1]
                ps = bank_of(step, 0, env)[:, :].bitcast(BF16)
                pe_.wait_ge(neg_parts, NG * b + g + 1)
                for t in range(NT):
                    ins = nc.tensor.transpose(ps[0:NPART * GH, t * P:(t + 1) * P],
                                              neg_p[:, g % 2, t, :, :].rearrange("p a h -> p (a h)"), identb[:])
                ins.then_inc(pe["negT"], 1)

            def s2(b, step, env):
                _, g, u = step
                ps = unit_of(step, env)
                if isinstance(b, int) and (b, g, u) == (0, 0, 0):
                    pe_.wait_ge(consts, N_CONSTS)
                if u == 0:
                    pe_.wait_ge(neg_rows[g % 2], 16 * (2 * b + g // 2 + 1))
                if u < GH:
                    pieces = [(0, 0, 0, GH * g + u), (1, 0, 1, GH * g + u), (1, 3 * P, 3, GH * g + u)]
                    masks = [(0, SEQ, 1), (1, 3 * P, 2)]
                else:
                    pieces = [(j // 2, (j % 2) * 2 * P, 2, GH * g + j) for j in range(GH)]
                    masks = [(0, 2 * P, 2), (1, 2 * P, 2)]
                for n_, (a, lo, kt, h) in enumerate(pieces):
                    n = SEQ - kt * P
                    nc.tensor.matmul(ps[:, a, lo:lo + n], k_st[0:MROWS, h, kt * P:(kt + 1) * P],
                                     q_st[0:MROWS, h, kt * P:SEQ], start=(lo == 0), stop=False, skip_group_check=True)
                for a, step_, cnt in masks:
                    if cnt == 1:
                        dst, rhs = ps[:, a, 0:P], mask_kq[:]
                    else:
                        if step_ == 3 * P:
                            dst = ps[:, a, :].rearrange("p (k n) -> p k n", n=P)[:, 0:NT:3, :]
                        else:
                            dst = ps[:, a, :].rearrange("p (k n) -> p k n", n=step_)[:, :, 0:P]
                        rhs = mask_kq[:].rearrange("p (o n) -> p o n", o=1).broadcast_to([P, cnt, P])
                    ins = nc.tensor.matmul(dst, identb[:], rhs, start=False, stop=True, skip_group_check=True)
                ins.then_inc(pe["s2"], 1)

            def av_(b, step, env):
                _, g, kt = step
                if kt == 0:
                    pe_.wait_ge(S["probs"], done("probs", b, NU2 * g + NU2 - 1))
                    pe_.wait_ge(av_out, NG * b + g)
                    if g == 0:
                        pe_.wait_ge(v_placed, b + 1)
                pr = probs[g % 2]
                n = SEQ - kt * P
                for j in range(GH):
                    if kt == 2:
                        rhs = pr[:, GH, j * 2 * P:j * 2 * P + n]
                    else:
                        lo = {0: 0, 1: SEQ, 3: SEQ + 3 * P}[kt]
                        rhs = pr[:, j, lo:lo + n]
                    ins = nc.tensor.matmul(ps_av[2 * DH * j:2 * DH * (j + 1), kt * P:SEQ], v_pad[:, kt, GH * g + j, :],
                                           rhs, start=(kt == 0), stop=(kt == NT - 1), skip_group_check=True)
                if kt == NT - 1:
                    ins.then_inc(pe["av"], 1)

            def avT(b, step, env):
                g = step[1]
                ps = bank_of(step, 0, env)
                pe_.wait_ge(av_out, NG * b + g + 1)
                for t in range(NT):
                    ins = nc.tensor.transpose(ps[:, t * P:(t + 1) * P], av[:, t * P:(t + 1) * P], ident[:])
                ins.then_inc(pe["avT"], 1)

            def aT(b, step, env):
                p_ = step[1]
                ps = bank_of(step, 0, env)
                pe_.wait_ge(S["attn"], done("attn", b, NG - 1))
                for t in range(2):
                    for c in range(KC):
                        lo = (t * KC + c) * P
                        ins = nc.tensor.transpose(ps[:, lo:lo + P], attn[:, 2 * p_ + t, c * P:(c + 1) * P], ident[:])
                ins.then_inc(pe["aT"], 1)

            def down(b, step, env):
                t = step[1]
                if t == 0:
                    unit_of(step, env)
                    pe_.wait_ge(S["hidden"], done("hidden", b, NM - 1))
                ps = ps_u[env[1][("down", 0)][0]]
                for m in range(NM):
                    nc.tensor.matmul(ps[:, t // 2, (t % 2) * D:(t % 2 + 1) * D], hid[:, m, t * P:(t + 1) * P],
                                     w_d[:, m, :], start=(t % 2 == 0 and m == 0), stop=False, skip_group_check=True)

            def oproj(b, step, env):
                p_ = step[1]
                ps = ps_u[env[1][("down", 0)][0]]
                pe_.wait_ge(S["attn_t"], done("attn_t", b, p_))
                for t in (2 * p_, 2 * p_ + 1):
                    for c in range(KC):
                        ins = nc.tensor.matmul(ps[:, p_, (t % 2) * D:(t % 2 + 1) * D], attn_t[:, c, t * P:(t + 1) * P],
                                               w_o[:, c, :], start=False, stop=(c == KC - 1), skip_group_check=True)
                ins.then_inc(pe["sum"], 1)

            def rank(b, step, env):
                ps = bank_of(step, 0, env)
                pe_.wait_ge(chosen_ready, b + 1)
                ch = chosen[:].rearrange("p t e -> p (t e)")
                nc.tensor.matmul(ps[:, 0:NT * E], before[:], ch, start=True, stop=False, skip_group_check=True)
                for k in range(1, NT):
                    nc.tensor.matmul(ps[:, k * E:NT * E], ones[:], ch[:, 0:(NT - k) * E], start=False, stop=False,
                                     skip_group_check=True)
                for k in range(NT):
                    ins = nc.tensor.matmul(ps[:, NT * E:(NT + 1) * E], ones[:], ch[:, k * E:(k + 1) * E], start=False,
                                           stop=(k == NT - 1), skip_group_check=True)
                ins.then_inc(pe["rank"], 1)

            def loaded(b, step, env):
                if step[1] == 0:
                    pe_.wait_ge(w_front, 16 * 3)
                else:
                    pe_.wait_ge(weights, 16 * 4)
                    pe_.wait_ge(consts, N_EARLY)

            pe_.wait_ge(consts, N_IDENT)
            run(pe_, {"loaded": loaded, "xT": xT, "qk": project("qk", 0, 2 * D), "vr": project("vr", 2 * D, D + E), "partsT": partsT,
                      "gate": hidden_part("gate", 0), "up": hidden_part("up", 1), "s1": s1, "negT": negT, "s2": s2, "av": av_,
                      "avT": avT, "aT": aT, "down": down, "oproj": oproj, "rank": rank})


def phase_bcd(nc, sb_, sem, ident, iota_e, counts, we_gu, we_d, ps_g, ps_u, ps_av, values, sum_dram, table, y_dram,
              out):
    outer = ExitStack()
    with outer:
        sums = sb_("sums_in", [P, TOKENS // P, D], F32, outer)
        phase_bc(nc, sb_, sem, ident, iota_e, counts, we_gu, we_d, ps_g, ps_u, ps_av, values, sum_dram, table, y_dram,
                 sums)
        phase_d(nc, sb_, sem, y_dram, sums, out)


def phase_bc(nc, sb_, sem, ident, iota_e, counts, we_gu, we_d, ps_g, ps_u, ps_av, values, sum_dram, table, y_dram, sums):
    stack = ExitStack()
    with stack:
        def sb(name, shape, dt=F32):
            return sb_(name, shape, dt, stack)

        w_gu = we_gu[:, :].rearrange("p (e c n) -> p e c n", e=E, c=KC)
        w_d = we_d[:, :].rearrange("p (e n) -> p e n", e=E)
        nb_i = sb("nb_i", [P, E], I32)
        nb_f = sb("nb_f", [P, E])
        nb_c = sb("nb_c", [E, 2])
        tri = sb("tri", [E, E])
        one_c = sb("one_c", [E, 1])
        blk_i = sb("blk_i", [E, NBLOCK])
        past = sb("past", [E, NBLOCK])
        row_f = sb("row_f", [1, 2, NBLOCK])
        place = sb("place", [1, NBLOCK], I32)
        expert = sb("expert", [1, NBLOCK], I32)

        NR = 16
        ent = [sb(f"ent{i}", [P, 2], I32) for i in range(NR)]
        xg = [sb(f"xg{i}", [P, D]) for i in range(NR)]
        x_t = [sb(f"x_t{i}", [P, D]) for i in range(2)]
        tnh = [sb(f"tnh{i}", [P, HE]) for i in range(2)]
        gt = [sb(f"gt{i}", [P, HE]) for i in range(2)]
        hw = [sb(f"hw{i}", [P, HE]) for i in range(2)]
        wh = [sb(f"wh{i}", [P, 1]) for i in range(2)]
        h_t = [sb(f"h_t{i}", [P, HE]) for i in range(2)]
        yb = [sb(f"yb{i}", [P, D]) for i in range(NR)]
        ps_x, ps_gu = [ps_g[0], ps_g[1]], [ps_g[2], ps_av]
        ps_h = [ps_u[0][:, i, :] for i in range(2)]
        ps_y = [ps_u[1][:, i, :] for i in range(2)]

        plan, plan_pe, ready = sem("plan"), sem("plan_pe"), sem("ready")
        c_pool, sums_in = sem("c_pool"), sem("sums_in")
        passed, passed_s = sem("passed"), sem("passed_s")
        block_in = [sem(f"block_in{i}") for i in range(NR)]
        y_out = [sem(f"y_out{i}") for i in range(NR)]
        xt_ps, gu_ps, ht_ps, y_ps = sem("xt_ps"), sem("gu_ps"), sem("ht_ps"), sem("y_ps")
        xt_sb, tanh_sb, gate_sb, h_sb, ht_sb, y_sb = [sem(n) for n in
                                                      ("xt_sb", "tanh_sb", "gate_sb", "h_sb", "ht_sb", "y_sb")]
        block = stack.enter_context(nc.Block())
        BODY = 2 * NR
        LOOPS = (NBLOCK - 2 * NR) // BODY
        assert NBLOCK == 2 * NR + LOOPS * BODY

        def expert_loop(eng, stage, once=None):
            for n in range(NR):
                stage(n, n, True)
            with eng.Fori(0, LOOPS) as i:
                for k in range(BODY):
                    stage(i * BODY + NR + k, k % NR, False)
                    if once and k == NR:
                        once(i)
            for n in range(NBLOCK - NR, NBLOCK):
                stage(n, n % NR, False)

        table_v = table.rearrange("(n p) c -> n p c", p=P)
        values_v = values.rearrange("(n p) c -> n p c", p=P)

        @block.sync
        def _(sp):
            sp.wait_ge(ready, 1)

            def stage(n, k, first):
                if k % 4:
                    return
                _, places = nc.values_load_multi_w_load_instructions(
                    place[0:1, bass.ds(n, 4)], engines=(mybir.EngineType.SP,), min_val=0, max_val=TABLE // P - 1)
                v_places = [at % (E * REGION // P) for at in places]
                for q in range(4):
                    if not first:
                        sp.wait_ge(y_out[k + q], (n + q - (k + q)) * (16 // NR))
                        hold(sp, passed_s)
                    sp.dma_start(ent[k + q][:, :], table_v[bass.ds(places[q], 1), :, :]).then_inc(block_in[k + q], 16)
                    sp.dma_start(xg[k + q][:, :], values_v[bass.ds(v_places[q], 1), :, :]
                                 ).then_inc(block_in[k + q], 16)

            def sums_part(i):
                nt = TOKENS // P // LOOPS
                sp.dma_start(sums[:, bass.ds(i * nt, nt), :],
                             sum_dram.rearrange("(t p) d -> p t d", p=P)[:, bass.ds(i * nt, nt), :]
                             ).then_inc(sums_in, 16)
            expert_loop(sp, stage, sums_part)
            sp.wait_ge(sums_in, 16 * LOOPS)

        @block.scalar
        def _(act):
            def tanh(n, k, first):
                s = k % 2
                act.wait_ge(gu_ps, n + 1)
                if not (first and k < 2):
                    act.wait_ge(gate_sb, n - 1)
                nc.scalar.activation(tnh[s][:], ps_gu[s][:, 0:HE], ACT.Tanh, scale=0.5).then_inc(tanh_sb, 1)

            def hidden(n, k, first):
                s = k % 2
                act.wait_ge(ht_ps, n + 1)
                if not (first and k < 2):
                    act.wait_ge(y_ps, n - 1)
                nc.scalar.activation(h_t[s][:], ps_h[s][:, 0:P], ACT.Copy).then_inc(ht_sb, 1)

            def result(n, k, first):
                s = k % 2
                act.wait_ge(y_ps, n + 1)
                if not first:
                    act.wait_ge(y_out[k], (n - k) * (16 // NR))
                nc.scalar.activation(yb[k][:], ps_y[s][:, 0:D], ACT.Copy).then_inc(y_sb, 1)

            def iteration(n, k, first):
                tanh(n, k, first)
                if not first or n >= 1:
                    hidden(n - 1, (k - 1) % NR, first)
                if not first or n >= 2:
                    result(n - 2, (k - 2) % NR, first)

            for n in range(NR):
                iteration(n, n, True)
            for n in range(NR, NR + 2):
                tanh(n, n - NR, False)
                hidden(n - 1, (n - 1) % NR, False)
                result(n - 2, n - 2, True)
            for n in range(NR + 2, 2 * NR):
                iteration(n, n % NR, False)
            with act.Fori(0, LOOPS) as i:
                for k in range(BODY):
                    iteration(i * BODY + 2 * NR + k, k % NR, False)
            hidden(NBLOCK - 1, NR - 1, False)
            result(NBLOCK - 2, NR - 2, False)
            result(NBLOCK - 1, NR - 1, False)

        @block.gpsimd
        def _(pool):
            pool.iota(blk_i[:], pattern=[[1, NBLOCK]], base=0, channel_multiplier=0,
                      allow_small_or_imprecise_dtypes=True).then_inc(c_pool, 1)
            pool.memset(one_c[:], 1.0).then_inc(c_pool, 1)
            pool.memset(tri[:], 0.0).then_inc(c_pool, 1)
            pool.wait_ge(c_pool, 3)
            pool.affine_select(out=tri[:], in_=tri[:], compare_op=ALU.is_ge, fill=1.0, base=-1,
                               pattern=[[-1, E]], channel_multiplier=1).then_inc(c_pool, 1)

            def scatter(n, k, first):
                pool.wait_ge(y_sb, n + 1)
                hold(pool, passed)
                pool.indirect_dma_start(y_dram[:, :], bass.IndirectOffsetOnAxis(ap=ent[k][:, 0:1], axis=0),
                                        yb[k][:, :], None, bounds_check=TOKENS * TOPK - 1, oob_is_err=False
                                        ).then_inc(y_out[k], 16)
            expert_loop(pool, scatter)
            for k in range(NR):
                pool.wait_ge(y_out[k], 16 * NBLOCK // NR)

        @block.tensor
        def _(pe):
            pe.wait_ge(plan, 1)
            nc.tensor.transpose(ps_g[0][0:E, 0:P], nb_f[:], ident[:]).then_inc(plan_pe, 1)
            pe.wait_ge(plan, 2)
            pe.wait_ge(c_pool, 4)
            nc.tensor.matmul(ps_g[1][0:E, 0:1], tri[:], nb_c[:, 0:1], start=True, stop=True).then_inc(plan_pe, 1)
            pe.wait_ge(plan, 4)
            nc.tensor.matmul(ps_g[0][0:1, 0:NBLOCK], one_c[:], past[:], start=True, stop=True)
            nc.tensor.matmul(ps_g[2][0:1, 0:NBLOCK], nb_c[:, 0:1], past[:], start=True, stop=True).then_inc(plan_pe, 1)
            pe.wait_ge(ready, 1)

            def xT(n, k, first):
                s = k % 2
                pe.wait_ge(block_in[k], (n - k) * (32 // NR) + 32)
                if not (first and k < 2):
                    pe.wait_ge(xt_sb, n - 1)
                for c in range(KC):
                    ins = nc.tensor.transpose(ps_x[s][:, c * P:(c + 1) * P], xg[k][:, c * P:(c + 1) * P], ident[:])
                ins.then_inc(xt_ps, 1)

            def expert_of(n):
                return pe.value_load(expert[0:1, bass.ds(n, 1)], min_val=0, max_val=E - 1)

            def gu(n, k, first, e):
                s = k % 2
                pe.wait_ge(xt_sb, n + 1)
                for c in range(KC):
                    ins = nc.tensor.matmul(ps_gu[s][:, 0:2 * HE], x_t[s][:, c * P:(c + 1) * P],
                                           w_gu[:, bass.ds(e, 1), c, :], start=(c == 0), stop=(c == KC - 1))
                ins.then_inc(gu_ps, 1)

            def hT(n, k, first):
                s = k % 2
                pe.wait_ge(h_sb, n + 1)
                nc.tensor.transpose(ps_h[s][:, 0:P], hw[s][:], ident[:]).then_inc(ht_ps, 1)

            def y(n, k, first, e):
                s = k % 2
                pe.wait_ge(ht_sb, n + 1)
                nc.tensor.matmul(ps_y[s][:, 0:D], h_t[s][:], w_d[:, bass.ds(e, 1), :], start=True, stop=True
                                 ).then_inc(y_ps, 1)

            def iterations(n0, count, first):
                e = {}

                def load(k):
                    if k not in e:
                        e[k] = expert_of(n0 + k)
                for k in range(count):
                    n = n0 + k
                    if not (isinstance(n, int) and n + 1 == NBLOCK):
                        xT(n + 1, (k + 1) % NR, first and k + 1 < NR)
                    load(k)
                    gu(n, k % NR, first, e[k])
                    if not first or k >= 2:
                        load(k - 2)
                    if k >= 1 and k + 1 < count:
                        load(k + 1)
                    if not first or k >= 1:
                        hT(n - 1, (k - 1) % NR, first)
                    if not first or k >= 2:
                        y(n - 2, (k - 2) % NR, first, e[k - 2])

            xT(0, 0, True)
            iterations(0, NR, True)
            with pe.Fori(0, LOOPS) as i:
                iterations(i * BODY + NR, BODY, False)
            iterations(NBLOCK - NR, NR, False)
            e = [expert_of(NBLOCK - 2), expert_of(NBLOCK - 1)]
            hT(NBLOCK - 1, NR - 1, False)
            y(NBLOCK - 2, NR - 2, False, e[0])
            y(NBLOCK - 1, NR - 1, False, e[1])

        @block.vector
        def _(dve):
            dchain = sem("plan_dve")
            n_ = [0]

            def link(ins):
                n_[0] += 1
                ins.then_inc(dchain, 1)
                dve.wait_ge(dchain, n_[0])
            link(nc.vector.tensor_scalar(nb_f[:], counts[:], float(P - 1), None, ALU.add))
            link(nc.vector.tensor_copy(nb_i[:], nb_f[:]))
            link(nc.vector.tensor_scalar(nb_i[:], nb_i[:], 7, None, ALU.arith_shift_right))
            nc.vector.tensor_copy(nb_f[:], nb_i[:]).then_inc(plan, 1)
            dve.wait_ge(plan_pe, 1)
            nc.vector.tensor_copy(nb_c[:, 0:1], ps_g[0][0:E, 0:1]).then_inc(plan, 1)
            dve.wait_ge(plan_pe, 2)
            nc.vector.tensor_copy(nb_c[:, 1:2], ps_g[1][0:E, 0:1]).then_inc(plan, 1)
            dve.wait_ge(plan, 3)
            dve.wait_ge(c_pool, 4)
            nc.vector.tensor_scalar(past[:], blk_i[:], nb_c[:, 1:2], None, ALU.is_ge).then_inc(plan, 1)
            dve.wait_ge(plan_pe, 3)
            link(nc.vector.tensor_tensor(row_f[:, 0, :], blk_i[0:1, :], ps_g[2][0:1, 0:NBLOCK], ALU.subtract))
            link(nc.vector.scalar_tensor_tensor(out=row_f[:, 1, :], in0=ps_g[0][0:1, 0:NBLOCK],
                                                scalar=float(REGION // P), in1=row_f[:, 0, :], op0=ALU.mult,
                                                op1=ALU.add))
            link(nc.vector.tensor_scalar(row_f[:, 1, :], row_f[:, 1, :], float(E * REGION // P), None, ALU.min))
            link(nc.vector.tensor_copy(place[:], row_f[:, 1, :]))
            link(nc.vector.tensor_scalar(row_f[:, 0, :], ps_g[0][0:1, 0:NBLOCK], float(E - 1), None, ALU.min))
            nc.vector.tensor_copy(expert[:], row_f[:, 0, :]).then_inc(ready, 1)

            def front(n, k, first):
                s = k % 2
                dve.wait_ge(xt_ps, n + 1)
                if not (first and k < 2):
                    dve.wait_ge(gu_ps, n - 1)
                nc.vector.tensor_copy(x_t[s][:], ps_x[s][:, 0:D]).then_inc(xt_sb, 1)

            def stage(n, k, first):
                s = k % 2
                dve.wait_ge(tanh_sb, n + 1)
                if not (first and k < 2):
                    dve.wait_ge(h_sb, n - 1)
                nc.vector.tensor_scalar(wh[s][:], ent[k][:, 1:2].bitcast(F32), 0.5, None, ALU.mult)
                nc.vector.scalar_tensor_tensor(out=gt[s][:], in0=tnh[s][:], scalar=1.0, in1=ps_gu[s][:, 0:HE],
                                               op0=ALU.add, op1=ALU.mult).then_inc(gate_sb, 1)
                dve.wait_ge(gate_sb, n + 1)
                if not (first and k < 2):
                    dve.wait_ge(ht_ps, n - 1)
                nc.vector.scalar_tensor_tensor(out=hw[s][:], in0=gt[s][:], scalar=wh[s][:, 0:1],
                                               in1=ps_gu[s][:, HE:2 * HE], op0=ALU.mult, op1=ALU.mult
                                               ).then_inc(h_sb, 1)
            front(0, 0, True)
            for n in range(NR):
                front(n + 1, (n + 1) % NR, n + 1 < NR)
                stage(n, n, True)
            with dve.Fori(0, LOOPS) as i:
                for k in range(BODY):
                    front(i * BODY + NR + k + 1, (k + 1) % NR, False)
                    stage(i * BODY + NR + k, k % NR, False)
            for n in range(NBLOCK - NR, NBLOCK):
                if n + 1 < NBLOCK:
                    front(n + 1, (n + 1) % NR, False)
                stage(n, n % NR, False)


def phase_d(nc, sb_, sem, y_dram, sums, out):
    stack = ExitStack()
    with stack:
        NTILE = TOKENS // P
        ND = 4
        ys = [sb_(f"ys{i}", [P, TOPK, D], F32, stack) for i in range(ND)]
        red = [sb_(f"red{i}", [P, 2, D], F32, stack) for i in range(ND)]
        res = [sb_(f"res{i}", [P, D], F32, stack) for i in range(ND)]
        y_in = [sem(f"y_in{i}") for i in range(ND)]
        stored = [sem(f"stored{i}") for i in range(ND)]
        half, added = sem("half"), sem("added")
        added_p, half_p = sem("added_p"), sem("half_p")
        block = stack.enter_context(nc.Block())
        y_v = y_dram.rearrange("(n p j) d -> n p j d", p=P, j=TOPK)

        def tiles(eng, stage):
            for n in range(ND):
                stage(n, n, True)
            with eng.Fori(1, NTILE // ND) as i:
                for k in range(ND):
                    stage(i * ND + k, k, False)

        @block.sync
        def _(sp):
            def load(n, k, first):
                if not first:
                    sp.wait_ge(added, n - ND + 1)
                sp.dma_start(ys[k][:, :, :], y_dram[bass.ds(n * (P * TOPK), P * TOPK), :].rearrange(
                    "(p j) d -> p j d", j=TOPK)).then_inc(y_in[k], 16)
            tiles(sp, load)

        @block.scalar
        def _(act):
            def store(n, k, first):
                act.wait_ge(added, n + 1)
                act.dma_start(out[bass.ds(n * P, P), :], res[k][:, :]).then_inc(stored[k], 16)
            tiles(act, store)
            for k in range(ND):
                act.wait_ge(stored[k], 16 * NTILE // ND)

        @block.vector
        def _(dve):
            def add(n, k, first):
                dve.wait_ge(y_in[k], (n - k) * (16 // ND) + 16)
                if not first:
                    dve.wait_ge(added, n - ND + 1)
                nc.vector.tensor_tensor(red[k][:], ys[k][:, 0:2, :], ys[k][:, 2:4, :], ALU.add).then_inc(half, 1)
                dve.wait_ge(half, 2 * n + 1)
                nc.vector.tensor_tensor(red[k][:, 0, :], red[k][:, 0, :], red[k][:, 1, :], ALU.add).then_inc(half, 1)
                dve.wait_ge(half, 2 * n + 2)
                if not first:
                    dve.wait_ge(stored[k], (n - k) * (16 // ND))
                nc.vector.tensor_tensor(res[k][:], red[k][:, 0, :],
                                        sums[:, bass.ds(n, 1), :].rearrange("p o d -> p (o d)"), ALU.add).then_inc(added, 1)
            tiles(dve, add)


def _rope_tables():
    inv = (1.0 / np.float32(10000.0) ** (np.arange(0, DH, 2, dtype=np.float32) / np.float32(DH))).astype(np.float32)
    ang = np.outer(np.arange(SEQ, dtype=np.float32), inv).astype(np.float32)
    c, s = np.cos(ang).astype(np.float32), np.sin(ang).astype(np.float32)
    per_head = P // DH
    return np.repeat(np.concatenate([c, c], 1), per_head, 1), np.repeat(np.concatenate([-s, s], 1), per_head, 1)


def _dims_first(w):
    return w.reshape(D, KC, P // DH, DH).transpose(0, 1, 3, 2).reshape(D, D)


def kernel(**inputs):
    import concourse.bacc as bacc
    from concourse.bass_utils import run_bass_kernel_spmd

    a = {k: np.asarray(v) for k, v in inputs.items()}
    cos, sin = _rope_tables()
    arrays = {
        "x": a["L0_attn_x"].reshape(TOKENS, D),
        "wqkvr": np.concatenate([_dims_first(a["L0_attn_Wq"].T), _dims_first(a["L0_attn_Wk"].T), a["L0_attn_Wv"].T, a["L0_ffn_router_w"].T], 1),
        "wo": a["L0_attn_Wo"].T,
        "wgu_s": np.concatenate([a["L0_ffn_sgate_w"].T, a["L0_ffn_sup_w"].T], 1),
        "wd_s": a["L0_ffn_sdown_w"].T,
        "bias": a["L0_ffn_router_bias"],
        "wgu_e": np.concatenate([a["L0_ffn_gate_w"].transpose(0, 2, 1), a["L0_ffn_up_w"].transpose(0, 2, 1)], 2),
        "wd_e": a["L0_ffn_down_w"].transpose(0, 2, 1),
        "rope_cos": cos,
        "rope_sin": sin,
    }
    arrays = {k: np.ascontiguousarray(v) for k, v in arrays.items()}
    nc = bacc.Bacc("TRN2", target_bir_lowering=False, num_devices=1)
    args = [nc.dram_tensor(k, v.shape, mybir.dt.from_np(v.dtype), kind="ExternalInput").ap() for k, v in arrays.items()]
    out = nc.dram_tensor("out", (TOKENS, D), F32, kind="ExternalOutput").ap()
    block_kernel(nc, *args, out)
    r = run_bass_kernel_spmd(nc, [arrays], core_ids=[0])
    return r.results[0]["out"].reshape(BATCH, SEQ, D)
```
